# Optimizing a Trainium2 kernel written in Bass

```python
import numpy as np
import jax
import jax.numpy as jnp

def _softmax(x, axis=-1):
    return jax.nn.softmax(x, axis=axis)

def _gelu(x):
    return jax.nn.gelu(x, approximate=True)

def _silu(x):
    return jax.nn.silu(x)

def _sigmoid(x):
    return jax.nn.sigmoid(x)

def _layernorm(x, axis=-1, eps=1e-05):
    m = jnp.mean(x, axis=axis, keepdims=True)
    v = jnp.var(x, axis=axis, keepdims=True)
    return (x - m) / jnp.sqrt(v + eps)

def _scatter_add(tgt, idx, src, axis=0):
    return tgt.at[idx].add(src)

def _segment_sum(src, seg, n):
    return jax.ops.segment_sum(src, seg, n)
kernel_name = 'mk_perceiver_d4_seqx_r8_5ab344'

def setup_inputs(seed: int=0):
    np.random.seed(seed)
    _w = jnp.asarray

    def _rec_inputs():
        import jax
        import jax.numpy as jnp
        _rk = jax.random.key(seed)
        x = -7.109e-05 + 0.9999 * jax.random.normal(jax.random.fold_in(_rk, 1), (1, 128, 512), jnp.float32)
        _lenS = 128 - jax.random.randint(jax.random.fold_in(_rk, 7), (1,), 0, max(1, 128 // 4) + 1, jnp.int32)
        _lenS2 = 2048 - jax.random.randint(jax.random.fold_in(_rk, 8), (1,), 0, max(1, 2048 // 4) + 1, jnp.int32)
        _ctx_4096P = jax.random.normal(jax.random.fold_in(_rk, 11), (1, 16, 512), jnp.float32)
        _ctx_4096c = jax.random.dirichlet(jax.random.fold_in(_rk, 511), 0.3 * jnp.ones((16,), jnp.float32), (1, 2048))
        _ctx_4096t = jnp.einsum('bsk,bkd->bsd', _ctx_4096c, _ctx_4096P)
        _ctx_4096t = _ctx_4096t * jax.lax.rsqrt(jnp.mean(jnp.square(_ctx_4096t)) + 1e-12) * 0.953939
        ctx_4096 = -2.6191e-05 + 0.999952 * (_ctx_4096t + 0.3 * jax.random.normal(jax.random.fold_in(_rk, 611), (1, 2048, 512), jnp.float32))
        _validS = jnp.arange(128)[None, :] < _lenS[:, None]
        _validS2 = jnp.arange(2048)[None, :] < _lenS2[:, None]
        _causal = jnp.tril(jnp.ones((128, 128), dtype=bool))
        mask_BxSxS2_ff0 = jnp.where(jnp.ones((1, 128, 2048), dtype=bool), 0.0, -1000000000.0).astype(jnp.float32)
        mask_1x1xSxS2_ff0 = jnp.where(jnp.ones((1, 1, 128, 2048), dtype=bool), 0.0, -1000000000.0).astype(jnp.float32)
        return (x, ctx_4096, mask_BxSxS2_ff0, mask_1x1xSxS2_ff0)
    x, ctx_4096, mask_BxSxS2_ff0, mask_1x1xSxS2_ff0 = _rec_inputs()

    def _L0_xattn_setup():
        import jax, jax.numpy as jnp
        import numpy as np
        TEXT_DIM = 512
        FEATURE_DIM = 512

        def _xavier_uniform(key, shape):
            fan_in, fan_out = (shape[1], shape[0])
            limit = float(np.sqrt(6.0 / (fan_in + fan_out)))
            return jax.random.uniform(key, shape, jnp.float32, -limit, limit)
        key = jax.random.key(seed)
        k1, k2, k3, k4 = jax.random.split(key, 4)
        text = jax.random.normal(k1, (8, 256, TEXT_DIM), jnp.float32)
        features = jax.random.normal(k2, (8, 72, FEATURE_DIM), jnp.float32)
        Wq = _xavier_uniform(k3, (FEATURE_DIM, TEXT_DIM))
        bq = jnp.zeros((FEATURE_DIM,), jnp.float32)
        Wk = _xavier_uniform(k4, (FEATURE_DIM, FEATURE_DIM))
        bk = jnp.zeros((FEATURE_DIM,), jnp.float32)
        return {'text': text, 'features': features, 'Wq': Wq, 'bq': bq, 'Wk': Wk, 'bk': bk}
    _L0_xattn_all = _L0_xattn_setup()
    _L0_xattn_in = {k: v for k, v in _L0_xattn_all.items() if k in ('Wq', 'bq', 'Wk', 'bk')}
    del _L0_xattn_all

    def _L0_attn_setup():
        import jax, jax.numpy as jnp
        import numpy as np
        HIDDEN = 512
        HEAD_DIM = 128
        N_Q_HEADS = 32
        N_KV_HEADS = 8
        SLIDING_WINDOW = 128
        ROPE_THETA = 10000.0
        BATCH, SEQ = (1, 256)

        def _rope(t, pos):
            d = t.shape[-1]
            half = d // 2
            inv_freq = ROPE_THETA ** (-jnp.arange(half, dtype=jnp.float32) / half)
            ang = pos[:, None].astype(jnp.float32) * inv_freq[None, :]
            cos = jnp.cos(ang)[None, :, None, :]
            sin = jnp.sin(ang)[None, :, None, :]
            t1, t2 = (t[..., :half], t[..., half:])
            return jnp.concatenate([t1 * cos - t2 * sin, t1 * sin + t2 * cos], axis=-1)
        key = jax.random.key(seed)
        ks = jax.random.split(key, 5)
        w_scale = HIDDEN ** (-0.5)
        return {'x': jax.random.normal(ks[0], (BATCH, SEQ, HIDDEN), jnp.float32), 'wq': jax.random.normal(ks[1], (HIDDEN, N_Q_HEADS * HEAD_DIM), jnp.float32) * w_scale, 'wk': jax.random.normal(ks[2], (HIDDEN, N_KV_HEADS * HEAD_DIM), jnp.float32) * w_scale, 'wv': jax.random.normal(ks[3], (HIDDEN, N_KV_HEADS * HEAD_DIM), jnp.float32) * w_scale, 'wo': jax.random.normal(ks[4], (N_Q_HEADS * HEAD_DIM, HIDDEN), jnp.float32) * w_scale}
    _L0_attn_all = _L0_attn_setup()
    _L0_attn_in = {k: v for k, v in _L0_attn_all.items() if k in ('wq', 'wk', 'wv', 'wo')}
    del _L0_attn_all

    def _L0_ffn_setup():
        import jax, jax.numpy as jnp
        import numpy as np
        B_, S, D_IN, D_OUT = (4, 256, 512, 512)
        N, RANK, ALPHA = (8, 16, 32)
        SCALE = ALPHA / RANK
        key = jax.random.key(seed)
        kx, ka, kb, kw, kbias = jax.random.split(key, 5)
        x = jax.random.normal(kx, (B_, S, D_IN), dtype=jnp.float32)
        lora_A = jax.random.normal(ka, (N, RANK, D_IN), dtype=jnp.float32) * (1.0 / np.sqrt(D_IN))
        lora_B = jax.random.normal(kb, (N, D_OUT, RANK), dtype=jnp.float32) * (1.0 / np.sqrt(RANK))
        W = jax.random.normal(kw, (D_OUT, D_IN), dtype=jnp.float32) * (1.0 / np.sqrt(D_IN))
        bias = jax.random.normal(kbias, (D_OUT,), dtype=jnp.float32) * 0.01
        lora_weights = jnp.full((N,), 1.0 / N, dtype=jnp.float32)
        return {'x': x, 'lora_A': lora_A, 'lora_B': lora_B, 'W': W, 'bias': bias, 'lora_weights': lora_weights}
    _L0_ffn_all = _L0_ffn_setup()
    _L0_ffn_in = {k: v for k, v in _L0_ffn_all.items() if k in ('lora_A', 'lora_B', 'W', 'bias', 'lora_weights')}
    del _L0_ffn_all

    def _L1_xattn_setup():
        import jax, jax.numpy as jnp
        import numpy as np
        EPS = 1e-06

        def rmsnorm(x, w):
            xf = x.astype(jnp.float32)
            var = jnp.mean(xf * xf, axis=-1, keepdims=True)
            return (xf * jax.lax.rsqrt(var + EPS)).astype(x.dtype) * w
        key = jax.random.key(seed)
        ks = jax.random.split(key, 6)
        B, T, S, Dt, Df = (4, 128, 72, 512, 512)
        text = jax.random.normal(ks[0], (B, T, Dt), dtype=jnp.float32)
        features = jax.random.normal(ks[1], (B, S, Df), dtype=jnp.float32)
        lim_q = float(np.sqrt(6.0 / (Dt + Df)))
        lim_k = float(np.sqrt(6.0 / (Df + Df)))
        Wq_w = jax.random.uniform(ks[2], (Df, Dt), minval=-lim_q, maxval=lim_q, dtype=jnp.float32)
        Wk_w = jax.random.uniform(ks[3], (Df, Df), minval=-lim_k, maxval=lim_k, dtype=jnp.float32)
        bq = 1.0 / np.sqrt(Dt)
        bk = 1.0 / np.sqrt(Df)
        Wq_b = jax.random.uniform(ks[4], (Df,), minval=-bq, maxval=bq, dtype=jnp.float32)
        Wk_b = jax.random.uniform(ks[5], (Df,), minval=-bk, maxval=bk, dtype=jnp.float32)
        fn_w = jnp.ones((Df,), dtype=jnp.float32)
        qn_w = jnp.ones((Df,), dtype=jnp.float32)
        kn_w = jnp.ones((Df,), dtype=jnp.float32)
        return {'text': text, 'features': features, 'Wq_w': Wq_w, 'Wq_b': Wq_b, 'Wk_w': Wk_w, 'Wk_b': Wk_b, 'fn_w': fn_w, 'qn_w': qn_w, 'kn_w': kn_w}
    _L1_xattn_all = _L1_xattn_setup()
    _L1_xattn_in = {k: v for k, v in _L1_xattn_all.items() if k in ('Wq_w', 'Wq_b', 'Wk_w', 'Wk_b', 'fn_w', 'qn_w', 'kn_w')}
    del _L1_xattn_all

    def _L1_attn_setup():
        import jax, jax.numpy as jnp
        import numpy as np
        H_SIZE = 512
        NH = 128
        HD = 64
        SS = 128
        K = 4
        NG = 8
        CHUNK = 128
        INTER = NH * HD
        CONV_DIM = INTER + 2 * NG * SS
        PROJ = INTER + CONV_DIM + NH
        DT_MIN, DT_MAX = (0.001, 100.0)
        EPS = 1e-05
        GROUP = INTER // NG

        def _ssd(x, Bm, Cm, D, dt, dt_bias):
            Bsz, S, H, P = x.shape
            N = Bm.shape[-1]
            A = -jnp.arange(1, H + 1, dtype=jnp.float32)
            dt = jnp.clip(jax.nn.softplus(dt + dt_bias), DT_MIN, DT_MAX)
            rep = H // Bm.shape[2]
            Bh = jnp.repeat(Bm, rep, axis=2)
            Ch = jnp.repeat(Cm, rep, axis=2)
            nc, L = (S // CHUNK, CHUNK)
            xc = x.reshape(Bsz, nc, L, H, P)
            dtc = dt.reshape(Bsz, nc, L, H)
            Bc = Bh.reshape(Bsz, nc, L, H, N)
            Cc = Ch.reshape(Bsz, nc, L, H, N)
            dA = jnp.swapaxes(dtc, 2, 3) * A[None, None, :, None]
            cs = jnp.cumsum(dA, axis=-1)
            seg = cs[..., :, None] - cs[..., None, :]
            tri = jnp.tril(jnp.ones((L, L), dtype=bool))
            Lmat = jnp.where(tri, jnp.exp(seg), 0.0)
            xdt = xc * dtc[..., None]
            scores = jnp.einsum('bclhn,bcshn->bchls', Cc, Bc) * Lmat
            Ydiag = jnp.einsum('bchls,bcshp->bclhp', scores, xdt)
            decay_states = jnp.exp(cs[..., -1:] - cs)
            states = jnp.einsum('bclhn,bchl,bclhp->bchpn', Bc, decay_states, xdt)
            chunk_decay = jnp.exp(cs[..., -1])

            def step(carry, inp):
                st, cd = inp
                new = carry * cd[:, :, None, None] + st
                return (new, carry)
            st_seq = jnp.moveaxis(states, 1, 0)
            cd_seq = jnp.moveaxis(chunk_decay, 1, 0)
            init = jnp.zeros_like(st_seq[0])
            _, prev = jax.lax.scan(step, init, (st_seq, cd_seq))
            prev = jnp.moveaxis(prev, 0, 1)
            Yoff = jnp.einsum('bclhn,bchpn,bchl->bclhp', Cc, prev, jnp.exp(cs))
            Y = (Ydiag + Yoff).reshape(Bsz, S, H, P) + x * D[None, None, :, None]
            return Y
        key = jax.random.key(seed)
        ks = jax.random.split(key, 5)
        s = 0.02
        return {'hidden_states': jax.random.normal(ks[0], (1, 256, H_SIZE), jnp.float32), 'in_proj_w': jax.random.normal(ks[1], (PROJ, H_SIZE), jnp.float32) * s, 'conv_w': jax.random.normal(ks[2], (CONV_DIM, 1, K), jnp.float32) * 0.1, 'conv_b': jnp.zeros((CONV_DIM,), jnp.float32), 'dt_bias': jnp.ones((NH,), jnp.float32), 'D': jnp.ones((NH,), jnp.float32), 'norm_w': jnp.ones((INTER,), jnp.float32), 'out_proj_w': jax.random.normal(ks[3], (H_SIZE, INTER), jnp.float32) * s}
    _L1_attn_all = _L1_attn_setup()
    _L1_attn_in = {k: v for k, v in _L1_attn_all.items() if k in ('in_proj_w', 'conv_w', 'conv_b', 'dt_bias', 'D', 'norm_w', 'out_proj_w')}
    del _L1_attn_all

    def _L1_ffn_setup():
        import jax, jax.numpy as jnp
        import numpy as np
        B, S, D, O, E, R = (4, 256, 512, 512, 8, 16)
        SCALING = 32.0 / 16.0
        MAX_THRESHOLD = 0.125
        key = jax.random.key(seed)
        ks = jax.random.split(key, 8)
        return {'x': jax.random.normal(ks[0], (B, S, D), jnp.float32), 'W_base': jax.random.normal(ks[1], (O, D), jnp.float32) * (1.0 / np.sqrt(D)), 'b_base': jax.random.normal(ks[2], (O,), jnp.float32) * 0.02, 'W_gate': jax.random.normal(ks[3], (E, D), jnp.float32) * (1.0 / np.sqrt(D)), 'W_thr': jax.random.normal(ks[4], (D,), jnp.float32) * (1.0 / np.sqrt(D)), 'b_thr': jax.random.normal(ks[5], (1,), jnp.float32) * 0.02, 'A_w': jax.random.normal(ks[6], (E, R, D), jnp.float32) * (1.0 / np.sqrt(D)), 'B_w': jax.random.normal(ks[7], (E, O, R), jnp.float32) * (1.0 / np.sqrt(R))}
    _L1_ffn_all = _L1_ffn_setup()
    _L1_ffn_in = {k: v for k, v in _L1_ffn_all.items() if k in ('W_base', 'b_base', 'W_gate', 'W_thr', 'b_thr', 'A_w', 'B_w')}
    del _L1_ffn_all

    def _L2_xattn_setup():
        import jax, jax.numpy as jnp
        import numpy as np
        BS, SEQ, D_MODEL = (4, 128, 512)
        N_Q_HEADS, N_KV_HEADS, D_K, D_V = (32, 8, 128, 128)
        ROPE_BASE = 10000.0

        def _rotate_half(x):
            x1, x2 = jnp.split(x, 2, axis=-1)
            return jnp.concatenate([-x2, x1], axis=-1)

        def _apply_rope(x, pos0):
            d = x.shape[-1]
            seq = x.shape[2]
            inv_freq = 1.0 / ROPE_BASE ** (jnp.arange(0, d, 2, dtype=jnp.float32) / d)
            pos = (pos0 + jnp.arange(seq)).astype(jnp.float32)
            ang = pos[:, None] * inv_freq[None, :]
            cos = jnp.concatenate([jnp.cos(ang), jnp.cos(ang)], axis=-1)
            sin = jnp.concatenate([jnp.sin(ang), jnp.sin(ang)], axis=-1)
            return x * cos[None, None] + _rotate_half(x) * sin[None, None]
        key = jax.random.key(seed)
        ks = jax.random.split(key, 8)
        w_scale = 0.02
        return {'query': jax.random.normal(ks[0], (BS, SEQ, D_MODEL), dtype=jnp.float32), 'key': jax.random.normal(ks[1], (BS, SEQ, D_MODEL), dtype=jnp.float32), 'value': jax.random.normal(ks[2], (BS, SEQ, D_MODEL), dtype=jnp.float32), 'mask': jnp.zeros((BS, SEQ, SEQ), dtype=jnp.float32), 'wq': jax.random.normal(ks[3], (D_MODEL, N_Q_HEADS * D_K), dtype=jnp.float32) * w_scale, 'wk': jax.random.normal(ks[4], (D_MODEL, N_KV_HEADS * D_K), dtype=jnp.float32) * w_scale, 'wv': jax.random.normal(ks[5], (D_MODEL, N_KV_HEADS * D_V), dtype=jnp.float32) * w_scale, 'wo': jax.random.normal(ks[6], (N_Q_HEADS * D_V, D_MODEL), dtype=jnp.float32) * w_scale, 'curr_seq_pos': 0}
    _L2_xattn_all = _L2_xattn_setup()
    _L2_xattn_in = {k: v for k, v in _L2_xattn_all.items() if k in ('wq', 'wk', 'wv', 'wo')}
    del _L2_xattn_all

    def _L2_attn_setup():
        import jax, jax.numpy as jnp
        import numpy as np
        import math
        HIDDEN = 512
        N_HEADS = 32
        N_KV_HEADS = 8
        HEAD_DIM = HIDDEN // N_HEADS
        GROUPS = N_HEADS // N_KV_HEADS
        ROPE_THETA = 10000.0
        TOKEN_BUDGET = 128
        INIT_BUDGET = 128
        RECENT_BUDGET = 128
        CHUNK = 16
        B, S = (1, 256)

        def _rotate_half(x):
            x1, x2 = jnp.split(x, 2, axis=-1)
            return jnp.concatenate([-x2, x1], axis=-1)

        def _rope(seq_len, dtype):
            inv_freq = 1.0 / ROPE_THETA ** (jnp.arange(0, HEAD_DIM, 2, dtype=jnp.float32) / HEAD_DIM)
            freqs = jnp.arange(seq_len, dtype=jnp.float32)[:, None] * inv_freq[None, :]
            emb = jnp.concatenate([freqs, freqs], axis=-1)
            return (jnp.cos(emb).astype(dtype), jnp.sin(emb).astype(dtype))
        key = jax.random.key(seed)
        ks = jax.random.split(key, 5)
        sc = 0.02
        return {'hidden_states': jax.random.normal(ks[0], (B, S, HIDDEN), dtype=jnp.float32), 'wq': jax.random.normal(ks[1], (N_HEADS * HEAD_DIM, HIDDEN), dtype=jnp.float32) * sc, 'wk': jax.random.normal(ks[2], (N_KV_HEADS * HEAD_DIM, HIDDEN), dtype=jnp.float32) * sc, 'wv': jax.random.normal(ks[3], (N_KV_HEADS * HEAD_DIM, HIDDEN), dtype=jnp.float32) * sc, 'wo': jax.random.normal(ks[4], (HIDDEN, N_HEADS * HEAD_DIM), dtype=jnp.float32) * sc}
    _L2_attn_all = _L2_attn_setup()
    _L2_attn_in = {k: v for k, v in _L2_attn_all.items() if k in ('wq', 'wk', 'wv', 'wo')}
    del _L2_attn_all

    def _L2_ffn_setup():
        import jax, jax.numpy as jnp
        import numpy as np
        NUM_EXPERTS = 8
        D_IN = 512
        D_OUT = 512
        key = jax.random.key(seed)
        k_x, k_gw, k_gb, k_ew, k_eb = jax.random.split(key, 5)
        x = jax.random.normal(k_x, (4, 256, D_IN), dtype=jnp.float32)
        gate_w = jax.random.normal(k_gw, (NUM_EXPERTS, D_IN), dtype=jnp.float32) * 0.02
        gate_b = jax.random.normal(k_gb, (NUM_EXPERTS,), dtype=jnp.float32) * 0.02
        expert_w = jax.random.normal(k_ew, (NUM_EXPERTS, D_OUT, D_IN), dtype=jnp.float32) * 0.02
        expert_b = jax.random.normal(k_eb, (NUM_EXPERTS, D_OUT), dtype=jnp.float32) * 0.02
        return {'x': x, 'gate_w': gate_w, 'gate_b': gate_b, 'expert_w': expert_w, 'expert_b': expert_b}
    _L2_ffn_all = _L2_ffn_setup()
    _L2_ffn_in = {k: v for k, v in _L2_ffn_all.items() if k in ('gate_w', 'gate_b', 'expert_w', 'expert_b')}
    del _L2_ffn_all

    def _L3_xattn_setup():
        import jax, jax.numpy as jnp
        import numpy as np
        B, Q, K, D = (1, 128, 6404, 512)
        H, KVH, HD = (32, 8, 128)
        GROUPS = H // KVH
        EPS = 1e-05

        def _rmsnorm(x, w):
            xf = x.astype(jnp.float32)
            var = jnp.mean(xf * xf, axis=-1, keepdims=True)
            return (xf * jax.lax.rsqrt(var + EPS)).astype(x.dtype) * w
        key = jax.random.key(seed)
        ks = jax.random.split(key, 8)
        s = 0.02
        return {'hidden_states': jax.random.normal(ks[0], (B, Q, D), jnp.float32), 'cross_attention_states': jax.random.normal(ks[1], (B, K, D), jnp.float32), 'attention_mask': jnp.zeros((B, 1, Q, K), jnp.float32), 'Wq': jax.random.normal(ks[2], (H * HD, D), jnp.float32) * s, 'Wk': jax.random.normal(ks[3], (KVH * HD, D), jnp.float32) * s, 'Wv': jax.random.normal(ks[4], (KVH * HD, D), jnp.float32) * s, 'Wo': jax.random.normal(ks[5], (D, H * HD), jnp.float32) * s, 'q_norm_w': jnp.ones((HD,), jnp.float32), 'k_norm_w': jnp.ones((HD,), jnp.float32)}
    _L3_xattn_all = _L3_xattn_setup()
    _L3_xattn_in = {k: v for k, v in _L3_xattn_all.items() if k in ('Wq', 'Wk', 'Wv', 'Wo', 'q_norm_w', 'k_norm_w')}
    del _L3_xattn_all

    def _L3_attn_setup():
        import jax, jax.numpy as jnp
        import numpy as np
        SEQ, BATCH, HIDDEN = (256, 1, 512)
        NUM_HEADS, NUM_KV_HEADS, HEAD_DIM = (32, 8, 128)
        Q_PER_GROUP = NUM_HEADS // NUM_KV_HEADS
        TOTAL_PROJ = NUM_KV_HEADS * (Q_PER_GROUP + 2) * HEAD_DIM
        key = jax.random.key(seed)
        k1, k2, k3 = jax.random.split(key, 3)
        tokens = jax.random.normal(k1, (SEQ, BATCH, HIDDEN), dtype=jnp.float32)
        weight_qkv = jax.random.normal(k2, (TOTAL_PROJ, HIDDEN), dtype=jnp.float32) * (2.0 / (TOTAL_PROJ + HIDDEN)) ** 0.5
        weight_proj = jax.random.normal(k3, (HIDDEN, NUM_HEADS * HEAD_DIM), dtype=jnp.float32) * (2.0 / (HIDDEN + NUM_HEADS * HEAD_DIM)) ** 0.5
        return {'tokens': tokens, 'weight_qkv': weight_qkv, 'weight_proj': weight_proj}
    _L3_attn_all = _L3_attn_setup()
    _L3_attn_in = {k: v for k, v in _L3_attn_all.items() if k in ('weight_qkv', 'weight_proj')}
    del _L3_attn_all

    def _L3_ffn_setup():
        import math
        import jax, jax.numpy as jnp
        import numpy as np
        SCALING = 16.0 / 32.0

        def real_fourier_orthogonal_multiply(c):
            n = c.shape[-1]
            sqrt_n = math.sqrt(n)
            pair_scale = math.sqrt(n / 2.0)
            max_f = (n - 1) // 2
            work = c.astype(jnp.float32)
            dc = (work[..., 0] * sqrt_n)[..., None].astype(jnp.complex64)
            cos = work[..., 1:1 + 2 * max_f:2] * pair_scale
            sin = work[..., 2:2 + 2 * max_f:2] * pair_scale
            mid = (cos - 1j * sin).astype(jnp.complex64)
            parts = [dc, mid]
            if n % 2 == 0:
                parts.append((work[..., -1] * sqrt_n)[..., None].astype(jnp.complex64))
            spectrum = jnp.concatenate(parts, axis=-1)
            return jnp.fft.irfft(spectrum, n=n, axis=-1).astype(c.dtype)
        key = jax.random.key(seed)
        ks = jax.random.split(key, 9)
        B, S, D_in, D_out, R0, R1, E = (4, 256, 512, 512, 32, 8, 3)
        x = jax.random.normal(ks[0], (B, S, D_in), dtype=jnp.float32)
        W_base = jax.random.normal(ks[1], (D_out, D_in), dtype=jnp.float32) * 0.02
        b_base = jax.random.normal(ks[2], (D_out,), dtype=jnp.float32) * 0.02
        enc0 = jax.random.normal(ks[3], (R0, D_in), dtype=jnp.float32) * 0.02
        enc1 = jax.random.normal(ks[4], (R1, D_in), dtype=jnp.float32) * 0.02
        coefs0 = jax.random.normal(ks[5], (E, D_out, R0), dtype=jnp.float32) * 0.02
        coefs1 = jax.random.normal(ks[6], (E, D_out, R1), dtype=jnp.float32) * 0.02
        mask0 = jax.random.randint(ks[7], (E, D_out, R0), 0, 2).astype(bool)
        mask1 = jax.random.randint(ks[8], (E, D_out, R1), 0, 2).astype(bool)
        return dict(x=x, W_base=W_base, b_base=b_base, enc0=enc0, enc1=enc1, coefs0=coefs0, coefs1=coefs1, mask0=mask0, mask1=mask1)
    _L3_ffn_all = _L3_ffn_setup()
    _L3_ffn_in = {k: v for k, v in _L3_ffn_all.items() if k in ('W_base', 'b_base', 'enc0', 'enc1', 'coefs0', 'coefs1', 'mask0', 'mask1')}
    del _L3_ffn_all
    return {'x': x, 'ctx_4096': ctx_4096, 'mask_BxSxS2_ff0': mask_BxSxS2_ff0, 'mask_1x1xSxS2_ff0': mask_1x1xSxS2_ff0, 'L0_xattn_Wq': _L0_xattn_in['Wq'], 'L0_xattn_bq': _L0_xattn_in['bq'], 'L0_xattn_Wk': _L0_xattn_in['Wk'], 'L0_xattn_bk': _L0_xattn_in['bk'], 'L0_attn_wq': _L0_attn_in['wq'], 'L0_attn_wk': _L0_attn_in['wk'], 'L0_attn_wv': _L0_attn_in['wv'], 'L0_attn_wo': _L0_attn_in['wo'], 'L0_ffn_lora_A': _L0_ffn_in['lora_A'], 'L0_ffn_lora_B': _L0_ffn_in['lora_B'], 'L0_ffn_W': _L0_ffn_in['W'], 'L0_ffn_bias': _L0_ffn_in['bias'], 'L0_ffn_lora_weights': _L0_ffn_in['lora_weights'], 'L1_xattn_Wq_w': _L1_xattn_in['Wq_w'], 'L1_xattn_Wq_b': _L1_xattn_in['Wq_b'], 'L1_xattn_Wk_w': _L1_xattn_in['Wk_w'], 'L1_xattn_Wk_b': _L1_xattn_in['Wk_b'], 'L1_xattn_fn_w': _L1_xattn_in['fn_w'], 'L1_xattn_qn_w': _L1_xattn_in['qn_w'], 'L1_xattn_kn_w': _L1_xattn_in['kn_w'], 'L1_attn_in_proj_w': _L1_attn_in['in_proj_w'], 'L1_attn_conv_w': _L1_attn_in['conv_w'], 'L1_attn_conv_b': _L1_attn_in['conv_b'], 'L1_attn_dt_bias': _L1_attn_in['dt_bias'], 'L1_attn_D': _L1_attn_in['D'], 'L1_attn_norm_w': _L1_attn_in['norm_w'], 'L1_attn_out_proj_w': _L1_attn_in['out_proj_w'], 'L1_ffn_W_base': _L1_ffn_in['W_base'], 'L1_ffn_b_base': _L1_ffn_in['b_base'], 'L1_ffn_W_gate': _L1_ffn_in['W_gate'], 'L1_ffn_W_thr': _L1_ffn_in['W_thr'], 'L1_ffn_b_thr': _L1_ffn_in['b_thr'], 'L1_ffn_A_w': _L1_ffn_in['A_w'], 'L1_ffn_B_w': _L1_ffn_in['B_w'], 'L2_xattn_wq': _L2_xattn_in['wq'], 'L2_xattn_wk': _L2_xattn_in['wk'], 'L2_xattn_wv': _L2_xattn_in['wv'], 'L2_xattn_wo': _L2_xattn_in['wo'], 'L2_attn_wq': _L2_attn_in['wq'], 'L2_attn_wk': _L2_attn_in['wk'], 'L2_attn_wv': _L2_attn_in['wv'], 'L2_attn_wo': _L2_attn_in['wo'], 'L2_ffn_gate_w': _L2_ffn_in['gate_w'], 'L2_ffn_gate_b': _L2_ffn_in['gate_b'], 'L2_ffn_expert_w': _L2_ffn_in['expert_w'], 'L2_ffn_expert_b': _L2_ffn_in['expert_b'], 'L3_xattn_Wq': _L3_xattn_in['Wq'], 'L3_xattn_Wk': _L3_xattn_in['Wk'], 'L3_xattn_Wv': _L3_xattn_in['Wv'], 'L3_xattn_Wo': _L3_xattn_in['Wo'], 'L3_xattn_q_norm_w': _L3_xattn_in['q_norm_w'], 'L3_xattn_k_norm_w': _L3_xattn_in['k_norm_w'], 'L3_attn_weight_qkv': _L3_attn_in['weight_qkv'], 'L3_attn_weight_proj': _L3_attn_in['weight_proj'], 'L3_ffn_W_base': _L3_ffn_in['W_base'], 'L3_ffn_b_base': _L3_ffn_in['b_base'], 'L3_ffn_enc0': _L3_ffn_in['enc0'], 'L3_ffn_enc1': _L3_ffn_in['enc1'], 'L3_ffn_coefs0': _L3_ffn_in['coefs0'], 'L3_ffn_coefs1': _L3_ffn_in['coefs1'], 'L3_ffn_mask0': _L3_ffn_in['mask0'], 'L3_ffn_mask1': _L3_ffn_in['mask1']}

def reference(x, ctx_4096, mask_BxSxS2_ff0, mask_1x1xSxS2_ff0, L0_xattn_Wq, L0_xattn_bq, L0_xattn_Wk, L0_xattn_bk, L0_attn_wq, L0_attn_wk, L0_attn_wv, L0_attn_wo, L0_ffn_lora_A, L0_ffn_lora_B, L0_ffn_W, L0_ffn_bias, L0_ffn_lora_weights, L1_xattn_Wq_w, L1_xattn_Wq_b, L1_xattn_Wk_w, L1_xattn_Wk_b, L1_xattn_fn_w, L1_xattn_qn_w, L1_xattn_kn_w, L1_attn_in_proj_w, L1_attn_conv_w, L1_attn_conv_b, L1_attn_dt_bias, L1_attn_D, L1_attn_norm_w, L1_attn_out_proj_w, L1_ffn_W_base, L1_ffn_b_base, L1_ffn_W_gate, L1_ffn_W_thr, L1_ffn_b_thr, L1_ffn_A_w, L1_ffn_B_w, L2_xattn_wq, L2_xattn_wk, L2_xattn_wv, L2_xattn_wo, L2_attn_wq, L2_attn_wk, L2_attn_wv, L2_attn_wo, L2_ffn_gate_w, L2_ffn_gate_b, L2_ffn_expert_w, L2_ffn_expert_b, L3_xattn_Wq, L3_xattn_Wk, L3_xattn_Wv, L3_xattn_Wo, L3_xattn_q_norm_w, L3_xattn_k_norm_w, L3_attn_weight_qkv, L3_attn_weight_proj, L3_ffn_W_base, L3_ffn_b_base, L3_ffn_enc0, L3_ffn_enc1, L3_ffn_coefs0, L3_ffn_coefs1, L3_ffn_mask0, L3_ffn_mask1):
    import jax
    import jax.numpy as jnp

    def _L0_xattn_ref(text, features, Wq, bq, Wk, bk):
        import jax, jax.numpy as jnp
        import numpy as np
        TEXT_DIM = 512
        FEATURE_DIM = 512

        def _xavier_uniform(key, shape):
            fan_in, fan_out = (shape[1], shape[0])
            limit = float(np.sqrt(6.0 / (fan_in + fan_out)))
            return jax.random.uniform(key, shape, jnp.float32, -limit, limit)
        Q = jnp.einsum('btx,dx->btd', text, Wq) + bq
        K = jnp.einsum('bpx,dx->bpd', features, Wk) + bk
        scale = 1.0 / jnp.sqrt(jnp.asarray(K.shape[-1], K.dtype))
        scores = jnp.einsum('btd,bpd->btp', Q, K) * scale
        attn = jax.nn.softmax(scores, axis=-1)
        attended = jnp.einsum('btp,bpd->btd', attn, features)
        return attended

    def _L0_attn_ref(x, wq, wk, wv, wo):
        import jax, jax.numpy as jnp
        import numpy as np
        HIDDEN = 512
        HEAD_DIM = 128
        N_Q_HEADS = 32
        N_KV_HEADS = 8
        SLIDING_WINDOW = 128
        ROPE_THETA = 10000.0
        BATCH, SEQ = (1, 256)

        def _rope(t, pos):
            d = t.shape[-1]
            half = d // 2
            inv_freq = ROPE_THETA ** (-jnp.arange(half, dtype=jnp.float32) / half)
            ang = pos[:, None].astype(jnp.float32) * inv_freq[None, :]
            cos = jnp.cos(ang)[None, :, None, :]
            sin = jnp.sin(ang)[None, :, None, :]
            t1, t2 = (t[..., :half], t[..., half:])
            return jnp.concatenate([t1 * cos - t2 * sin, t1 * sin + t2 * cos], axis=-1)
        B, S, _ = x.shape
        G = N_Q_HEADS // N_KV_HEADS
        sm_scale = HEAD_DIM ** (-0.5)
        q = (x @ wq).reshape(B, S, N_Q_HEADS, HEAD_DIM)
        k = (x @ wk).reshape(B, S, N_KV_HEADS, HEAD_DIM)
        v = (x @ wv).reshape(B, S, N_KV_HEADS, HEAD_DIM)
        pos = jnp.arange(S)
        q = _rope(q, pos)
        k = _rope(k, pos)
        qg = q.reshape(B, S, N_KV_HEADS, G, HEAD_DIM)
        scores = jnp.einsum('bqhgd,bshd->bhgqs', qg, k) * sm_scale
        i = pos[:, None]
        j = pos[None, :]
        allowed = (j <= i) & (j > i - SLIDING_WINDOW)
        neg = jnp.finfo(scores.dtype).min
        scores = jnp.where(allowed[None, None, None], scores, neg)
        attn = jax.nn.softmax(scores, axis=-1)
        out = jnp.einsum('bhgqs,bshd->bqhgd', attn, v).reshape(B, S, N_Q_HEADS * HEAD_DIM)
        return out @ wo

    def _L0_ffn_ref(x, lora_A, lora_B, W, bias, lora_weights):
        import jax, jax.numpy as jnp
        import numpy as np
        B_, S, D_IN, D_OUT = (4, 256, 512, 512)
        N, RANK, ALPHA = (8, 16, 32)
        SCALE = ALPHA / RANK
        h = jnp.einsum('bsd,nrd->nbsr', x, lora_A)
        coef = (SCALE * lora_weights)[:, None, None]
        lora_out = jnp.einsum('nbsr,nor->bso', h, lora_B * coef)
        base = jnp.einsum('bsd,od->bso', x, W) + bias
        return base + lora_out

    def _L1_xattn_ref(text, features, Wq_w, Wq_b, Wk_w, Wk_b, fn_w, qn_w, kn_w):
        import jax, jax.numpy as jnp
        import numpy as np
        EPS = 1e-06

        def rmsnorm(x, w):
            xf = x.astype(jnp.float32)
            var = jnp.mean(xf * xf, axis=-1, keepdims=True)
            return (xf * jax.lax.rsqrt(var + EPS)).astype(x.dtype) * w
        features_n = rmsnorm(features, fn_w)
        Q = jnp.einsum('btd,fd->btf', text, Wq_w) + Wq_b
        K = jnp.einsum('bsd,fd->bsf', features_n, Wk_w) + Wk_b
        Q = rmsnorm(Q, qn_w)
        K = rmsnorm(K, kn_w)
        scale = 1.0 / jnp.sqrt(jnp.asarray(K.shape[-1], dtype=Q.dtype))
        scores = jnp.einsum('btf,bsf->bts', Q, K) * scale
        attn = jax.nn.softmax(scores, axis=-1)
        attended = jnp.einsum('bts,bsf->btf', attn, features_n)
        return attended

    def _L1_attn_ref(hidden_states, in_proj_w, conv_w, conv_b, dt_bias, D, norm_w, out_proj_w):
        import jax, jax.numpy as jnp
        import numpy as np
        H_SIZE = 512
        NH = 128
        HD = 64
        SS = 128
        K = 4
        NG = 8
        CHUNK = 128
        INTER = NH * HD
        CONV_DIM = INTER + 2 * NG * SS
        PROJ = INTER + CONV_DIM + NH
        DT_MIN, DT_MAX = (0.001, 100.0)
        EPS = 1e-05
        GROUP = INTER // NG

        def _ssd(x, Bm, Cm, D, dt, dt_bias):
            Bsz, S, H, P = x.shape
            N = Bm.shape[-1]
            A = -jnp.arange(1, H + 1, dtype=jnp.float32)
            dt = jnp.clip(jax.nn.softplus(dt + dt_bias), DT_MIN, DT_MAX)
            rep = H // Bm.shape[2]
            Bh = jnp.repeat(Bm, rep, axis=2)
            Ch = jnp.repeat(Cm, rep, axis=2)
            nc, L = (S // CHUNK, CHUNK)
            xc = x.reshape(Bsz, nc, L, H, P)
            dtc = dt.reshape(Bsz, nc, L, H)
            Bc = Bh.reshape(Bsz, nc, L, H, N)
            Cc = Ch.reshape(Bsz, nc, L, H, N)
            dA = jnp.swapaxes(dtc, 2, 3) * A[None, None, :, None]
            cs = jnp.cumsum(dA, axis=-1)
            seg = cs[..., :, None] - cs[..., None, :]
            tri = jnp.tril(jnp.ones((L, L), dtype=bool))
            Lmat = jnp.where(tri, jnp.exp(seg), 0.0)
            xdt = xc * dtc[..., None]
            scores = jnp.einsum('bclhn,bcshn->bchls', Cc, Bc) * Lmat
            Ydiag = jnp.einsum('bchls,bcshp->bclhp', scores, xdt)
            decay_states = jnp.exp(cs[..., -1:] - cs)
            states = jnp.einsum('bclhn,bchl,bclhp->bchpn', Bc, decay_states, xdt)
            chunk_decay = jnp.exp(cs[..., -1])

            def step(carry, inp):
                st, cd = inp
                new = carry * cd[:, :, None, None] + st
                return (new, carry)
            st_seq = jnp.moveaxis(states, 1, 0)
            cd_seq = jnp.moveaxis(chunk_decay, 1, 0)
            init = jnp.zeros_like(st_seq[0])
            _, prev = jax.lax.scan(step, init, (st_seq, cd_seq))
            prev = jnp.moveaxis(prev, 0, 1)
            Yoff = jnp.einsum('bclhn,bchpn,bchl->bclhp', Cc, prev, jnp.exp(cs))
            Y = (Ydiag + Yoff).reshape(Bsz, S, H, P) + x * D[None, None, :, None]
            return Y
        Bsz, S, _ = hidden_states.shape
        proj = hidden_states @ in_proj_w.T
        gate, xBC, dt = jnp.split(proj, [INTER, INTER + CONV_DIM], axis=-1)
        xBC_t = jnp.swapaxes(xBC, 1, 2)
        conv = jax.lax.conv_general_dilated(xBC_t, conv_w, window_strides=(1,), padding=[(K - 1, 0)], feature_group_count=CONV_DIM)
        conv = conv + conv_b[None, :, None]
        xBC = jax.nn.silu(jnp.swapaxes(conv, 1, 2))
        x, Bm, Cm = jnp.split(xBC, [INTER, INTER + NG * SS], axis=-1)
        y = _ssd(x.reshape(Bsz, S, NH, HD), Bm.reshape(Bsz, S, NG, SS), Cm.reshape(Bsz, S, NG, SS), D, dt, dt_bias)
        y = y.reshape(Bsz, S, INTER)
        yg = y * jax.nn.silu(gate)
        yg_g = yg.reshape(Bsz, S, NG, GROUP)
        rstd = jax.lax.rsqrt(jnp.mean(jnp.square(yg_g), axis=-1, keepdims=True) + EPS)
        out = (yg_g * rstd).reshape(Bsz, S, INTER) * norm_w
        return out @ out_proj_w.T

    def _L1_ffn_ref(x, W_base, b_base, W_gate, W_thr, b_thr, A_w, B_w):
        import jax, jax.numpy as jnp
        import numpy as np
        B, S, D, O, E, R = (4, 256, 512, 512, 8, 16)
        SCALING = 32.0 / 16.0
        MAX_THRESHOLD = 0.125
        base = jnp.einsum('bsd,od->bso', x, W_base) + b_base
        xf = x.reshape(-1, D)
        gate = jax.nn.softmax(xf @ W_gate.T, axis=-1)
        thr = jax.nn.sigmoid(xf @ W_thr + b_thr[0]) * MAX_THRESHOLD
        adapted = gate - thr[:, None]
        selected = (adapted >= 0).astype(x.dtype)
        w = adapted * selected
        wsum = jnp.sum(w, axis=-1, keepdims=True)
        wsum = jnp.where(wsum == 0, jnp.ones_like(wsum), wsum)
        w = w / wsum
        h = jnp.einsum('nd,erd->ner', xf, A_w)
        moe = jnp.einsum('ner,ne,eor->no', h, w, B_w) * SCALING
        return base + moe.reshape(base.shape)

    def _L2_xattn_ref(query, key, value, mask, wq, wk, wv, wo, curr_seq_pos):
        import jax, jax.numpy as jnp
        import numpy as np
        BS, SEQ, D_MODEL = (4, 128, 512)
        N_Q_HEADS, N_KV_HEADS, D_K, D_V = (32, 8, 128, 128)
        ROPE_BASE = 10000.0

        def _rotate_half(x):
            x1, x2 = jnp.split(x, 2, axis=-1)
            return jnp.concatenate([-x2, x1], axis=-1)

        def _apply_rope(x, pos0):
            d = x.shape[-1]
            seq = x.shape[2]
            inv_freq = 1.0 / ROPE_BASE ** (jnp.arange(0, d, 2, dtype=jnp.float32) / d)
            pos = (pos0 + jnp.arange(seq)).astype(jnp.float32)
            ang = pos[:, None] * inv_freq[None, :]
            cos = jnp.concatenate([jnp.cos(ang), jnp.cos(ang)], axis=-1)
            sin = jnp.concatenate([jnp.sin(ang), jnp.sin(ang)], axis=-1)
            return x * cos[None, None] + _rotate_half(x) * sin[None, None]
        bs, sq, _ = query.shape
        n_groups = N_Q_HEADS // N_KV_HEADS
        q = (query @ wq).reshape(bs, sq, N_Q_HEADS, D_K).transpose((0, 2, 1, 3))
        sk = key.shape[1]
        k = (key @ wk).reshape(bs, sk, N_KV_HEADS, 1, D_K)
        k = jnp.repeat(k, n_groups, axis=3).reshape(bs, sk, N_Q_HEADS, D_K).transpose((0, 2, 1, 3))
        v = (value @ wv).reshape(bs, sk, N_KV_HEADS, 1, D_V)
        v = jnp.repeat(v, n_groups, axis=3).reshape(bs, sk, N_Q_HEADS, D_V).transpose((0, 2, 1, 3))
        scale = jnp.sqrt(jnp.float32(D_K))
        q = _apply_rope(q, curr_seq_pos)
        k = _apply_rope(k, curr_seq_pos)
        raw = jnp.einsum('bhqd,bhkd->bhqk', q, k) / scale
        masked = raw + mask[:bs, None, curr_seq_pos:curr_seq_pos + sq, :sk]
        attn = jax.nn.softmax(masked, axis=-1)
        out = jnp.einsum('bhqk,bhkd->bhqd', attn, v)
        out = out.transpose((0, 2, 1, 3)).reshape(bs, sq, N_Q_HEADS * D_V)
        return out @ wo

    def _L2_attn_ref(hidden_states, wq, wk, wv, wo):
        import jax, jax.numpy as jnp
        import numpy as np
        import math
        HIDDEN = 512
        N_HEADS = 32
        N_KV_HEADS = 8
        HEAD_DIM = HIDDEN // N_HEADS
        GROUPS = N_HEADS // N_KV_HEADS
        ROPE_THETA = 10000.0
        TOKEN_BUDGET = 128
        INIT_BUDGET = 128
        RECENT_BUDGET = 128
        CHUNK = 16
        B, S = (1, 256)

        def _rotate_half(x):
            x1, x2 = jnp.split(x, 2, axis=-1)
            return jnp.concatenate([-x2, x1], axis=-1)

        def _rope(seq_len, dtype):
            inv_freq = 1.0 / ROPE_THETA ** (jnp.arange(0, HEAD_DIM, 2, dtype=jnp.float32) / HEAD_DIM)
            freqs = jnp.arange(seq_len, dtype=jnp.float32)[:, None] * inv_freq[None, :]
            emb = jnp.concatenate([freqs, freqs], axis=-1)
            return (jnp.cos(emb).astype(dtype), jnp.sin(emb).astype(dtype))
        b, s, _ = hidden_states.shape
        dtype = hidden_states.dtype
        NEG = jnp.finfo(dtype).min
        q = (hidden_states @ wq.T).reshape(b, s, N_HEADS, HEAD_DIM).transpose(0, 2, 1, 3)
        k = (hidden_states @ wk.T).reshape(b, s, N_KV_HEADS, HEAD_DIM).transpose(0, 2, 1, 3)
        v = (hidden_states @ wv.T).reshape(b, s, N_KV_HEADS, HEAD_DIM).transpose(0, 2, 1, 3)
        cos, sin = _rope(s, dtype)
        q = q * cos[None, None] + _rotate_half(q) * sin[None, None]
        k = k * cos[None, None] + _rotate_half(k) * sin[None, None]
        k = jnp.repeat(k, GROUPS, axis=1)
        v = jnp.repeat(v, GROUPS, axis=1)
        scores = jnp.einsum('bhqd,bhkd->bhqk', q, k) / math.sqrt(HEAD_DIM)
        q_pos = jnp.arange(s)[:, None]
        k_pos = jnp.arange(s)[None, :]
        causal = k_pos <= q_pos
        masked = jnp.where(causal[None, None], scores, NEG)
        pad = -s % CHUNK
        padded = jnp.pad(masked, ((0, 0), (0, 0), (0, 0), (0, pad)), constant_values=NEG)
        n_chunks = (s + pad) // CHUNK
        chunk_max = padded.reshape(b, N_HEADS, s, n_chunks, CHUNK).max(axis=-1)
        k_top = min(max(3, TOKEN_BUDGET // CHUNK), n_chunks)
        _, topk_idx = jax.lax.top_k(chunk_max, k_top)
        chunk_mask = jnp.any(topk_idx[..., None] == jnp.arange(n_chunks), axis=-2)
        tok_mask = jnp.repeat(chunk_mask, CHUNK, axis=-1)[..., :s]
        init_mask = k_pos < INIT_BUDGET
        recent_mask = k_pos > q_pos - RECENT_BUDGET
        allowed = causal[None, None] & (tok_mask | init_mask[None, None] | recent_mask[None, None])
        final = jnp.where(allowed, scores, NEG)
        attn = jax.nn.softmax(final, axis=-1)
        out = jnp.einsum('bhqk,bhkd->bhqd', attn, v)
        out = out.transpose(0, 2, 1, 3).reshape(b, s, N_HEADS * HEAD_DIM)
        return out @ wo.T

    def _L2_ffn_ref(x, gate_w, gate_b, expert_w, expert_b):
        import jax, jax.numpy as jnp
        import numpy as np
        NUM_EXPERTS = 8
        D_IN = 512
        D_OUT = 512
        orig_shape = x.shape
        xf = x.reshape(-1, x.shape[-1])
        gate_logits = xf @ gate_w.T + gate_b
        gates = jax.nn.softmax(gate_logits, axis=-1)
        selected = jnp.argmax(gates, axis=-1)
        out = jnp.zeros((xf.shape[0], expert_w.shape[1]), dtype=xf.dtype)
        for j in range(expert_w.shape[0]):
            yj = xf @ expert_w[j].T + expert_b[j]
            out = out + jnp.where((selected == j)[:, None], yj, 0.0)
        return out.reshape(*orig_shape[:-1], expert_w.shape[1])

    def _L3_xattn_ref(hidden_states, cross_attention_states, attention_mask, Wq, Wk, Wv, Wo, q_norm_w, k_norm_w):
        import jax, jax.numpy as jnp
        import numpy as np
        B, Q, K, D = (1, 128, 6404, 512)
        H, KVH, HD = (32, 8, 128)
        GROUPS = H // KVH
        EPS = 1e-05

        def _rmsnorm(x, w):
            xf = x.astype(jnp.float32)
            var = jnp.mean(xf * xf, axis=-1, keepdims=True)
            return (xf * jax.lax.rsqrt(var + EPS)).astype(x.dtype) * w
        bsz, q_len, _ = hidden_states.shape
        kv_len = cross_attention_states.shape[1]
        q = (hidden_states @ Wq.T).reshape(bsz, q_len, H, HD).transpose(0, 2, 1, 3)
        k = (cross_attention_states @ Wk.T).reshape(bsz, kv_len, KVH, HD).transpose(0, 2, 1, 3)
        v = (cross_attention_states @ Wv.T).reshape(bsz, kv_len, KVH, HD).transpose(0, 2, 1, 3)
        q = _rmsnorm(q, q_norm_w)
        k = jnp.repeat(k, GROUPS, axis=1)
        v = jnp.repeat(v, GROUPS, axis=1)
        k = _rmsnorm(k, k_norm_w)
        scale = 1.0 / np.sqrt(HD)
        scores = jnp.einsum('bhqd,bhkd->bhqk', q, k) * scale
        scores = scores + attention_mask[:, :, :, :kv_len]
        probs = jax.nn.softmax(scores.astype(jnp.float32), axis=-1).astype(q.dtype)
        out = jnp.einsum('bhqk,bhkd->bhqd', probs, v)
        out = out.transpose(0, 2, 1, 3).reshape(bsz, q_len, H * HD)
        return out @ Wo.T

    def _L3_attn_ref(tokens, weight_qkv, weight_proj):
        import jax, jax.numpy as jnp
        import numpy as np
        SEQ, BATCH, HIDDEN = (256, 1, 512)
        NUM_HEADS, NUM_KV_HEADS, HEAD_DIM = (32, 8, 128)
        Q_PER_GROUP = NUM_HEADS // NUM_KV_HEADS
        TOTAL_PROJ = NUM_KV_HEADS * (Q_PER_GROUP + 2) * HEAD_DIM
        S, B, H = tokens.shape
        scale = 1.0 / HEAD_DIM ** 0.5
        qkv = jnp.einsum('sbh,ph->sbp', tokens, weight_qkv)
        qkv = qkv.reshape(S, B, NUM_KV_HEADS, Q_PER_GROUP + 2, HEAD_DIM)
        q = qkv[:, :, :, :Q_PER_GROUP, :].reshape(S, B, NUM_HEADS, HEAD_DIM)
        k = qkv[:, :, :, Q_PER_GROUP, :]
        v = qkv[:, :, :, Q_PER_GROUP + 1, :]
        k = jnp.repeat(k, Q_PER_GROUP, axis=2)
        v = jnp.repeat(v, Q_PER_GROUP, axis=2)
        q = q.transpose(1, 2, 0, 3)
        k = k.transpose(1, 2, 0, 3)
        v = v.transpose(1, 2, 0, 3)
        scores = jnp.einsum('bhsd,bhtd->bhst', q, k) * scale
        causal = jnp.tril(jnp.ones((S, S), dtype=bool))
        scores = jnp.where(causal, scores, jnp.finfo(scores.dtype).min)
        attn = jax.nn.softmax(scores, axis=-1)
        out = jnp.einsum('bhst,bhtd->bhsd', attn, v)
        out = out.transpose(2, 0, 1, 3).reshape(S, B, NUM_HEADS * HEAD_DIM)
        return jnp.einsum('sbe,he->sbh', out, weight_proj)

    def _L3_ffn_ref(x, W_base, b_base, enc0, enc1, coefs0, coefs1, mask0, mask1):
        import math
        import jax, jax.numpy as jnp
        import numpy as np
        SCALING = 16.0 / 32.0

        def real_fourier_orthogonal_multiply(c):
            n = c.shape[-1]
            sqrt_n = math.sqrt(n)
            pair_scale = math.sqrt(n / 2.0)
            max_f = (n - 1) // 2
            work = c.astype(jnp.float32)
            dc = (work[..., 0] * sqrt_n)[..., None].astype(jnp.complex64)
            cos = work[..., 1:1 + 2 * max_f:2] * pair_scale
            sin = work[..., 2:2 + 2 * max_f:2] * pair_scale
            mid = (cos - 1j * sin).astype(jnp.complex64)
            parts = [dc, mid]
            if n % 2 == 0:
                parts.append((work[..., -1] * sqrt_n)[..., None].astype(jnp.complex64))
            spectrum = jnp.concatenate(parts, axis=-1)
            return jnp.fft.irfft(spectrum, n=n, axis=-1).astype(c.dtype)
        base = jnp.einsum('bsd,od->bso', x, W_base) + b_base
        e0 = jnp.einsum('bsd,rd->bsr', x, enc0)
        e1 = jnp.einsum('bsd,rd->bsr', x, enc1)
        w0 = coefs0 * mask0.astype(coefs0.dtype)
        w1 = coefs1 * mask1.astype(coefs1.dtype)
        decoded = jnp.einsum('bsr,eor->ebso', e0, w0) + jnp.einsum('bsr,eor->ebso', e1, w1)
        transformed = real_fourier_orthogonal_multiply(decoded)
        update = transformed.sum(axis=0)
        return base + update * SCALING
    x = x + _L0_xattn_ref(_layernorm(x, axis=-1), ctx_4096, L0_xattn_Wq, L0_xattn_bq, L0_xattn_Wk, L0_xattn_bk)
    x = x + _L0_attn_ref(_layernorm(x, axis=-1), L0_attn_wq, L0_attn_wk, L0_attn_wv, L0_attn_wo)
    x = x + _L0_ffn_ref(_layernorm(x, axis=-1), L0_ffn_lora_A, L0_ffn_lora_B, L0_ffn_W, L0_ffn_bias, L0_ffn_lora_weights)
    x = x + _L1_xattn_ref(_layernorm(x, axis=-1), ctx_4096, L1_xattn_Wq_w, L1_xattn_Wq_b, L1_xattn_Wk_w, L1_xattn_Wk_b, L1_xattn_fn_w, L1_xattn_qn_w, L1_xattn_kn_w)
    x = x + _L1_attn_ref(_layernorm(x, axis=-1), L1_attn_in_proj_w, L1_attn_conv_w, L1_attn_conv_b, L1_attn_dt_bias, L1_attn_D, L1_attn_norm_w, L1_attn_out_proj_w)
    x = x + _L1_ffn_ref(_layernorm(x, axis=-1), L1_ffn_W_base, L1_ffn_b_base, L1_ffn_W_gate, L1_ffn_W_thr, L1_ffn_b_thr, L1_ffn_A_w, L1_ffn_B_w)
    x = x + _L2_xattn_ref(_layernorm(x, axis=-1), ctx_4096, ctx_4096, mask_BxSxS2_ff0, L2_xattn_wq, L2_xattn_wk, L2_xattn_wv, L2_xattn_wo, 0)
    x = x + _L2_attn_ref(_layernorm(x, axis=-1), L2_attn_wq, L2_attn_wk, L2_attn_wv, L2_attn_wo)
    x = x + _L2_ffn_ref(_layernorm(x, axis=-1), L2_ffn_gate_w, L2_ffn_gate_b, L2_ffn_expert_w, L2_ffn_expert_b)
    x = x + _L3_xattn_ref(_layernorm(x, axis=-1), ctx_4096, mask_1x1xSxS2_ff0, L3_xattn_Wq, L3_xattn_Wk, L3_xattn_Wv, L3_xattn_Wo, L3_xattn_q_norm_w, L3_xattn_k_norm_w)
    x = x + _L3_attn_ref(_layernorm(x, axis=-1), L3_attn_weight_qkv, L3_attn_weight_proj)
    x = x + _L3_ffn_ref(_layernorm(x, axis=-1), L3_ffn_W_base, L3_ffn_b_base, L3_ffn_enc0, L3_ffn_enc1, L3_ffn_coefs0, L3_ffn_coefs1, L3_ffn_mask0, L3_ffn_mask1)
    return x

_drawn_inputs = setup_inputs


def setup_inputs(seed=0):
    import zlib

    import numpy as np

    out = dict(_drawn_inputs(seed))
    spreads = {'L0_xattn_bq': (0.0, 0.1),
     'L0_xattn_bk': (0.0, 0.8),
     'L0_ffn_lora_weights': (0.125, 0.2),
     'L1_xattn_fn_w': (1.0, 0.2),
     'L1_xattn_qn_w': (1.0, 0.6),
     'L1_xattn_kn_w': (1.0, 0.6),
     'L1_attn_conv_b': (0.0, 0.1),
     'L1_attn_dt_bias': (1.0, 0.6),
     'L1_attn_D': (1.0, 0.2),
     'L1_attn_norm_w': (1.0, 0.2),
     'L3_xattn_q_norm_w': (1.0, 0.6),
     'L3_xattn_k_norm_w': (1.0, 0.6)}
    factors = {'L0_ffn_bias': 8.0,
     'L1_xattn_Wq_b': 8.0,
     'L1_xattn_Wk_b': 8.0,
     'L1_ffn_b_base': 8.0,
     'L2_xattn_wq': 8.0,
     'L2_xattn_wk': 8.0,
     'L2_attn_wq': 8.0,
     'L2_attn_wk': 8.0,
     'L2_ffn_gate_b': 5.34,
     'L2_ffn_expert_b': 8.0,
     'L3_ffn_b_base': 8.0,
     'L3_ffn_enc0': 6.352,
     'L3_ffn_enc1': 8.0,
     'L3_ffn_coefs0': 6.962,
     'L3_ffn_coefs1': 8.0}
    for name, (base, spread) in spreads.items():
        noise = np.random.default_rng([zlib.crc32(name.encode()), seed]).standard_normal(out[name].shape)
        drawn = base * np.exp(spread * noise) if base else spread * noise
        out[name] = jnp.asarray(drawn.astype(out[name].dtype))
    for name, factor in factors.items():
        out[name] = (out[name] * factor).astype(out[name].dtype)
    return out
```

```python
from contextlib import ExitStack

import numpy as np

import concourse.bass as bass
from concourse import mybir

F32 = mybir.dt.float32
U8 = mybir.dt.uint8
ACT = mybir.ActivationFunctionType
ALU = mybir.AluOpType
AX_X = mybir.AxisListType.X

P = 128
D = 512
DC = D // P
KEYS = 2048
KT = KEYS // P
GROUPS = 8
PER_GROUP = 4
NEG = -1.0e30
NEG_MAX = -3.0e38


class Phase:

    def __init__(self, prog, events, times=1):
        self.prog, self.at, self.per = prog, {}, {}
        for name, sem in events:
            self.per[sem] = self.per.get(sem, 0) + 1
            self.at[name] = (sem, self.per[sem])
        self.base = dict(prog.counts)
        for sem, n in self.per.items():
            prog.counts[sem] = prog.counts.get(sem, 0) + n * times

    def value(self, name, i=0):
        sem, k = self.at[name]
        return self.base.get(sem, 0) + k + i * self.per[sem]

    def filled(self, name, i=0):
        return self.prog.sem("filled_" + self.at[name][0]), self.value(name, i)

    def drained(self, name, i=0):
        return self.prog.sem("drained_" + self.at[name][0]), self.value(name, i) + 1

    def room(self, name, i=0):
        return self.prog.sem("drained_" + self.at[name][0]), self.value(name, i)

    def fill(self, name):
        return self.prog.sem("filled_" + self.at[name][0])

    def drain(self, name):
        return self.prog.sem("drained_" + self.at[name][0])

    def done(self, name, i=0):
        return self.prog.sem(self.at[name][0]), self.value(name, i)

    def mark(self, name):
        return self.prog.sem(self.at[name][0])

    def loaded(self, name, i=0):
        return self.prog.sem(self.at[name][0]), self.value(name, i) * 16

    def before(self, sem, i=0, kind=""):
        return self.prog.sem(kind + sem), self.base.get(sem, 0) + (kind == "drained_") + i * self.per.get(sem, 0)


class Chain:

    def __init__(self, eng, sem):
        self.eng, self.sem, self.n, self.i, self.per = eng, sem, 0, None, 0

    def link(self, ins):
        self.n += 1
        ins.then_inc(self.sem, 1)
        self.eng.wait_ge(self.sem, self.n if self.i is None else self.n + self.i * self.per)

    def loop(self, i, per):
        self.i, self.per, self.start = i, per, self.n

    def end(self, times):
        assert self.n - self.start == self.per, f"{self.n - self.start} links an iteration"
        self.n, self.i = self.start + self.per * times, None


def columns(*parts):
    out, at = {}, 0
    for name, n in parts:
        out[name] = slice(at, at + n)
        at += n
    out["all"] = at
    return out


HALF = P // 2
C_CONST = columns(("ident", P), ("causal", P), ("minus_half", 16))
C_L0X = columns(("wq", DC * D), ("wk", DC * D), ("bq", D), ("bk", D))
C_L0F = columns(("w", DC * D), ("a", DC * P), ("b", D), ("bias", D), ("coef", 1))
C_L1X = columns(("wq", DC * D), ("wk", DC * D), ("bq", D), ("bk", D), ("fn_row", D),
                ("fn", DC), ("qn", DC), ("kn", DC))
E8 = 8
C_L1F = columns(("w", DC * D), ("a", DC * P), ("gate", DC * (E8 + 1)), ("b", D), ("bias", D), ("bthr", 1))
HD2 = 16
C_L2A = columns(("wq", DC * D), ("wkv", DC * 256), ("wo", DC * D), ("cos", 8), ("sin", 8))
C_L2F = columns(("gate", DC * E8), ("bgate", E8), ("rank", E8))
R3 = 40
C_L3F = columns(("w", DC * D), ("enc", DC * R3), ("coef", DC * 3 * R3), ("bias", D))
C_ROPE_Q = columns(("cos", HALF), ("sin", HALF), ("nsin", HALF))
C_QKV = columns(("q", DC * D), ("kv", DC * 256))


AREA = columns(("ctxT", DC * KEYS), ("ctx", KT * D), ("weights", 13312), ("pack0", 5760), ("pack1", 5760),
               ("work", 9728), ("x", D), ("xn", D), ("xnT", D), ("ident", P), ("causal", P),
               ("minus_half", 16), ("zeros", P), ("small", 128))


class Program:

    def __init__(self, nc, ctx, dram):
        self.nc, self.dram, self.counts, self.sems = nc, dram, {}, {}
        self.ctx = ctx
        self.mem = ctx.enter_context(nc.sbuf_tensor("mem", [P, AREA["all"]], F32))
        self.bank = [ctx.enter_context(nc.psum_tensor(f"bank{b}", [P, 512], F32)) for b in range(4, 8)]
        self.wide = ctx.enter_context(nc.psum_tensor("wide", [P, 4 * 512], F32))
        self.x, self.xn, self.ident = self.area("x"), self.area("xn"), self.area("ident")
        self.zeros = self.area("zeros")
        self.causal, self.minus_half = self.area("causal"), self.area("minus_half")
        self.xnT = self.area("xnT").rearrange("p (o t) -> p o t", o=DC)
        self.ctxT = self.area("ctxT").rearrange("p (o s) -> p o s", o=DC)
        self.ctxN = self.area("ctx").rearrange("p (t d) -> p t d", t=KT)
        small = self.area("small")
        self.stats, self.mv, self.var, self.rstd = small[:, 0:6], small[:, 6:8], small[:, 8:9], small[:, 9:10]
        self.small = small[:, 16:128]

    def area(self, name, a=0, b=None):
        s = AREA[name]
        return self.mem[:, s.start + a:(s.start + b if b is not None else s.stop)]

    def ps(self, b):
        return self.wide[:, 512 * b:512 * b + 512] if b < 4 else self.bank[b - 4][:, :]

    def sem(self, name):
        if name not in self.sems:
            self.sems[name] = self.ctx.enter_context(self.nc.semaphore(name))
        return self.sems[name]


def heads(ap, h):
    return ap.rearrange("p (h n) -> p h n", h=h)


def per_head(ap, n):
    return ap.unsqueeze(2).broadcast_to([ap.shape[0], ap.shape[1], n])


def every_head(ap, h):
    return ap.unsqueeze(1).broadcast_to([ap.shape[0], h, ap.shape[1]])


LN_EVENTS = [("ln_var", "ln_var"), ("ln_rstd", "ln_rstd"), ("ln_xn", "ln_xn"), ("ln", "4")]


class Layer:
    def __init__(self, k):
        self.k = k

    def sp(self, sp):
        pass

    def pool(self, pool):
        self.ln_pool(pool, self.p)

    def ln_dve(self, v, ph):
        k = self.k
        k.link(v.bn_stats(k.stats, k.x))
        k.link(v.bn_aggr(k.mv, k.stats))
        v.tensor_scalar(k.var, k.mv[:, 1:2], 1e-5, None, ALU.add).then_inc(ph.mark("ln_var"), 1)
        v.wait_ge(*ph.done("ln_rstd"))
        v.tensor_scalar(k.xn, k.x, k.mv[:, 0:1], k.rstd, ALU.subtract, ALU.mult).then_inc(ph.mark("ln_xn"), 1)

    def add_output(self, v, ph):
        k = self.k
        v.tensor_tensor(k.x, k.ps(7), k.x, ALU.add).then_inc(ph.drain("y"), 1)
        v.wait_ge(*ph.drained("y"))

    def ln_pool(self, pool, ph):
        k = self.k
        pool.wait_ge(*ph.done("ln_var"))
        pool.tensor_tensor(k.rstd, k.var, k.minus_half[:, 0:1], ALU.pow).then_inc(ph.mark("ln_rstd"), 1)

    def ln_pe(self, pe, ph):
        k = self.k
        pe.wait_ge(*ph.done("ln_xn"))
        pe.wait_ge(*ph.room("ln"))
        self.turn(pe, k.ps(4), k.xn, DC).then_inc(ph.fill("ln"), 1)

    def ln_act(self, act, ph):
        k = self.k
        act.wait_ge(*ph.filled("ln"))
        act.activation(k.xnT, heads(k.ps(4), DC), ACT.Copy).then_inc(ph.drain("ln"), 1)

    def turn(self, pe, out, src, n):
        for j in range(n):
            last = pe.transpose(out[:, j * P:(j + 1) * P], src[:, j * P:(j + 1) * P], self.k.ident)
        return last

    def project(self, pe, out, w, n, start=True, stop=True, src=None):
        src = self.k.xnT if src is None else src
        for o in range(DC):
            last = pe.matmul(out[:, 0:n], src[:, o, :], w[:, o, :], start=start and o == 0, stop=stop and o == DC - 1)
        return last

    def softmax_turn_pe(self, pe, ph, probs, names):
        for j, name in enumerate(names):
            pe.wait_ge(*ph.room(name))
            self.turn(pe, self.k.ps(int(ph.at[name][0])), probs[:, j * 512:(j + 1) * 512], 4).then_inc(ph.fill(name), 1)


class L0Xattn(Layer):
    TURNS = ["t0", "t1", "t2", "t3"]

    def __init__(self, k):
        super().__init__(k)
        self.y = self.p = Phase(k, [("load_pack", "load_pack0"), ("load_ctxT", "load_ctxT"), ("load_ctx", "load_ctx")] + LN_EVENTS + [
            ("q", "5"), ("qT", "4"), ("q2", "5"), ("q2T", "4"), ("s", "0"), ("shift", "shift"),
            ("t0", "4"), ("t1", "5"), ("t2", "4"), ("t3", "5"), ("y", "7")])
        pack = k.area("pack0")
        self.wq, self.wk = (pack[:, C_L0X[n]].rearrange("p (o n) -> p o n", o=DC) for n in ("wq", "wk"))
        self.bq, self.bk = pack[:, C_L0X["bq"]], pack[:, C_L0X["bk"]]
        w = k.area("work")
        self.q, self.qT, self.q2, self.q2T = w[:, 0:512], heads(w[:, 512:1024], DC), w[:, 1024:1536], heads(w[:, 1536:2048], DC)
        self.junk = w[:, 2048:2560]
        self.probs, self.probsT = w[:, 2560:4608], heads(w[:, 4608:6656], KT)
        self.c, self.m, self.b, self.sum, self.inv = (k.small[:, j:j + 1] for j in range(5))
        self.scale = float(D) ** -0.5

    def sp(self, sp):
        k = self.k
        sp.dma_start(k.area("pack0", 0, C_L0X["all"]), k.dram["l0x"]).then_inc(self.p.mark("load_pack"), 16)
        sp.dma_start(k.area("ctxT"), k.dram["ctxT"]).then_inc(self.p.mark("load_ctxT"), 16)
        sp.dma_start(k.area("ctx"), k.dram["ctx"]).then_inc(self.p.mark("load_ctx"), 16)

    def pe(self, pe):
        k, p = self.k, self.p
        self.ln_pe(pe, p)
        pe.wait_ge(*p.drained("ln"))
        pe.wait_ge(*p.loaded("load_pack"))
        pe.wait_ge(*p.room("q"))
        self.project(pe, k.ps(5), self.wq, D).then_inc(p.fill("q"), 1)
        pe.wait_ge(*p.drained("q"))
        self.turn(pe, k.ps(4), self.q, DC).then_inc(p.fill("qT"), 1)
        pe.wait_ge(*p.drained("qT"))
        self.project(pe, k.ps(5), self.wk, D, src=self.qT).then_inc(p.fill("q2"), 1)
        pe.wait_ge(*p.drained("q2"))
        self.turn(pe, k.ps(4), self.q2, DC).then_inc(p.fill("q2T"), 1)
        pe.wait_ge(*p.drained("q2T"))
        pe.wait_ge(*p.loaded("load_ctxT"))
        pe.wait_ge(*p.room("s"))
        for c in range(4):
            last = self.project(pe, k.ps(c), k.ctxT[:, :, c * 512:(c + 1) * 512], 512, src=self.q2T)
        last.then_inc(p.fill("s"), 1)
        pe.wait_ge(*p.drained("s"))
        self.softmax_turn_pe(pe, p, self.probs, self.TURNS)
        pe.wait_ge(*p.loaded("load_ctx"))
        pe.wait_ge(*p.room("y"))
        for t in range(KT):
            if t % 4 == 0:
                pe.wait_ge(*p.drained(self.TURNS[t // 4]))
            last = pe.matmul(k.ps(7), self.probsT[:, t, :], k.ctxN[:, t, :], start=t == 0, stop=t == KT - 1)
        last.then_inc(p.fill("y"), 1)

    def act(self, act):
        k, p = self.k, self.p
        self.ln_act(act, p)
        for name, out in (("qT", self.qT), ("q2T", self.q2T)):
            act.wait_ge(*p.filled(name))
            act.activation(out, heads(k.ps(4), DC), ACT.Copy).then_inc(p.drain(name), 1)
        act.wait_ge(*p.done("shift"))
        act.activation(self.probs, k.wide[:, :], ACT.Exp, bias=self.b, scale=self.scale, accum_out=self.sum).then_inc(p.drain("s"), 1)
        for j in (1, 3):
            name = self.TURNS[j]
            act.wait_ge(*p.filled(name))
            act.activation(self.probsT[:, 4 * j:4 * j + 4, :], heads(k.ps(5), 4), ACT.Copy).then_inc(p.drain(name), 1)

    def dve(self, v):
        k, p = self.k, self.p
        self.ln_dve(v, p)
        v.wait_ge(*p.loaded("load_pack"))
        v.wait_ge(*p.filled("q"))
        v.tensor_tensor(self.q, k.ps(5), self.bq, ALU.add).then_inc(p.drain("q"), 1)
        v.wait_ge(*p.drained("q"))
        k.link(v.tensor_tensor_reduce(out=self.junk, in0=self.q, in1=self.bk, scale=1.0, scalar=0.0,
                                      op0=ALU.mult, op1=ALU.add, accum_out=self.c))
        v.wait_ge(*p.filled("q2"))
        v.tensor_copy(self.q2, k.ps(5)).then_inc(p.drain("q2"), 1)
        v.wait_ge(*p.filled("s"))
        k.link(v.reduce_max(self.m, k.wide[:, :], AX_X))
        k.link(v.tensor_scalar(self.m, self.m, self.c, None, ALU.add))
        v.tensor_scalar(self.b, self.c, self.m, self.scale, ALU.subtract, ALU.mult).then_inc(p.mark("shift"), 1)
        for j in (0, 2):
            name = self.TURNS[j]
            v.wait_ge(*p.filled(name))
            v.tensor_copy(self.probsT[:, 4 * j:4 * j + 4, :], heads(k.ps(4), 4)).then_inc(p.drain(name), 1)
        v.wait_ge(*p.drained("s"))
        k.link(v.reciprocal(self.inv, self.sum))
        v.wait_ge(*p.filled("y"))
        v.scalar_tensor_tensor(out=k.x, in0=k.ps(7), scalar=self.inv, in1=k.x, op0=ALU.mult, op1=ALU.add).then_inc(p.drain("y"), 1)
        v.wait_ge(*p.drained("y"))


class L0Ffn(Layer):
    def __init__(self, k):
        super().__init__(k)
        self.y = self.p = Phase(k, [("load_pack", "load_pack1")] + LN_EVENTS + [
            ("h", "5"), ("ready", "l0f_ready"), ("hT", "4"), ("y", "7")])
        pack = k.area("pack1")
        self.w, self.a = (pack[:, C_L0F[n]].rearrange("p (o n) -> p o n", o=DC) for n in ("w", "a"))
        self.b, self.bias, self.coef = (pack[:, C_L0F[n]] for n in ("b", "bias", "coef"))
        w = k.area("work")
        self.h, self.hT, self.coef2 = w[:, 0:P], w[:, P:2 * P], k.small[:, 0:1]

    def sp(self, sp):
        k = self.k
        sp.dma_start(k.area("pack1", 0, C_L0F["all"]), k.dram["l0f"]).then_inc(self.p.mark("load_pack"), 16)

    def pe(self, pe):
        k, p = self.k, self.p
        self.ln_pe(pe, p)
        pe.wait_ge(*p.drained("ln"))
        pe.wait_ge(*p.loaded("load_pack"))
        pe.wait_ge(*p.room("h"))
        self.project(pe, k.ps(5), self.a, P).then_inc(p.fill("h"), 1)
        pe.wait_ge(*p.room("y"))
        self.project(pe, k.ps(7), self.w, D, stop=False)
        pe.wait_ge(*p.drained("h"))
        self.turn(pe, k.ps(4), self.h, 1).then_inc(p.fill("hT"), 1)
        pe.wait_ge(*p.drained("hT"))
        pe.matmul(k.ps(7), self.hT, self.b, start=False, stop=True).then_inc(p.fill("y"), 1)

    def act(self, act):
        k, p = self.k, self.p
        self.ln_act(act, p)
        act.wait_ge(*p.filled("h"))
        act.activation(self.h, k.ps(5)[:, 0:P], ACT.Copy).then_inc(p.drain("h"), 1)

    def dve(self, v):
        k, p = self.k, self.p
        self.ln_dve(v, p)
        v.wait_ge(*p.loaded("load_pack"))
        k.link(v.tensor_scalar(self.coef2, self.coef, 2.0, None, ALU.mult))
        v.wait_ge(*p.filled("hT"))
        v.tensor_scalar(self.hT, k.ps(4)[:, 0:P], self.coef2, None, ALU.mult).then_inc(p.drain("hT"), 1)
        k.link(v.tensor_tensor(k.x, k.x, self.bias, ALU.add))
        v.wait_ge(*p.filled("y"))
        self.add_output(v, p)


class SelfAttention(Layer):
    PROJECT = [("load_qkv", "load_qkv"), ("q", "0"), ("kv", "1"), ("v", "v_ready"), ("qT", "4"), ("kT", "5")]
    ATTEND = [("load_wo", "load_wo"), ("s", "2"), ("shift", "shift"), ("exp", "exp"), ("norm", "norm"),
              ("pT", "3"), ("oT", "6")]

    def __init__(self, k):
        super().__init__(k)
        self.first = self.p = Phase(k, [("load_rope", "load_rope")] + LN_EVENTS + self.PROJECT)
        self.body = Phase(k, self.ATTEND + [("part", "part_done")] + self.PROJECT, GROUPS - 1)
        self.y = self.last = Phase(k, self.ATTEND + [("y", "7")])
        m = k.area("weights", 0, 5120)
        self.wqkv, self.wo = m[:, 0:3072], m[:, 3072:5120].rearrange("p (h n) -> p h n", h=PER_GROUP)
        self.wq = self.wqkv[:, C_QKV["q"]].rearrange("p (o n) -> p o n", o=DC)
        self.wkv = self.wqkv[:, C_QKV["kv"]].rearrange("p (o n) -> p o n", o=DC)
        w = k.area("work")
        take = iter(range(0, 9728, 512))
        nxt = lambda: w[:, (a := next(take)):a + 512]
        self.qn, self.qT, self.tmp, self.probs, self.probsT, self.oT, kk = (nxt() for _ in range(7))
        self.tabs = k.area("pack1", 5000, 5000 + C_ROPE_Q["all"])
        self.kn, self.kT, self.v, self.tmpk = (kk[:, j * P:(j + 1) * P] for j in range(4))
        self.max, self.sum, self.inv = (k.small[:, 4 * j:4 * j + 4] for j in range(3))
        self.scale = float(P) ** -0.5

    def sp(self, sp):
        k = self.k
        sp.dma_start(self.tabs[:, 0:C_ROPE_Q["all"]], k.dram["rope_self"]).then_inc(self.first.mark("load_rope"), 16)
        src = k.dram["l0a"]

        def load(g, qkv):
            a, b = (0, 3072) if qkv else (3072, 5120)
            row = src[g] if isinstance(g, int) else src[bass.ds(g, 1), :, :].rearrange("a p n -> p (a n)")
            return sp.dma_start(self.wqkv if qkv else self.wo.rearrange("p h n -> p (h n)"), row[:, a:b])

        load(0, True).then_inc(self.first.mark("load_qkv"), 16)
        load(0, False).then_inc(self.body.mark("load_wo"), 16)
        sp.wait_ge(*self.first.filled("kv"))
        load(1, True).then_inc(self.body.mark("load_qkv"), 16)
        with sp.Fori(0, GROUPS - 2) as g:
            sp.wait_ge(*self.body.filled("kv", g))
            load(g + 2, True).then_inc(self.body.mark("load_qkv"), 16)
            sp.wait_ge(*self.body.done("part", g))
            load(g + 1, False).then_inc(self.body.mark("load_wo"), 16)
        sp.wait_ge(*self.body.done("part", GROUPS - 2))
        load(GROUPS - 1, False).then_inc(self.body.mark("load_wo"), 16)

    def pe_queries(self, pe, ph, g=0):
        k = self.k
        pe.wait_ge(*ph.loaded("load_qkv", g))
        pe.wait_ge(*ph.room("q", g))
        self.project(pe, k.ps(0), self.wq, D).then_inc(ph.fill("q"), 1)

    def pe_keys(self, pe, ph, g=0):
        k = self.k
        pe.wait_ge(*ph.room("kv", g))
        if not self.first_group(ph):
            pe.wait_ge(*ph.before("v_ready", g))
        self.project(pe, k.ps(1), self.wkv, 256).then_inc(ph.fill("kv"), 1)

    def first_group(self, ph):
        return ph is self.first

    def pe_turn(self, pe, ph, g=0):
        k = self.k
        for name, src, n in (("qT", self.qn, PER_GROUP), ("kT", self.kn, 1)):
            pe.wait_ge(*ph.drained({"qT": "q", "kT": "kv"}[name], g))
            pe.wait_ge(*ph.room(name, g))
            self.turn(pe, k.ps(int(ph.at[name][0])), src, n).then_inc(ph.fill(name), 1)

    def pe_scores(self, pe, ph, g=0):
        k = self.k
        pe.wait_ge(*ph.before("4", g, "drained_"))
        pe.wait_ge(*ph.before("5", g, "drained_"))
        pe.wait_ge(*ph.room("s", g))
        for h in range(PER_GROUP):
            last = pe.matmul(k.ps(2)[:, h * P:(h + 1) * P], self.qT[:, h * P:(h + 1) * P], self.kT, start=True, stop=True)
        last.then_inc(ph.fill("s"), 1)

    def pe_probs(self, pe, ph, g=0):
        pe.wait_ge(*ph.done("norm", g))
        pe.wait_ge(*ph.room("pT", g))
        self.turn(pe, self.k.ps(3), self.probs, PER_GROUP).then_inc(ph.fill("pT"), 1)

    def pe_attend(self, pe, ph, g=0):
        pe.wait_ge(*ph.drained("pT", g))
        pe.wait_ge(*ph.before("v_ready", g))
        pe.wait_ge(*ph.room("oT", g))
        pe.matmul(self.k.ps(6), self.v, self.probsT, start=True, stop=True).then_inc(ph.fill("oT"), 1)

    def pe_out(self, pe, ph, g=0, stop=False):
        pe.wait_ge(*ph.drained("oT", g))
        pe.wait_ge(*ph.loaded("load_wo", g))
        for h in range(PER_GROUP):
            last = pe.matmul(self.k.ps(7), self.oT[:, h * P:(h + 1) * P], self.wo[:, h, :], start=False,
                             stop=stop and h == PER_GROUP - 1, skip_group_check=True)
        return last

    def pe(self, pe):
        k = self.k
        self.ln_pe(pe, self.first)
        pe.wait_ge(*self.last.room("y"))
        pe.matmul(k.ps(7), k.zeros, k.xn, start=True, stop=False, skip_group_check=True)
        pe.wait_ge(*self.first.drained("ln"))
        self.pe_queries(pe, self.first)
        self.pe_keys(pe, self.first)
        self.pe_turn(pe, self.first)
        with pe.Fori(0, GROUPS - 1) as g:
            self.pe_scores(pe, self.body, g)
            self.pe_queries(pe, self.body, g)
            self.pe_probs(pe, self.body, g)
            self.pe_attend_and_keys(pe, self.body, g)
            self.pe_turn(pe, self.body, g)
            self.pe_out(pe, self.body, g).then_inc(self.body.mark("part"), 1)
        self.pe_scores(pe, self.last)
        self.pe_probs(pe, self.last)
        self.pe_attend(pe, self.last)
        self.pe_out(pe, self.last, stop=True).then_inc(self.last.fill("y"), 1)

    def pe_attend_and_keys(self, pe, ph, g):
        self.pe_keys(pe, ph, g)
        self.pe_attend(pe, ph, g)

    def act_values(self, act, ph, g=0):
        act.wait_ge(*ph.drained("kv", g))
        if not self.first_group(ph):
            act.wait_ge(*ph.filled("oT", g))
        act.activation(self.v, self.k.ps(1)[:, P:2 * P], ACT.Copy).then_inc(ph.mark("v"), 1)

    def act_queries_T(self, act, ph, g=0):
        act.wait_ge(*ph.filled("qT", g))
        act.activation(self.qT, self.k.ps(4), ACT.Copy).then_inc(ph.drain("qT"), 1)

    def act_exp(self, act, ph, g=0):
        act.wait_ge(*ph.done("shift", g))
        act.activation(self.probs, self.probs, ACT.Exp).then_inc(ph.mark("exp"), 1)

    def act_probs_T(self, act, ph, g=0):
        act.wait_ge(*ph.filled("pT", g))
        act.activation(self.probsT, self.k.ps(3), ACT.Copy).then_inc(ph.drain("pT"), 1)

    def act(self, act):
        self.ln_act(act, self.first)
        self.act_values(act, self.first)
        self.act_queries_T(act, self.first)
        with act.Fori(0, GROUPS - 1) as g:
            self.act_exp(act, self.body, g)
            self.act_probs_T(act, self.body, g)
            self.act_values(act, self.body, g)
            self.act_queries_T(act, self.body, g)
        self.act_exp(act, self.last)
        self.act_probs_T(act, self.last)

    def dve_rope(self, v, src, out, tmp, n):
        k = self.k
        cos, sin, nsin = (self.tabs[:, C_ROPE_Q[c]] for c in ("cos", "sin", "nsin"))
        halves = lambda ap: ap.rearrange("p (h n) -> p h n", n=HALF)
        both = lambda ap: ap.rearrange("p (h s n) -> p h s n", s=2, n=HALF)
        v.tensor_tensor(both(tmp)[:, :, 0, :], both(src)[:, :, 1, :], every_head(nsin, n), ALU.mult)
        v.tensor_tensor(both(tmp)[:, :, 1, :], both(src)[:, :, 0, :], every_head(sin, n), ALU.mult)
        k.link(v.tensor_tensor(halves(out), halves(src), every_head(cos, 2 * n), ALU.mult))
        return v.tensor_tensor(out, out, tmp, ALU.add)

    def dve_queries(self, v, ph, g=0):
        v.wait_ge(*ph.filled("q", g))
        self.dve_rope(v, self.k.ps(0), self.qn, self.tmp, PER_GROUP).then_inc(ph.drain("q"), 1)

    def dve_keys(self, v, ph, g=0):
        v.wait_ge(*ph.filled("kv", g))
        src = self.k.ps(1)[:, 0:P]
        self.dve_rope(v, src, self.kn, self.tmpk, 1).then_inc(ph.drain("kv"), 1)
        v.wait_ge(*ph.filled("kT", g))
        v.tensor_copy(self.kT, self.k.ps(5)[:, 0:P]).then_inc(ph.drain("kT"), 1)

    def dve_softmax_shift(self, v, ph, g=0):
        k = self.k
        v.wait_ge(*ph.filled("s", g))
        v.scalar_tensor_tensor(out=heads(self.probs, PER_GROUP), in0=heads(k.ps(2), PER_GROUP), scalar=self.scale,
                               in1=every_head(k.causal, PER_GROUP), op0=ALU.mult, op1=ALU.add).then_inc(ph.drain("s"), 1)
        v.wait_ge(*ph.drained("s", g))
        k.link(v.reduce_max(self.max, heads(self.probs, PER_GROUP), AX_X))
        v.tensor_tensor(heads(self.probs, PER_GROUP), heads(self.probs, PER_GROUP), per_head(self.max, P),
                        ALU.subtract).then_inc(ph.mark("shift"), 1)

    def dve_softmax_norm(self, v, ph, g=0):
        k = self.k
        v.wait_ge(*ph.done("exp", g))
        k.link(v.reduce_sum(self.sum, heads(self.probs, PER_GROUP), AX_X))
        k.link(v.reciprocal(self.inv, self.sum))
        v.tensor_tensor(heads(self.probs, PER_GROUP), heads(self.probs, PER_GROUP), per_head(self.inv, P),
                        ALU.mult).then_inc(ph.mark("norm"), 1)

    def dve_out_T(self, v, ph, g=0):
        v.wait_ge(*ph.filled("oT", g))
        v.tensor_copy(self.oT, self.k.ps(6)).then_inc(ph.drain("oT"), 1)

    def dve(self, v):
        k = self.k
        self.ln_dve(v, self.first)
        v.wait_ge(*self.first.loaded("load_rope"))
        self.dve_queries(v, self.first)
        self.dve_keys(v, self.first)
        with v.Fori(0, GROUPS - 1) as g:
            k.chain.loop(g, 5)
            self.dve_softmax_shift(v, self.body, g)
            self.dve_softmax_norm(v, self.body, g)
            self.dve_queries(v, self.body, g)
            self.dve_out_and_keys(v, self.body, g)
        k.chain.end(GROUPS - 1)
        self.dve_softmax_shift(v, self.last)
        self.dve_softmax_norm(v, self.last)
        self.dve_out_T(v, self.last)
        v.wait_ge(*self.last.filled("y"))
        self.add_output(v, self.last)

    def dve_out_and_keys(self, v, ph, g):
        self.dve_out_T(v, ph, g)
        self.dve_keys(v, ph, g)


class L1Xattn(Layer):
    TURNS = ["t0", "t1", "t2", "t3"]
    BATCHES = KT // 4

    def __init__(self, k):
        super().__init__(k)
        keys = []
        for b in range(self.BATCHES):
            keys += [(f"k{t}", "45"[t % 2]) for t in range(4 * b, 4 * b + 4)]
            keys += [(f"ssq{b}", "k_squares"), (f"kvar{b}", "k_var"), (f"krs{b}", "k_rstd"), (f"kn{b}", "k_normed")]
            keys += [(f"kT{b}{c}", str(c)) for c in range(DC)]
            keys += [(f"kst{t}", "k_row") for t in range(4 * b, 4 * b + 4)]
        self.y = self.p = Phase(k, [("load_pack", "load_pack0"), ("f_ssq", "ctx_squares"), ("f_var", "k_var"), ("f_rs", "k_rstd")]
                                + keys + LN_EVENTS + [("wk", "wk_scaled"), ("q", "5"), ("q_var", "k_var"), ("q_rs", "k_rstd"),
                                ("qn", "k_normed"), ("qT", "4"), ("s", "0"), ("shift", "shift"),
                                ("t0", "4"), ("t1", "5"), ("t2", "4"), ("t3", "5"), ("y", "7")])
        pack_ = k.area("pack0")
        self.wq, self.wk = (pack_[:, C_L1X[n]].rearrange("p (o n) -> p o n", o=DC) for n in ("wq", "wk"))
        self.bq, self.bk, self.fn_row, self.fn, self.qnw, self.knw = (pack_[:, C_L1X[n]] for n in ("bq", "bk", "fn_row", "fn", "qn", "kn"))
        self.keysT = k.area("work", 0, 8192).rearrange("p (o s) -> p o s", o=DC)
        self.q, self.qT = k.area("work", 8192, 8704), k.area("work", 8704, 9216)
        self.junk = k.area("work", 9216, 9728)
        stage = k.area("weights", 9216)
        self.stage = [stage[:, j * 2048:(j + 1) * 2048] for j in range(2)]
        self.probs, self.probsT = self.stage[0], heads(self.stage[1], KT)
        s = k.small
        self.f_ssq, self.rf, self.k_ssq, self.rk = (s[:, 16 * j:16 * j + 16] for j in range(4))
        self.q_ssq, self.rq, self.m, self.sum, self.inv = (s[:, 64 + j:65 + j] for j in range(5))
        self.qk = s[:, 72:76]
        self.scale = float(D) ** -0.5

    def sp(self, sp):
        k = self.k
        if "L0x" in k.layers:
            sp.wait_ge(*k.layers["L0x"].y.drained("y"))
        sp.dma_start(k.area("pack0", 0, C_L1X["all"]), k.dram["l1x"]).then_inc(self.p.mark("load_pack"), 16)
        if "L0x" not in k.layers:
            load_context(sp, k)

    def pool(self, pool):
        k, p = self.k, self.p

        def power(var, out, dst, src):
            pool.wait_ge(*p.done(var))
            pool.tensor_tensor(dst, src, k.minus_half[:, 0:dst.shape[1]], ALU.pow).then_inc(p.mark(out), 1)

        power("f_var", "f_rs", self.rf, self.f_ssq)
        for b in range(self.BATCHES):
            power(f"kvar{b}", f"krs{b}", self.rk[:, 4 * b:4 * b + 4], self.k_ssq[:, 4 * b:4 * b + 4])
        self.ln_pool(pool, p)
        power("q_var", "q_rs", self.rq, self.q_ssq)

    def pe(self, pe):
        k, p = self.k, self.p
        pe.wait_ge(*p.done("wk"))
        pe.wait_ge(*context_loaded(k))
        for b in range(self.BATCHES + 1):
            if b < self.BATCHES:
                for t in range(4 * b, 4 * b + 4):
                    pe.wait_ge(*p.room(f"k{t}"))
                    self.project(pe, k.ps(4 + t % 2), self.wk, D, src=k.ctxT[:, :, t * P:(t + 1) * P]).then_inc(p.fill(f"k{t}"), 1)
            if b >= 1:
                pe.wait_ge(*p.done(f"kn{b - 1}"))
                rows_ = self.stage[(b - 1) % 2].rearrange("p (t n) -> p t n", t=4)
                for c in range(DC):
                    pe.wait_ge(*p.room(f"kT{b - 1}{c}"))
                    for t in range(4):
                        last = pe.transpose(k.ps(c)[:, t * P:(t + 1) * P], rows_[:, t, c * P:(c + 1) * P], k.ident)
                    last.then_inc(p.fill(f"kT{b - 1}{c}"), 1)
        self.ln_pe(pe, p)
        pe.wait_ge(*p.drained("ln"))
        pe.wait_ge(*p.room("q"))
        self.project(pe, k.ps(5), self.wq, D).then_inc(p.fill("q"), 1)
        pe.wait_ge(*p.done("qn"))
        pe.wait_ge(*p.room("qT"))
        self.turn(pe, k.ps(4), self.q, DC).then_inc(p.fill("qT"), 1)
        pe.wait_ge(*p.drained("qT"))
        for c in range(DC):
            pe.wait_ge(*p.drained(f"kT{self.BATCHES - 1}{c}"))
        qT = heads(self.qT, DC)
        for c in range(4):
            last = self.project(pe, k.ps(c), self.keysT[:, :, c * 512:(c + 1) * 512], 512, src=qT)
        last.then_inc(p.fill("s"), 1)
        pe.wait_ge(*p.drained("s"))
        self.softmax_turn_pe(pe, p, self.probs, self.TURNS)
        pe.wait_ge(*p.room("y"))
        for t in range(KT):
            if t % 4 == 0:
                pe.wait_ge(*p.drained(self.TURNS[t // 4]))
            last = pe.matmul(k.ps(7), self.probsT[:, t, :], k.ctxN[:, t, :], start=t == 0, stop=t == KT - 1)
        last.then_inc(p.fill("y"), 1)

    def act(self, act):
        k, p = self.k, self.p
        act.wait_ge(*context_rows_loaded(k))
        if "L0f" in k.layers:
            act.wait_ge(*k.layers["L0f"].y.drained("y"))
        for t in range(KT):
            ins = act.activation(self.junk, k.ctxN[:, t, :], ACT.Square, accum_out=self.f_ssq[:, t:t + 1])
            if t < KT - 1:
                k.act_link(ins)
        ins.then_inc(p.mark("f_ssq"), 1)
        act.wait_ge(*p.done("f_ssq"))
        for b in range(self.BATCHES + 1):
            if b < self.BATCHES:
                for t in range(4 * b, 4 * b + 4):
                    act.wait_ge(*p.done(f"kst{t}"))
                    row = self.stage[b % 2][:, (t % 4) * 512:(t % 4 + 1) * 512]
                    ins = act.activation(self.junk, row, ACT.Square, accum_out=self.k_ssq[:, t:t + 1])
                    if t % 4 < 3:
                        k.act_link(ins)
                ins.then_inc(p.mark(f"ssq{b}"), 1)
                act.wait_ge(*p.done(f"ssq{b}"))
            if b >= 1:
                self.keys_out(act.activation, act, b - 1, (1, 3), ACT.Copy)
        self.ln_act(act, p)
        act.wait_ge(*p.done("shift"))
        act.activation(self.probs, k.wide[:, :], ACT.Exp, bias=self.m, scale=self.scale, accum_out=self.sum).then_inc(p.drain("s"), 1)

    def keys_out(self, copy, eng, b, chunks, *func):
        for c in chunks:
            eng.wait_ge(*self.p.filled(f"kT{b}{c}"))
            copy(self.keysT[:, c, b * 512:(b + 1) * 512], self.k.ps(c), *func).then_inc(self.p.drain(f"kT{b}{c}"), 1)

    def dve(self, v):
        k, p = self.k, self.p
        v.wait_ge(*p.loaded("load_pack"))
        for o in range(DC):
            last = v.tensor_scalar(self.wk[:, o, :], self.wk[:, o, :], self.fn[:, o:o + 1], None, ALU.mult)
        last.then_inc(p.mark("wk"), 1)
        k.link(v.tensor_tensor(self.qk, self.qnw, self.knw, ALU.mult))
        v.wait_ge(*p.done("f_ssq"))
        v.tensor_scalar(self.f_ssq, self.f_ssq, 1.0 / D, 1e-6, ALU.mult, ALU.add).then_inc(p.mark("f_var"), 1)
        v.wait_ge(*p.done("f_rs"))
        for b in range(self.BATCHES + 1):
            if b < self.BATCHES:
                for t in range(4 * b, 4 * b + 4):
                    v.wait_ge(*p.filled(f"k{t}"))
                    row = self.stage[b % 2][:, (t % 4) * 512:(t % 4 + 1) * 512]
                    v.scalar_tensor_tensor(out=row, in0=k.ps(4 + t % 2), scalar=self.rf[:, t:t + 1], in1=self.bk,
                                           op0=ALU.mult, op1=ALU.add).then_inc(p.drain(f"k{t}"), 1)
                    v.wait_ge(*p.drained(f"k{t}"))
                    v.engine_nop().then_inc(p.mark(f"kst{t}"), 1)
                v.wait_ge(*p.done(f"ssq{b}"))
                four = slice(4 * b, 4 * b + 4)
                v.tensor_scalar(self.k_ssq[:, four], self.k_ssq[:, four], 1.0 / D, 1e-6, ALU.mult, ALU.add).then_inc(p.mark(f"kvar{b}"), 1)
                v.wait_ge(*p.done(f"krs{b}"))
                v.tensor_tensor(heads(self.stage[b % 2], 4), heads(self.stage[b % 2], 4), per_head(self.rk[:, four], 512),
                                ALU.mult).then_inc(p.mark(f"kn{b}"), 1)
            if b >= 1:
                self.keys_out(v.tensor_copy, v, b - 1, (0, 2))
        self.ln_dve(v, p)
        v.wait_ge(*p.filled("q"))
        v.tensor_tensor(self.q, k.ps(5), self.bq, ALU.add).then_inc(p.drain("q"), 1)
        v.wait_ge(*p.drained("q"))
        k.link(v.tensor_tensor_reduce(out=self.junk, in0=self.q, in1=self.q, scale=1.0, scalar=0.0,
                                      op0=ALU.mult, op1=ALU.add, accum_out=self.q_ssq))
        v.tensor_scalar(self.q_ssq, self.q_ssq, 1.0 / D, 1e-6, ALU.mult, ALU.add).then_inc(p.mark("q_var"), 1)
        v.wait_ge(*p.done("q_rs"))
        v.tensor_scalar(self.q, self.q, self.rq, None, ALU.mult).then_inc(p.mark("qn"), 1)
        v.wait_ge(*p.filled("qT"))
        v.tensor_tensor(heads(self.qT, DC), heads(k.ps(4), DC), per_head(self.qk, P), ALU.mult).then_inc(p.drain("qT"), 1)
        v.wait_ge(*p.filled("s"))
        k.link(v.reduce_max(self.m, k.wide[:, :], AX_X))
        v.tensor_scalar(self.m, self.m, -self.scale, None, ALU.mult).then_inc(p.mark("shift"), 1)
        for j, name in enumerate(self.TURNS):
            v.wait_ge(*p.filled(name))
            v.tensor_tensor(self.probsT[:, 4 * j:4 * j + 4, :], heads(k.ps(4 + j % 2), 4), per_head(self.rf[:, 4 * j:4 * j + 4], P),
                            ALU.mult).then_inc(p.drain(name), 1)
        v.wait_ge(*p.drained("s"))
        k.link(v.reciprocal(self.inv, self.sum))
        v.wait_ge(*p.filled("y"))
        k.link(v.scalar_tensor_tensor(out=self.q, in0=k.ps(7), scalar=self.inv, in1=self.fn_row, op0=ALU.mult, op1=ALU.mult))
        v.tensor_tensor(k.x, k.x, self.q, ALU.add).then_inc(p.drain("y"), 1)
        v.wait_ge(*p.drained("y"))


def load_context(sp, k, rows_too=True):
    k.context = Phase(k, [("load_ctxT", "load_ctxT"), ("load_ctx", "load_ctx")])
    sp.dma_start(k.area("ctxT"), k.dram["ctxT"]).then_inc(k.context.mark("load_ctxT"), 16)
    if rows_too:
        sp.dma_start(k.area("ctx"), k.dram["ctx"]).then_inc(k.context.mark("load_ctx"), 16)


def context_loaded(k):
    return k.sem("load_ctxT"), 16


def context_rows_loaded(k):
    return k.sem("load_ctx"), 16


XT, HG = 8, 16
CHANNELS = XT + 2
GROUP_D = XT * P
PAD = 3
C_SCAN = columns(("xbc", DC * CHANNELS * P), ("gate", DC * GROUP_D), ("out", XT * D))
C_SCAN_S = columns(("dtw", DC * P), ("conv", GROUPS * CHANNELS * 5), ("table", GROUPS * 56), ("dtb", P), ("minus_a", 1), ("mask", P))


class Scan(Layer):
    PROJECT = [("load_xbc", "load_xbc"), ("bc", "0"), ("x0", "1"), ("x1", "2"), ("load_gate", "load_gate"), ("g0", "3"), ("g1", "4"),
               ("tg0", "gate_tanh"), ("tg1", "gate_tanh"), ("conv", "conv"), ("th", "conv_tanh"), ("sx", "channels")]
    MIX = [("load_cs", "load_cs"), ("cs_g", "group_cs"), ("rel", "relative_cs"), ("diff", "decay_diff"), ("decay", "decay"), ("xs0", "5"), ("xs1", "6"), ("s", "4"),
           ("xdt", "xdt"), ("mix", "mix"), ("y0", "5"), ("y1", "6"), ("yg", "gated"), ("ssq", "gated_squares"),
           ("yvar", "gated_var"), ("yrs", "gated_rstd"), ("yn", "normed"), ("yT0", "5"), ("yT1", "6"),
           ("load_out", "load_out"), ("part", "scan_part")]

    def __init__(self, k):
        super().__init__(k)
        self.first = self.p = Phase(k, [("load_small", "load_pack1"), ("pad", "conv_pad")] + LN_EVENTS + [("dt", "5"), ("later", "later_mask"), ("absdt", "abs_dt"), ("expdt", "exp_dt"),
                                    ("lndt", "ln_dt"), ("dtn", "dt_ready"), ("dtT", "4"), ("csT", "csT_ready"), ("store_cs", "store_cs"), ("cs", "4")] + self.PROJECT)
        self.body = Phase(k, self.MIX + self.PROJECT, GROUPS - 1)
        self.last = Phase(k, self.MIX + [("y", "7")])
        self.y = self.last
        w = k.area("weights")
        self.wx = w[:, C_SCAN["xbc"]].rearrange("p (o n) -> p o n", o=DC)
        self.wg = w[:, C_SCAN["gate"]].rearrange("p (o n) -> p o n", o=DC)
        self.wout = w[:, C_SCAN["out"]].rearrange("p (t n) -> p t n", t=XT)
        small = k.area("pack1")
        self.dtw, self.convw, self.table, self.dtb, self.minus_a, self.mask = (
            small[:, C_SCAN_S[n]] for n in ("dtw", "conv", "table", "dtb", "minus_a", "mask"))
        self.dtw = self.dtw.rearrange("p (o n) -> p o n", o=DC)
        self.tab = self.table.rearrange("p (g n) -> p g n", g=GROUPS)
        c = k.area("ctx")
        self.decay, self.mixer = c[:, 0:2048], c[:, 2048:4096]
        self.xc = c[:, 4096:4096 + CHANNELS * (P + PAD)].rearrange("p (t n) -> p t n", t=CHANNELS)
        self.conv = c[:, 5440:5440 + CHANNELS * P].rearrange("p (t n) -> p t n", t=CHANNELS)
        self.tanh = c[:, 6720:6720 + CHANNELS * P].rearrange("p (t n) -> p t n", t=CHANNELS)
        a = k.area("work")
        self.sx = a[:, 0:1280].rearrange("p (t n) -> p t n", t=CHANNELS)
        self.xdt, self.xd, self.tg, self.gate, self.yv, self.yT = (a[:, 1280 + 1024 * j:1280 + 1024 * (j + 1)] for j in range(6))
        rest = a[:, 7424:9728]
        self.masked, self.dtv, self.dta, self.dte, self.dt, self.da, self.csT, self.ones = (rest[:, P * j:P * (j + 1)] for j in range(8))
        self.table_g = rest[:, 1024:1024 + 56]
        self.normw, self.cs_g, self.dt_g, self.d_g = self.table_g[:, 0:8], self.table_g[:, 8:24], self.table_g[:, 24:40], self.table_g[:, 40:56]
        self.conv_g = rest[:, 1088:1088 + 50]
        self.ssq, self.rs = k.small[:, 0:1], k.small[:, 1:2]
        self.decay_cs = k.small[:, 16:32]
        self.later = c[:, 8000:8000 + P]
        self.squares = self.mixer[:, 0:GROUP_D]

    def load(self, sp, part, g):
        k = self.k
        src = k.dram["l1a"]
        row = src[g] if isinstance(g, int) else src[bass.ds(g, 1), :, :].rearrange("a p n -> p (a n)")
        return sp.dma_start(k.area("weights")[:, C_SCAN[part]], row[:, C_SCAN[part]])

    def load_cs(self, sp, g):
        rows_ = self.k.dram["cs"]
        row = rows_[g] if isinstance(g, int) else rows_[bass.ds(g, 1), :].rearrange("a n -> (a n)")
        return sp.dma_start(self.decay, row.partition_broadcast(P))

    def sp(self, sp):
        k, b = self.k, self.body
        for name, event, kind in (("L0f", "y", "drained"), ("L0a", "y", "drained")):
            if name in k.layers:
                sp.wait_ge(*k.layers[name].y.drained("y"))
        sp.dma_start(k.area("pack1", 0, C_SCAN_S["all"]), k.dram["l1a_small"]).then_inc(self.first.mark("load_small"), 16)
        self.load(sp, "xbc", 0).then_inc(self.first.mark("load_xbc"), 16)
        self.load(sp, "gate", 0).then_inc(self.first.mark("load_gate"), 16)
        if "L1x" in k.layers:
            sp.wait_ge(*k.layers["L1x"].y.filled("y"))
        self.load(sp, "out", 0).then_inc(b.mark("load_out"), 16)
        sp.wait_ge(*self.first.done("csT"))
        sp.dma_start(k.dram["cs"].rearrange("g (h l) -> (g h) l", h=HG), self.csT).then_inc(self.first.mark("store_cs"), 16)
        sp.wait_ge(*self.first.loaded("store_cs"))
        self.load_cs(sp, 0).then_inc(b.mark("load_cs"), 16)
        sp.wait_ge(*b.before("2", 0, "filled_"))
        self.load(sp, "xbc", 1).then_inc(b.mark("load_xbc"), 16)
        sp.wait_ge(*b.before("4", 0, "filled_"))
        self.load(sp, "gate", 1).then_inc(b.mark("load_gate"), 16)

        def iteration(g, more):
            if more:
                sp.wait_ge(*b.filled("x1", g))
                self.load(sp, "xbc", g + 2).then_inc(b.mark("load_xbc"), 16)
            sp.wait_ge(*b.done("mix", g))
            self.load_cs(sp, g + 1).then_inc(b.mark("load_cs"), 16)
            if more:
                sp.wait_ge(*b.filled("g1", g))
                self.load(sp, "gate", g + 2).then_inc(b.mark("load_gate"), 16)
            sp.wait_ge(*b.done("part", g))
            self.load(sp, "out", g + 1).then_inc(b.mark("load_out"), 16)

        with sp.Fori(0, GROUPS - 2) as g:
            iteration(g, True)
        iteration(GROUPS - 2, False)

    def pool(self, pool):
        k = self.k
        self.ln_pool(pool, self.first)

        def rstd(ph, g=0):
            pool.wait_ge(*ph.done("yvar", g))
            pool.tensor_tensor(self.rs, self.ssq, k.minus_half[:, 0:1], ALU.pow).then_inc(ph.mark("yrs"), 1)

        pool.wait_ge(*self.first.drained("cs"))
        pool.wait_ge(*self.first.done("later"))
        self.pool_diff(pool, self.body, 0, 0)
        with pool.Fori(0, GROUPS - 1) as g:
            rstd(self.body, g)
            self.pool_diff(pool, self.body, g + 1, g + 1)
        rstd(self.last)

    def pool_diff(self, pool, ph, g, group):
        pool.wait_ge(*ph.loaded("load_cs", g))
        src = self.table[:, 8:24] if isinstance(group, int) else self.table[:, bass.ds(group * 56 + 8, 16)]
        pool.tensor_copy(self.decay_cs, src).then_inc(ph.mark("cs_g"), 1)
        pool.wait_ge(*ph.done("cs_g", g))
        decay = heads(self.decay, HG)
        pool.tensor_tensor(decay, decay, per_head(self.decay_cs, P), ALU.subtract).then_inc(ph.mark("rel"), 1)
        pool.wait_ge(*ph.done("rel", g))
        pool.tensor_tensor(decay, decay, every_head(self.later, HG), ALU.add).then_inc(ph.mark("diff"), 1)

    def pe_channels(self, pe, ph, g=0):
        k = self.k
        pe.wait_ge(*ph.loaded("load_xbc", g))
        for name, tiles_ in (("bc", range(XT, XT + 2)), ("x0", range(0, 4)), ("x1", range(4, 8))):
            pe.wait_ge(*ph.room(name, g))
            out = k.ps(int(ph.at[name][0]))
            for j, t in enumerate(tiles_):
                for o in range(DC):
                    last = pe.matmul(out[:, j * P:(j + 1) * P], self.wx[:, o, t * P:(t + 1) * P], k.xnT[:, o, :], start=o == 0, stop=o == DC - 1)
            last.then_inc(ph.fill(name), 1)

    def pe_gate(self, pe, ph, g=0):
        k = self.k
        pe.wait_ge(*ph.loaded("load_gate", g))
        for j, name in enumerate(("g0", "g1")):
            pe.wait_ge(*ph.room(name, g))
            self.project(pe, k.ps(int(ph.at[name][0])), self.wg[:, :, j * 512:(j + 1) * 512], 512).then_inc(ph.fill(name), 1)

    def pe_rows(self, pe, ph, g=0):
        k = self.k
        pe.wait_ge(*ph.before("channels", g))
        for j, name in enumerate(("xs0", "xs1")):
            pe.wait_ge(*ph.room(name, g))
            for t in range(4):
                last = pe.transpose(k.ps(5 + j)[:, t * P:(t + 1) * P], self.sx[:, 4 * j + t, :], k.ident)
            last.then_inc(ph.fill(name), 1)
        pe.wait_ge(*ph.room("s", g))
        pe.matmul(k.ps(4)[:, 0:P], self.sx[:, XT, :], self.sx[:, XT + 1, :], start=True, stop=True).then_inc(ph.fill("s"), 1)

    def pe_mix(self, pe, ph, g=0):
        k = self.k
        pe.wait_ge(*ph.done("mix", g))
        for j, name in enumerate(("y0", "y1")):
            pe.wait_ge(*ph.room(name, g))
            for h in range(8 * j, 8 * j + 8):
                last = pe.matmul(k.ps(5 + j)[:, (h % 8) * 64:(h % 8 + 1) * 64], self.mixer[:, h * P:(h + 1) * P],
                                 self.xdt[:, h * 64:(h + 1) * 64], start=True, stop=True)
            last.then_inc(ph.fill(name), 1)

    def pe_out(self, pe, ph, g=0, stop=False):
        k = self.k
        pe.wait_ge(*ph.done("yn", g))
        for j, name in enumerate(("yT0", "yT1")):
            pe.wait_ge(*ph.room(name, g))
            self.turn(pe, k.ps(5 + j), self.yv[:, 512 * j:512 * j + 512], 4).then_inc(ph.fill(name), 1)
        pe.wait_ge(*ph.loaded("load_out", g))
        for t in range(XT):
            if t % 4 == 0:
                pe.wait_ge(*ph.drained(f"yT{t // 4}", g))
            last = pe.matmul(k.ps(7), self.yT[:, t * P:(t + 1) * P], self.wout[:, t, :], start=False, stop=stop and t == XT - 1, skip_group_check=True)
        return last

    def pe(self, pe):
        k, f = self.k, self.first
        self.ln_pe(pe, f)
        pe.wait_ge(*self.last.room("y"))
        pe.matmul(k.ps(7), k.zeros, k.xn, start=True, stop=False, skip_group_check=True)
        pe.wait_ge(*f.drained("ln"))
        pe.wait_ge(*f.loaded("load_small"))
        pe.wait_ge(*f.room("dt"))
        self.project(pe, k.ps(5), self.dtw, P).then_inc(f.fill("dt"), 1)
        self.pe_channels(pe, f)
        pe.wait_ge(*f.done("dtn"))
        self.turn(pe, k.ps(4), self.dt, 1).then_inc(f.fill("dtT"), 1)
        pe.wait_ge(*f.done("csT"))
        self.turn(pe, k.ps(4), self.csT, 1).then_inc(f.fill("cs"), 1)
        self.pe_gate(pe, f)
        with pe.Fori(0, GROUPS - 1) as g:
            self.pe_rows(pe, self.body, g)
            self.pe_channels(pe, self.body, g)
            self.pe_mix(pe, self.body, g)
            self.pe_gate(pe, self.body, g)
            self.pe_out(pe, self.body, g).then_inc(self.body.mark("part"), 1)
        self.pe_rows(pe, self.last)
        self.pe_mix(pe, self.last)
        self.pe_out(pe, self.last, stop=True).then_inc(self.last.fill("y"), 1)

    def act_channels(self, act, ph, g=0):
        k = self.k
        if ph is not self.first:
            act.wait_ge(*ph.before("conv", g))
        for name, a, b in (("bc", XT, XT + 2), ("x0", 0, 4), ("x1", 4, 8)):
            act.wait_ge(*ph.filled(name, g))
            src = k.ps(int(ph.at[name][0]))[:, 0:(b - a) * P]
            act.activation(self.xc[:, a:b, PAD:PAD + P], heads(src, b - a), ACT.Copy).then_inc(ph.drain(name), 1)

    def act_tanh(self, act, ph, g=0):
        act.wait_ge(*ph.done("conv", g))
        act.activation(self.tanh, self.conv, ACT.Tanh, scale=0.5).then_inc(ph.mark("th"), 1)

    def act_gate(self, act, ph, g=0):
        for j, name in enumerate(("g0", "g1")):
            act.wait_ge(*ph.filled(name, g))
            if ph is not self.first:
                act.wait_ge(*ph.before(str(3 + j), g, "drained_"))
            act.activation(self.tg[:, 512 * j:512 * j + 512], self.k.ps(3 + j), ACT.Tanh, scale=0.5).then_inc(ph.mark(f"tg{j}"), 1)

    def act_decay(self, act, ph, g=0):
        act.wait_ge(*ph.done("diff", g))
        act.activation(self.decay, self.decay, ACT.Exp).then_inc(ph.mark("decay"), 1)

    def act_square(self, act, ph, g=0):
        act.wait_ge(*ph.done("yg", g))
        act.activation(self.squares, self.yv, ACT.Square, accum_out=self.ssq).then_inc(ph.mark("ssq"), 1)

    def act(self, act):
        f = self.first
        self.ln_act(act, f)
        act.wait_ge(*f.done("pad"))
        self.act_channels(act, f)
        act.wait_ge(*f.done("absdt"))
        act.activation(self.dte, self.dta, ACT.Exp, scale=-1.0).then_inc(f.mark("expdt"), 1)
        act.wait_ge(*f.done("expdt"))
        act.activation(self.dte, self.dte, ACT.Ln, bias=1.0).then_inc(f.mark("lndt"), 1)
        self.act_tanh(act, f)
        self.act_gate(act, f)
        self.act_decay(act, self.body, 0)
        with act.Fori(0, GROUPS - 1) as g:
            self.act_channels(act, self.body, g)
            self.act_square(act, self.body, g)
            self.act_tanh(act, self.body, g)
            self.act_gate(act, self.body, g)
            self.act_decay(act, self.body, g + 1)
        self.act_square(act, self.last)

    def dve_taps(self, v, ph, name, g=0):
        k = self.k
        tiles_ = {"bc": range(XT, XT + 2), "x0": range(0, 4), "x1": range(4, 8)}[name]
        w = lambda t, j: self.conv_g[:, 5 * t + j:5 * t + j + 1]
        v.wait_ge(*ph.drained(name, g))
        for j in range(4):
            for t in tiles_:
                src, out = self.xc[:, t, PAD - j:PAD - j + P], self.conv[:, t, :]
                if j == 0:
                    last = v.tensor_scalar(out, src, w(t, 3), w(t, 4), ALU.mult, ALU.add)
                else:
                    last = v.scalar_tensor_tensor(out=out, in0=src, scalar=w(t, 3 - j), in1=out, op0=ALU.mult, op1=ALU.add)
            if j < 3:
                k.link(last)
        return last

    def dve_conv_first(self, v, ph, g=0, group=0):
        n = CHANNELS * 5
        self.k.link(v.tensor_copy(self.conv_g, self.convw[:, bass.ds(group * n, n)] if ph is not self.first else self.convw[:, 0:n]))
        self.dve_taps(v, ph, "bc", g)
        self.dve_taps(v, ph, "x0", g)

    def dve_conv_last(self, v, ph, g=0):
        self.dve_taps(v, ph, "x1", g).then_inc(ph.mark("conv"), 1)

    def dve_silu(self, v, ph, g=0):
        v.wait_ge(*ph.done("th", g))
        v.wait_ge(*ph.done("conv", g))
        flat = lambda ap: ap.rearrange("p t n -> p (t n)")
        v.scalar_tensor_tensor(out=flat(self.sx), in0=flat(self.tanh), scalar=1.0, in1=flat(self.conv), op0=ALU.add,
                               op1=ALU.mult).then_inc(ph.mark("sx"), 1)

    def dve_gate(self, v, ph, g=0):
        for j, name in enumerate(("g0", "g1")):
            v.wait_ge(*ph.done(f"tg{j}", g))
            s = slice(512 * j, 512 * j + 512)
            v.scalar_tensor_tensor(out=self.gate[:, s], in0=self.tg[:, s], scalar=1.0, in1=self.k.ps(3 + j), op0=ALU.add,
                                   op1=ALU.mult).then_inc(ph.drain(name), 1)

    def dve_table(self, v, ph, g=0, group=0):
        n = 56
        src = self.table[:, (GROUPS - 1) * n:] if isinstance(group, int) else self.table[:, bass.ds(group * n, n)]
        v.wait_ge(*ph.before("4", g, "drained_"))
        self.k.link(v.tensor_copy(self.table_g, src))

    def dve_rows(self, v, ph, g=0):
        k = self.k
        for j, name in enumerate(("xs0", "xs1")):
            v.wait_ge(*ph.filled(name, g))
            s = slice(512 * j, 512 * j + 512)
            h = slice(8 * j, 8 * j + 8)
            v.tensor_tensor(heads(self.xdt[:, s], 8), heads(k.ps(5 + j), 8), per_head(self.dt_g[:, h], 64), ALU.mult)
            v.tensor_tensor(heads(self.xd[:, s], 8), heads(k.ps(5 + j), 8), per_head(self.d_g[:, h], 64), ALU.mult).then_inc(ph.drain(name), 1)
        v.wait_ge(*ph.filled("s", g))
        v.scalar_tensor_tensor(out=self.masked, in0=k.ps(4)[:, 0:P], scalar=0.25, in1=self.mask, op0=ALU.mult, op1=ALU.mult).then_inc(ph.drain("s"), 1)
        v.wait_ge(*ph.drained("s", g))
        v.wait_ge(*ph.done("decay", g))
        v.tensor_tensor(heads(self.mixer, HG), heads(self.decay, HG), every_head(self.masked, HG), ALU.mult).then_inc(ph.mark("mix"), 1)

    def dve_gated(self, v, ph, g=0):
        k = self.k
        v.wait_ge(*ph.before("channels", g))
        for j, name in enumerate(("y0", "y1")):
            v.wait_ge(*ph.filled(name, g))
            s = slice(512 * j, 512 * j + 512)
            last = v.tensor_tensor(self.yv[:, s], k.ps(5 + j), self.xd[:, s], ALU.add)
            last.then_inc(ph.drain(name), 1)
        v.wait_ge(*ph.drained("y1", g))
        v.wait_ge(*ph.drained("y0", g))
        v.tensor_tensor(self.yv, self.yv, self.gate, ALU.mult).then_inc(ph.mark("yg"), 1)

    def dve_norm(self, v, ph, g=0):
        v.wait_ge(*ph.done("ssq", g))
        v.tensor_scalar(self.ssq, self.ssq, 0.25 / GROUP_D, 1e-5, ALU.mult, ALU.add).then_inc(ph.mark("yvar"), 1)
        v.wait_ge(*ph.done("yrs", g))
        v.tensor_scalar(self.yv, self.yv, self.rs, 0.5, ALU.mult, ALU.mult).then_inc(ph.mark("yn"), 1)

    def dve_out_T(self, v, ph, g=0):
        for j, name in enumerate(("yT0", "yT1")):
            v.wait_ge(*ph.filled(name, g))
            v.tensor_tensor(heads(self.yT[:, 512 * j:512 * j + 512], 4), heads(self.k.ps(5 + j), 4), per_head(self.normw[:, 4 * j:4 * j + 4], P),
                            ALU.mult).then_inc(ph.drain(name), 1)

    def dve(self, v):
        k, f = self.k, self.first
        self.ln_dve(v, f)
        v.memset(self.xc[:, :, 0:PAD], 0.0).then_inc(f.mark("pad"), 1)
        v.memset(self.ones, 1.0)
        v.wait_ge(*f.loaded("load_small"))
        v.tensor_scalar(self.later, self.mask, -1.0, -NEG, ALU.add, ALU.mult).then_inc(f.mark("later"), 1)
        v.wait_ge(*f.filled("dt"))
        v.tensor_tensor(self.dtv, k.ps(5)[:, 0:P], self.dtb, ALU.add).then_inc(f.drain("dt"), 1)
        v.wait_ge(*f.drained("dt"))
        k.link(v.tensor_scalar(self.dta, self.dtv, -1.0, None, ALU.mult))
        v.tensor_tensor(self.dta, self.dta, self.dtv, ALU.max).then_inc(f.mark("absdt"), 1)
        k.link(v.tensor_scalar(self.dtv, self.dtv, 0.0, None, ALU.max))
        v.wait_ge(*f.done("lndt"))
        k.link(v.tensor_tensor(self.dt, self.dtv, self.dte, ALU.add))
        v.tensor_scalar(self.dt, self.dt, 0.001, 100.0, ALU.max, ALU.min).then_inc(f.mark("dtn"), 1)
        v.wait_ge(*f.done("dtn"))
        half = lambda part: self.tab[:, :, part]
        v.tensor_scalar(half(slice(24, 40)), self.dt.rearrange("p (g n) -> p g n", g=GROUPS), 0.5, None, ALU.mult)
        v.tensor_scalar(half(slice(40, 56)), half(slice(40, 56)), 0.5, None, ALU.mult)
        v.wait_ge(*f.filled("dtT"))
        v.tensor_scalar(self.da, k.ps(4)[:, 0:P], self.minus_a, None, ALU.mult).then_inc(f.drain("dtT"), 1)
        v.wait_ge(*f.drained("dtT"))
        v.tensor_tensor_scan(self.csT, self.ones, self.da, 0.0, ALU.mult, ALU.add).then_inc(f.mark("csT"), 1)
        v.wait_ge(*f.filled("cs"))
        v.tensor_copy(half(slice(8, 24)), heads(k.ps(4)[:, 0:P], GROUPS)).then_inc(f.drain("cs"), 1)
        v.wait_ge(*f.drained("cs"))
        self.dve_conv_first(v, f)
        self.dve_conv_last(v, f)
        self.dve_silu(v, f)
        self.dve_gate(v, f)
        with v.Fori(0, GROUPS - 1) as g:
            k.chain.loop(g, 11)
            self.dve_table(v, self.body, g, g)
            self.dve_rows(v, self.body, g)
            self.dve_conv_first(v, self.body, g, g + 1)
            self.dve_gated(v, self.body, g)
            self.dve_conv_last(v, self.body, g)
            self.dve_norm(v, self.body, g)
            self.dve_silu(v, self.body, g)
            self.dve_out_T(v, self.body, g)
            self.dve_gate(v, self.body, g)
        k.chain.end(GROUPS - 1)
        self.dve_table(v, self.last)
        self.dve_rows(v, self.last)
        self.dve_gated(v, self.last)
        self.dve_norm(v, self.last)
        self.dve_out_T(v, self.last)
        v.wait_ge(*self.last.filled("y"))
        self.add_output(v, self.last)


class L1Ffn(Layer):
    def __init__(self, k):
        super().__init__(k)
        self.y = self.p = Phase(k, [("load_pack", "load_pack0")] + LN_EVENTS + [
            ("g", "6"), ("h", "5"), ("shift", "shift"), ("thr", "threshold_exp"), ("exp", "exp"), ("hw", "hidden"), ("hT", "4"), ("y", "7")])
        pack_ = k.area("pack0")
        self.w, self.a, self.wg = (pack_[:, C_L1F[n]].rearrange("p (o n) -> p o n", o=DC) for n in ("w", "a", "gate"))
        self.b, self.bias, self.bthr = (pack_[:, C_L1F[n]] for n in ("b", "bias", "bthr"))
        w = k.area("work")
        self.h, self.hT = w[:, 0:P], w[:, P:2 * P]
        s = k.small
        self.g, self.e, self.w8, self.t8 = s[:, 0:9], s[:, 16:24], s[:, 24:32], s[:, 32:40]
        self.m, self.sum, self.inv, self.te, self.th, self.ws = (s[:, 48 + j:49 + j] for j in range(6))

    def sp(self, sp):
        k = self.k
        if "L1x" in k.layers:
            sp.wait_ge(*k.layers["L1x"].y.drained("y"))
        sp.dma_start(k.area("pack0", 0, C_L1F["all"]), k.dram["l1f"]).then_inc(self.p.mark("load_pack"), 16)

    def pe(self, pe):
        k, p = self.k, self.p
        self.ln_pe(pe, p)
        pe.wait_ge(*p.drained("ln"))
        pe.wait_ge(*p.loaded("load_pack"))
        pe.wait_ge(*p.room("g"))
        self.project(pe, k.ps(6), self.wg, E8 + 1).then_inc(p.fill("g"), 1)
        pe.wait_ge(*p.room("h"))
        self.project(pe, k.ps(5), self.a, P).then_inc(p.fill("h"), 1)
        pe.wait_ge(*p.room("y"))
        self.project(pe, k.ps(7), self.w, D, stop=False)
        pe.wait_ge(*p.drained("h"))
        self.turn(pe, k.ps(4), self.h, 1).then_inc(p.fill("hT"), 1)
        pe.wait_ge(*p.drained("hT"))
        pe.matmul(k.ps(7), self.hT, self.b, start=False, stop=True).then_inc(p.fill("y"), 1)

    def act(self, act):
        k, p = self.k, self.p
        self.ln_act(act, p)
        act.wait_ge(*p.done("shift"))
        act.activation(self.te, self.g[:, 8:9], ACT.Exp, scale=-1.0)
        act.activation(self.e, self.e, ACT.Exp, accum_out=self.sum).then_inc(p.mark("exp"), 1)
        act.wait_ge(*p.filled("hT"))
        act.activation(self.hT, k.ps(4)[:, 0:P], ACT.Copy).then_inc(p.drain("hT"), 1)

    def dve(self, v):
        k, p = self.k, self.p
        self.ln_dve(v, p)
        v.wait_ge(*p.loaded("load_pack"))
        v.wait_ge(*p.filled("g"))
        v.tensor_copy(self.g, k.ps(6)[:, 0:9]).then_inc(p.drain("g"), 1)
        v.wait_ge(*p.drained("g"))
        v.tensor_scalar(self.g[:, 8:9], self.g[:, 8:9], self.bthr, None, ALU.add)
        k.link(v.reduce_max(self.m, self.g[:, 0:8], AX_X))
        v.tensor_scalar(self.e, self.g[:, 0:8], self.m, None, ALU.subtract).then_inc(p.mark("shift"), 1)
        v.wait_ge(*p.done("exp"))
        k.link(v.tensor_scalar(self.te, self.te, 1.0, None, ALU.add))
        k.link(v.reciprocal(self.th, self.te))
        k.link(v.reciprocal(self.inv, self.sum))
        k.link(v.tensor_scalar(self.th, self.th, 0.125, None, ALU.mult))
        k.link(v.tensor_scalar(self.w8, self.e, self.inv, self.th, ALU.mult, ALU.subtract))
        k.link(v.tensor_scalar(self.w8, self.w8, 0.0, None, ALU.max))
        k.link(v.reduce_sum(self.ws, self.w8, AX_X))
        k.link(v.tensor_scalar(self.m, self.ws, 0.0, None, ALU.is_equal))
        k.link(v.tensor_tensor(self.ws, self.ws, self.m, ALU.add))
        k.link(v.reciprocal(self.inv, self.ws))
        k.link(v.tensor_scalar(self.w8, self.w8, self.inv, 2.0, ALU.mult, ALU.mult))
        v.wait_ge(*p.filled("h"))
        v.tensor_tensor(heads(self.h, E8), heads(k.ps(5)[:, 0:P], E8), per_head(self.w8, 16), ALU.mult).then_inc(p.drain("h"), 1)
        k.link(v.tensor_tensor(k.x, k.x, self.bias, ALU.add))
        v.wait_ge(*p.filled("y"))
        self.add_output(v, p)


C_ROPE_K = columns(("cos", KT * HALF), ("sin", KT * HALF))


class CrossAttention(Layer):
    KV_ORDER = ["kv0", "kv1", "oT", "kv2", "kv3", "kT0", "out", "kv4", "kv5", "kT1", "kv6", "kv7", "kT2", "qT", "kT3"]
    KV_BANK = {"kv0": "5", "kv1": "4", "kv2": "5", "kv3": "4", "kT0": "5", "kv4": "4", "kv5": "5", "kT1": "4", "kv6": "5",
               "kv7": "4", "kT2": "5", "kT3": "4", "qT": "6", "oT": "6"}

    def __init__(self, k, source, rope):
        super().__init__(k)
        self.source, self.rope = source, rope
        q = [("load_q", "load_q"), ("q", "4")]
        if not rope:
            q += [("q_sq", "q_squares"), ("q_var", "k_var"), ("q_rs", "k_rstd")]
        kv = [("load_kv", "load_kv")]
        for name in self.KV_ORDER:
            if name in ("oT", "out"):
                continue
            kv.append((name, self.KV_BANK[name]))
            if name.startswith("kv"):
                kv += [("v" + name[2:], "v_ready")]
                if not rope:
                    kv += [("k_var" + name[2:], "k_var"), ("k_rs" + name[2:], "k_rstd")]
        attend = []
        for h in range(PER_GROUP):
            attend += [(f"s{h}", "0"), (f"shift{h}", "shift"), (f"exp{h}", "exp")]
            attend += [(f"t{h}{j}", "54"[j % 2]) for j in range(4)]
        attend += [("o", "6"), ("oT", "6"), ("load_wo", "load_wo")]
        self.first = self.p = Phase(k, [("load_mask", "load_mask"), ("load_tab", "load_rope")] + LN_EVENTS + q + kv)
        self.body = Phase(k, q + attend + [("part", "part_done")] + kv, GROUPS - 1)
        self.last = self.y = Phase(k, attend + [("y", "7")])
        w = k.area("weights", 0, 5120)
        self.wq, self.wkv = w[:, 0:2048].rearrange("p (o n) -> p o n", o=DC), w[:, 2048:3072].rearrange("p (o n) -> p o n", o=DC)
        self.wo = w[:, 3072:5120].rearrange("p (h n) -> p h n", h=PER_GROUP)
        c, a, b = k.area("ctx"), k.area("work"), k.area("pack0")
        self.probsT, self.mask, self.tab, self.keysT = c[:, 0:2048], c[:, 2048:4096], c[:, 4096:6144], c[:, 6144:8192]
        self.values, self.keys = a[:, 0:2048], a[:, 6144:8192]
        self.probs = [a[:, 2048:4096], a[:, 4096:6144]]
        self.qn, self.qT, self.tmp = a[:, 8192:8704], a[:, 8704:9216], a[:, 9216:9728]
        self.on, self.oT, self.tmpk = b[:, 4096:4608], b[:, 4608:5120], b[:, 5120:5376]
        self.qw, self.kw = self.tab[:, 0:1], self.tab[:, 1:2]
        s = k.small
        self.sum, self.inv, self.q_ssq, self.rq = (s[:, 4 * j:4 * j + 4] for j in range(4))
        self.tick = s[:, 110:111]
        self.m, self.k_ssq, self.rk = s[:, 16:20], s[:, 20:36], s[:, 36:52]
        self.scale = float(P) ** -0.5

    def load(self, sp, part, g):
        src = self.k.dram[self.source]
        row = src[g] if isinstance(g, int) else src[bass.ds(g, 1), :, :].rearrange("a p n -> p (a n)")
        a, b = {"q": (0, 2048), "kv": (2048, 3072), "wo": (3072, 5120)}[part]
        return sp.dma_start(self.k.area("weights", a, b), row[:, a:b])

    def sp(self, sp):
        k, f, b = self.k, self.first, self.body
        before = "L1a" if self.rope else "L2x"
        for name in (("L1x", "L1a", "L1f") if self.rope else ("L2x", "L2f")):
            if name in k.layers:
                sp.wait_ge(*k.layers[name].y.drained("y"))
        if "L0x" not in k.layers and (self.rope or "L2x" not in k.layers):
            load_context(sp, k, False)
        self.load(sp, "q", 0).then_inc(f.mark("load_q"), 16)
        self.load(sp, "kv", 0).then_inc(f.mark("load_kv"), 16)
        tab = self.tab if self.rope else self.tab[:, 0:2]
        sp.dma_start(tab, k.dram["rope_keys" if self.rope else "l3x_norm"]).then_inc(f.mark("load_tab"), 16)
        sp.dma_start(self.mask, k.dram["mask2" if self.rope else "mask3"]).then_inc(f.mark("load_mask"), 16)
        self.load(sp, "wo", 0).then_inc(b.mark("load_wo"), 16)
        with sp.Fori(0, GROUPS - 1) as g:
            sp.wait_ge(*b.filled("kv1", g - 1))
            self.load(sp, "q", g + 1).then_inc(b.mark("load_q"), 16)
            sp.wait_ge(*b.before("4", g, "filled_"))
            self.load(sp, "kv", g + 1).then_inc(b.mark("load_kv"), 16)
            sp.wait_ge(*b.done("part", g))
            self.load(sp, "wo", g + 1).then_inc(b.mark("load_wo"), 16)

    def pool(self, pool):
        k = self.k
        self.ln_pool(pool, self.first)
        if self.rope:
            return

        def power(ph, var, out, dst, src, g):
            pool.wait_ge(*ph.done(var, g))
            pool.tensor_tensor(dst, src, k.minus_half[:, 0:dst.shape[1]], ALU.pow).then_inc(ph.mark(out), 1)

        def norms(ph, g=0):
            power(ph, "q_var", "q_rs", self.rq, self.q_ssq, g)
            for f in range(8):
                s = slice(2 * f, 2 * f + 2)
                power(ph, f"k_var{f}", f"k_rs{f}", self.rk[:, s], self.k_ssq[:, s], g)

        norms(self.first)
        with pool.Fori(0, GROUPS - 1) as g:
            norms(self.body, g)

    def pe_q(self, pe, ph, g=0):
        pe.wait_ge(*ph.loaded("load_q", g))
        pe.wait_ge(*ph.room("q", g))
        self.project(pe, self.k.ps(4), self.wq, D).then_inc(ph.fill("q"), 1)

    def pe_scores(self, pe, ph, h, g=0):
        k = self.k
        pe.wait_ge(*ph.room(f"s{h}", g))
        for c in range(4):
            last = pe.matmul(k.ps(c), self.qT[:, h * P:(h + 1) * P], self.keysT[:, c * 512:(c + 1) * 512], start=True, stop=True)
        last.then_inc(ph.fill(f"s{h}"), 1)

    def pe_attend(self, pe, ph, h, g=0):
        k = self.k
        pe.wait_ge(*ph.done(f"exp{h}", g))
        for j in range(4):
            name = f"t{h}{j}"
            pe.wait_ge(*ph.room(name, g))
            self.turn(pe, k.ps(5 - j % 2), self.probs[h % 2][:, j * 512:(j + 1) * 512], 4).then_inc(ph.fill(name), 1)
        if h == 0:
            pe.wait_ge(*ph.room("o", g))
        for t in range(KT):
            if t % 4 == 0:
                pe.wait_ge(*ph.drained(f"t{h}{t // 4}", g))
            last = pe.matmul(k.ps(6)[:, h * P:(h + 1) * P], self.probsT[:, t * P:(t + 1) * P], self.values[:, t * P:(t + 1) * P],
                             start=t == 0, stop=t == KT - 1)
        if h == PER_GROUP - 1:
            last.then_inc(ph.fill("o"), 1)

    def pe_out(self, pe, ph, g=0, stop=False):
        pe.wait_ge(*ph.drained("oT", g))
        pe.wait_ge(*ph.loaded("load_wo", g))
        for h in range(PER_GROUP):
            last = pe.matmul(self.k.ps(7), self.oT[:, h * P:(h + 1) * P], self.wo[:, h, :], start=False,
                             stop=stop and h == PER_GROUP - 1, skip_group_check=True)
        return last

    def pe_heads_T(self, pe, ph, g=0):
        pe.wait_ge(*ph.drained("o", g))
        self.turn(pe, self.k.ps(6), self.on, PER_GROUP).then_inc(ph.fill("oT"), 1)

    def pe_kv(self, pe, ph, g=0):
        k = self.k
        pe.wait_ge(*ph.loaded("load_kv", g))
        for name in self.KV_ORDER:
            if name in ("oT", "out"):
                if ph is not self.first:
                    if name == "oT":
                        self.pe_heads_T(pe, ph, g)
                    else:
                        self.pe_out(pe, ph, g).then_inc(ph.mark("part"), 1)
                continue
            bank = k.ps(int(self.KV_BANK[name]))
            if name == "qT":
                pe.wait_ge(*ph.drained("q", g))
            elif name.startswith("kT"):
                for f in (2 * int(name[2]), 2 * int(name[2]) + 1):
                    pe.wait_ge(*ph.drained(f"kv{f}", g))
            pe.wait_ge(*ph.room(name, g))
            if name.startswith("kv"):
                for j in range(2):
                    t = 2 * int(name[2]) + j
                    last = self.project(pe, bank[:, 256 * j:256 * j + 256], self.wkv, 256, src=k.ctxT[:, :, t * P:(t + 1) * P])
            else:
                src = self.qn if name == "qT" else self.keys[:, 512 * int(name[2]):512 * int(name[2]) + 512]
                last = self.turn(pe, bank, src, 4)
            last.then_inc(ph.fill(name), 1)

    def pe_heads(self, pe, ph, g=0, middle=None):
        self.pe_scores(pe, ph, 0, g)
        if middle:
            middle()
        for h in range(PER_GROUP):
            if h + 1 < PER_GROUP:
                self.pe_scores(pe, ph, h + 1, g)
            self.pe_attend(pe, ph, h, g)

    def pe(self, pe):
        k, f = self.k, self.first
        self.ln_pe(pe, f)
        pe.wait_ge(*self.last.room("y"))
        pe.matmul(k.ps(7), k.zeros, k.xn, start=True, stop=False, skip_group_check=True)
        pe.wait_ge(*f.drained("ln"))
        pe.wait_ge(*context_loaded(k))
        self.pe_q(pe, f)
        self.pe_kv(pe, f)
        with pe.Fori(0, GROUPS - 1) as g:
            for b in "456":
                pe.wait_ge(*self.body.before(b, g, "drained_"))
            self.pe_heads(pe, self.body, g, lambda: self.pe_q(pe, self.body, g))
            self.pe_kv(pe, self.body, g)
        for b in "456":
            pe.wait_ge(*self.last.before(b, 0, "drained_"))
        self.pe_heads(pe, self.last)
        self.pe_heads_T(pe, self.last)
        self.pe_out(pe, self.last, stop=True).then_inc(self.last.fill("y"), 1)

    def act_exp(self, act, ph, h, g=0):
        act.wait_ge(*ph.done(f"shift{h}", g))
        pr = self.probs[h % 2]
        act.activation(pr, pr, ACT.Exp, bias=self.m[:, h:h + 1], accum_out=self.sum[:, h:h + 1]).then_inc(ph.mark(f"exp{h}"), 1)

    def act_turned(self, act, ph, h, g=0):
        for j in range(4):
            act.wait_ge(*ph.filled(f"t{h}{j}", g))
            act.activation(self.probsT[:, 512 * j:512 * j + 512], self.k.ps(5 - j % 2), ACT.Copy).then_inc(ph.drain(f"t{h}{j}"), 1)

    def act_q(self, act, ph, g=0):
        if not self.rope:
            act.wait_ge(*ph.filled("q", g))
            act.activation(self.tmp, self.k.ps(4), ACT.Square).then_inc(ph.mark("q_sq"), 1)

    def act_heads_T(self, act, ph, g=0):
        act.wait_ge(*ph.filled("oT", g))
        act.activation(self.oT, self.k.ps(6), ACT.Copy).then_inc(ph.drain("oT"), 1)

    def act_kv(self, act, ph, g=0):
        k = self.k
        for name in self.KV_ORDER:
            if name == "out" or (name == "oT" and ph is self.first):
                continue
            if name == "oT":
                self.act_heads_T(act, ph, g)
                continue
            bank = k.ps(int(self.KV_BANK[name]))
            act.wait_ge(*ph.filled(name, g))
            if name.startswith("kv"):
                f = int(name[2])
                src = bank.rearrange("p (t s n) -> p t s n", t=2, s=2)
                if not self.rope:
                    for j in range(2):
                        ins = act.activation(self.tmpk[:, j * P:(j + 1) * P], src[:, j, 0, :], ACT.Square,
                                             accum_out=self.k_ssq[:, 2 * f + j:2 * f + j + 1])
                    k.act_link(ins)
                act.activation(heads(self.values[:, 256 * f:256 * f + 256], 2), src[:, :, 1, :], ACT.Copy).then_inc(ph.mark(f"v{f}"), 1)
            elif name == "qT":
                act.activation(self.qT, bank, ACT.Copy, scale=self.scale if self.rope else self.qw).then_inc(ph.drain(name), 1)
            else:
                c = int(name[2])
                out = self.keysT[:, 512 * c:512 * c + 512]
                if self.rope:
                    act.activation(out, bank, ACT.Copy).then_inc(ph.drain(name), 1)
                else:
                    act.activation(out, bank, ACT.Copy, scale=self.kw).then_inc(ph.drain(name), 1)

    def act(self, act):
        k = self.k
        self.ln_act(act, self.first)
        act.wait_ge(*self.first.loaded("load_tab"))
        self.act_q(act, self.first)
        self.act_kv(act, self.first)
        with act.Fori(0, GROUPS - 1) as g:
            b = self.body
            k.act_chain.loop(g, 0 if self.rope else 8)
            self.act_exp(act, b, 0, g)
            self.act_q(act, b, g)
            for h in range(PER_GROUP):
                self.act_turned(act, b, h, g)
                if h + 1 < PER_GROUP:
                    self.act_exp(act, b, h + 1, g)
            self.act_kv(act, b, g)
        k.act_chain.end(GROUPS - 1)
        self.act_exp(act, self.last, 0)
        for h in range(PER_GROUP):
            self.act_turned(act, self.last, h)
            if h + 1 < PER_GROUP:
                self.act_exp(act, self.last, h + 1)
        self.act_heads_T(act, self.last)

    def rotate(self, v, src, out, tmp, cos, sin, n):
        k = self.k
        both = lambda ap: ap.rearrange("p h (s n) -> p h s n", s=2)
        v.scalar_tensor_tensor(out=both(tmp)[:, :, 0, :], in0=both(src)[:, :, 1, :], scalar=-1.0, in1=sin, op0=ALU.mult, op1=ALU.mult)
        v.tensor_tensor(both(tmp)[:, :, 1, :], both(src)[:, :, 0, :], sin, ALU.mult)
        v.tensor_tensor(both(out)[:, :, 0, :], both(src)[:, :, 0, :], cos, ALU.mult)
        k.link(v.tensor_tensor(both(out)[:, :, 1, :], both(src)[:, :, 1, :], cos, ALU.mult))
        return v.tensor_tensor(out, out, tmp, ALU.add)

    def tables(self, t, n):
        cos, sin = self.tab[:, C_ROPE_K["cos"]], self.tab[:, C_ROPE_K["sin"]]
        return tuple(ap[:, t * HALF:(t + n) * HALF].rearrange("p (t n) -> p t n", n=HALF) for ap in (cos, sin))

    def dve_q(self, v, ph, g=0):
        k = self.k
        if self.rope:
            v.wait_ge(*ph.filled("q", g))
            cos, sin = (every_head(c[:, 0, :], PER_GROUP) for c in self.tables(0, 1))
            self.rotate(v, heads(k.ps(4), 4), heads(self.qn, 4), heads(self.tmp, 4), cos, sin, PER_GROUP).then_inc(ph.drain("q"), 1)
            return
        v.wait_ge(*ph.done("q_sq", g))
        k.link(v.reduce_sum(self.q_ssq, heads(self.tmp, PER_GROUP), AX_X))
        v.tensor_scalar(self.q_ssq, self.q_ssq, 1.0 / P, 1e-5, ALU.mult, ALU.add).then_inc(ph.mark("q_var"), 1)
        v.wait_ge(*ph.done("q_rs", g))
        v.tensor_tensor(heads(self.qn, PER_GROUP), heads(k.ps(4), PER_GROUP), per_head(self.rq, P), ALU.mult).then_inc(ph.drain("q"), 1)

    def dve_softmax(self, v, ph, h, g=0):
        k = self.k
        v.wait_ge(*ph.filled(f"s{h}", g))
        v.memset(self.tick, 0.0)
        v.tensor_tensor_reduce(out=self.probs[h % 2], in0=k.wide[:, :], in1=self.mask, scale=1.0, scalar=NEG_MAX,
                               op0=ALU.add, op1=ALU.max, accum_out=self.m[:, h:h + 1]).then_inc(ph.drain(f"s{h}"), 1)
        v.wait_ge(*ph.drained(f"s{h}", g))
        v.tensor_scalar(self.m[:, h:h + 1], self.m[:, h:h + 1], -1.0, None, ALU.mult).then_inc(ph.mark(f"shift{h}"), 1)

    def dve_norm(self, v, ph, g=0):
        k = self.k
        v.wait_ge(*ph.done("exp3", g))
        k.link(v.reciprocal(self.inv, self.sum))
        v.wait_ge(*ph.filled("o", g))
        v.tensor_tensor(heads(self.on, PER_GROUP), heads(k.ps(6), PER_GROUP), per_head(self.inv, P), ALU.mult).then_inc(ph.drain("o"), 1)

    def dve_kv(self, v, ph, g=0):
        k = self.k
        for f in range(8):
            bank = k.ps(int(self.KV_BANK[f"kv{f}"]))
            src = bank.rearrange("p (t s n) -> p t s n", t=2, s=2)[:, :, 0, :]
            out = heads(self.keys[:, 256 * f:256 * f + 256], 2)
            v.wait_ge(*ph.done(f"v{f}", g))
            if self.rope:
                cos, sin = self.tables(2 * f, 2)
                self.rotate(v, src, out, heads(self.tmpk, 2), cos, sin, 2).then_inc(ph.drain(f"kv{f}"), 1)
                v.wait_ge(*ph.drained(f"kv{f}", g))
                continue
            s = slice(2 * f, 2 * f + 2)
            v.tensor_scalar(self.k_ssq[:, s], self.k_ssq[:, s], 1.0 / P, 1e-5, ALU.mult, ALU.add).then_inc(ph.mark(f"k_var{f}"), 1)
            v.wait_ge(*ph.done(f"k_rs{f}", g))
            v.tensor_tensor(out, src, per_head(self.rk[:, s], P), ALU.mult).then_inc(ph.drain(f"kv{f}"), 1)

    def dve(self, v):
        k, f = self.k, self.first
        self.ln_dve(v, f)
        v.wait_ge(*f.loaded("load_tab"))
        if not self.rope:
            k.link(v.tensor_scalar(self.qw, self.qw, self.scale, None, ALU.mult))
        v.wait_ge(*f.loaded("load_mask"))
        self.dve_q(v, f)
        self.dve_kv(v, f)
        with v.Fori(0, GROUPS - 1) as g:
            b = self.body
            k.chain.loop(g, 10 if self.rope else 2)
            self.dve_softmax(v, b, 0, g)
            self.dve_q(v, b, g)
            for h in range(1, PER_GROUP):
                self.dve_softmax(v, b, h, g)
            self.dve_norm(v, b, g)
            self.dve_kv(v, b, g)
        k.chain.end(GROUPS - 1)
        self.dve_softmax(v, self.last, 0)
        for h in range(1, PER_GROUP):
            self.dve_softmax(v, self.last, h)
        self.dve_norm(v, self.last)
        v.wait_ge(*self.last.filled("y"))
        self.add_output(v, self.last)


class L2Attn(Layer):

    def __init__(self, k):
        super().__init__(k)
        ev = [("load_pack", "load_pack1")] + LN_EVENTS + [("q", "0"), ("kv", "1"), ("v", "v_ready")]
        ev += [(f"kT{j}", "3") for j in range(2)]
        for g in range(GROUPS):
            ev += [(f"qT{g}", "45"[g % 2])]
        for g in range(GROUPS):
            ev += [(f"s{g}", "01"[g % 2]), (f"shift{g}", "shift"), (f"exp{g}", "exp"), (f"norm{g}", "norm"), (f"pT{g}", "23"[g % 2])]
        self.y = self.p = Phase(k, ev + [("o", "6"), ("oT", "4"), ("y", "7")])
        pack_ = k.area("pack1")
        self.wq, self.wkv = (pack_[:, C_L2A[n]].rearrange("p (o n) -> p o n", o=DC) for n in ("wq", "wkv"))
        self.wo = pack_[:, C_L2A["wo"]].rearrange("p (o n) -> p o n", o=DC)
        self.cos, self.sin = pack_[:, C_L2A["cos"]], pack_[:, C_L2A["sin"]]
        w = k.area("work")
        self.qn, self.tmp, self.kn, self.tmpk, self.v = w[:, 0:512], w[:, 512:1024], w[:, 1024:1152], w[:, 1152:1280], w[:, 1280:1408]
        self.qT, self.kT = w[0:HD2, 1536:5632], w[0:HD2, 5632:6656]
        self.probs = [w[:, 6656:7168], w[:, 7168:7680]]
        self.pT = [w[:, 7680:8192], w[:, 8192:8704]]
        self.on, self.oT = w[:, 8704:9216], w[:, 9216:9728]
        self.max, self.sum, self.inv = (k.small[:, 4 * j:4 * j + 4] for j in range(3))

    def sp(self, sp):
        k = self.k
        if "L1a" in k.layers:
            sp.wait_ge(*k.layers["L1a"].y.drained("y"))
        sp.dma_start(k.area("pack1", 0, C_L2A["all"]), k.dram["l2a"]).then_inc(self.p.mark("load_pack"), 16)

    def pe(self, pe):
        k, p = self.k, self.p
        self.ln_pe(pe, p)
        pe.wait_ge(*p.drained("ln"))
        pe.wait_ge(*p.loaded("load_pack"))
        pe.wait_ge(*p.room("q"))
        self.project(pe, k.ps(0), self.wq, D).then_inc(p.fill("q"), 1)
        pe.wait_ge(*p.room("kv"))
        self.project(pe, k.ps(1), self.wkv, 256).then_inc(p.fill("kv"), 1)
        pe.wait_ge(*p.drained("q"))

        def turn16(name, bank, src, first):
            pe.wait_ge(*p.room(name))
            for j in range(4):
                c = (first + j) * HD2
                last = pe.transpose(k.ps(bank)[0:HD2, j * P:(j + 1) * P], src[:, c:c + HD2], k.ident)
            last.then_inc(p.fill(name), 1)

        for g in range(GROUPS):
            turn16(f"qT{g}", 4 + g % 2, self.qn, 4 * g)
        pe.wait_ge(*p.drained("kv"))
        for j in range(2):
            turn16(f"kT{j}", 3, self.kn, 4 * j)
        pe.wait_ge(*p.done("v"))
        pe.wait_ge(*p.drained("kT1"))
        pe.wait_ge(*p.room("o"))

        def scores(g):
            pe.wait_ge(*p.drained(f"qT{g}"))
            pe.wait_ge(*p.room(f"s{g}"))
            for h in range(4):
                c = 4 * g + h
                last = pe.matmul(k.ps(g % 2)[:, h * P:(h + 1) * P], self.qT[:, c * P:(c + 1) * P], self.kT[:, g * P:(g + 1) * P], start=True, stop=True)
            last.then_inc(p.fill(f"s{g}"), 1)

        def attend(g):
            pe.wait_ge(*p.drained(f"pT{g}"))
            for h in range(4):
                c = 4 * g + h
                last = pe.matmul(k.ps(6)[:, c * HD2:(c + 1) * HD2], self.pT[g % 2][:, h * P:(h + 1) * P], self.v[:, g * HD2:(g + 1) * HD2], start=True, stop=True)
            if g == GROUPS - 1:
                last.then_inc(p.fill("o"), 1)

        scores(0)
        for g in range(GROUPS + 1):
            if g + 1 < GROUPS:
                scores(g + 1)
            if g < GROUPS:
                pe.wait_ge(*p.done(f"norm{g}"))
                pe.wait_ge(*p.room(f"pT{g}"))
                self.turn(pe, k.ps(2 + g % 2), self.probs[g % 2], 4).then_inc(p.fill(f"pT{g}"), 1)
            if g >= 1:
                attend(g - 1)
        pe.wait_ge(*p.drained("o"))
        pe.wait_ge(*p.room("oT"))
        self.turn(pe, k.ps(4), self.on, DC).then_inc(p.fill("oT"), 1)
        pe.wait_ge(*p.drained("oT"))
        pe.wait_ge(*p.room("y"))
        self.project(pe, k.ps(7), self.wo, D, src=heads(self.oT, DC)).then_inc(p.fill("y"), 1)

    def act(self, act):
        k, p = self.k, self.p
        self.ln_act(act, p)
        for g in range(GROUPS):
            act.wait_ge(*p.filled(f"qT{g}"))
            act.activation(self.qT[:, 512 * g:512 * g + 512], k.ps(4 + g % 2)[0:HD2, :], ACT.Copy).then_inc(p.drain(f"qT{g}"), 1)
        for j in range(2):
            act.wait_ge(*p.filled(f"kT{j}"))
            act.activation(self.kT[:, 512 * j:512 * j + 512], k.ps(3)[0:HD2, :], ACT.Copy).then_inc(p.drain(f"kT{j}"), 1)
        for g in range(GROUPS + 1):
            if g < GROUPS:
                act.wait_ge(*p.done(f"shift{g}"))
                act.activation(self.probs[g % 2], self.probs[g % 2], ACT.Exp).then_inc(p.mark(f"exp{g}"), 1)
            if g >= 1:
                act.wait_ge(*p.filled(f"pT{g - 1}"))
                act.activation(self.pT[(g - 1) % 2], k.ps(2 + (g - 1) % 2), ACT.Copy).then_inc(p.drain(f"pT{g - 1}"), 1)

    def rotate(self, v, src, out, tmp, n):
        both = lambda ap: ap.rearrange("p (h s n) -> p h s n", s=2, n=8)
        cos, sin = every_head(self.cos, n), every_head(self.sin, n)
        v.scalar_tensor_tensor(out=both(tmp)[:, :, 0, :], in0=both(src)[:, :, 1, :], scalar=-1.0, in1=sin, op0=ALU.mult, op1=ALU.mult)
        v.tensor_tensor(both(tmp)[:, :, 1, :], both(src)[:, :, 0, :], sin, ALU.mult)
        v.tensor_tensor(both(out)[:, :, 0, :], both(src)[:, :, 0, :], cos, ALU.mult)
        self.k.link(v.tensor_tensor(both(out)[:, :, 1, :], both(src)[:, :, 1, :], cos, ALU.mult))
        return v.tensor_tensor(out, out, tmp, ALU.add)

    def dve(self, v):
        k, p = self.k, self.p
        self.ln_dve(v, p)
        v.wait_ge(*p.loaded("load_pack"))
        v.wait_ge(*p.filled("q"))
        self.rotate(v, k.ps(0), self.qn, self.tmp, 32).then_inc(p.drain("q"), 1)
        v.wait_ge(*p.filled("kv"))
        v.tensor_copy(self.v, k.ps(1)[:, P:2 * P]).then_inc(p.mark("v"), 1)
        self.rotate(v, k.ps(1)[:, 0:P], self.kn, self.tmpk, 8).then_inc(p.drain("kv"), 1)

        def shift(g):
            pr = heads(self.probs[g % 2], 4)
            v.wait_ge(*p.filled(f"s{g}"))
            v.scalar_tensor_tensor(out=pr, in0=heads(k.ps(g % 2), 4), scalar=float(HD2) ** -0.5, in1=every_head(k.causal, 4),
                                   op0=ALU.mult, op1=ALU.add).then_inc(p.drain(f"s{g}"), 1)
            v.wait_ge(*p.drained(f"s{g}"))
            k.link(v.reduce_max(self.max, pr, AX_X))
            v.tensor_tensor(pr, pr, per_head(self.max, P), ALU.subtract).then_inc(p.mark(f"shift{g}"), 1)

        def norm(g):
            pr = heads(self.probs[g % 2], 4)
            v.wait_ge(*p.done(f"exp{g}"))
            k.link(v.reduce_sum(self.sum, pr, AX_X))
            k.link(v.reciprocal(self.inv, self.sum))
            v.tensor_tensor(pr, pr, per_head(self.inv, P), ALU.mult).then_inc(p.mark(f"norm{g}"), 1)

        for g in range(GROUPS + 1):
            if g < GROUPS:
                shift(g)
            if g >= 1:
                norm(g - 1)
        v.wait_ge(*p.filled("o"))
        v.tensor_copy(self.on, k.ps(6)).then_inc(p.drain("o"), 1)
        v.wait_ge(*p.filled("oT"))
        v.tensor_copy(self.oT, k.ps(4)).then_inc(p.drain("oT"), 1)
        v.wait_ge(*p.filled("y"))
        self.add_output(v, p)


class L2Ffn(Layer):
    SLOTS = 4

    def __init__(self, k):
        super().__init__(k)
        ev = [("load_pack", "load_pack0"), ("load_bias", "load_bias")] + [(f"load{j}", f"load_expert{j % self.SLOTS}") for j in range(E8)]
        ev += LN_EVENTS + [("g", "6"), ("shift", "shift"), ("exp", "exp"), ("sel", "chosen"), ("selT", "5")]
        ev += [(f"e{j}", str(j % 4)) for j in range(E8)] + [("y", "7")]
        self.y = self.p = Phase(k, ev)
        pack_ = k.area("pack0")
        self.wg = pack_[:, C_L2F["gate"]].rearrange("p (o n) -> p o n", o=DC)
        self.bg, self.rank = pack_[:, C_L2F["bgate"]], pack_[:, C_L2F["rank"]]
        self.bias, self.selT = k.area("work", 0, 512)[0:E8, :], k.area("work", 512, 640)[0:E8, :]
        self.slots = [k.area("weights", 5120 + 2048 * j, 5120 + 2048 * (j + 1)).rearrange("p (o n) -> p o n", o=DC) for j in range(self.SLOTS)]
        s = k.small
        self.g, self.e, self.sel = s[:, 0:8], s[:, 8:16], s[:, 16:24]
        self.m, self.sum, self.inv, self.top = (s[:, 32 + j:33 + j] for j in range(4))

    def load_expert(self, sp, j):
        slot = self.slots[j % self.SLOTS].rearrange("p o n -> p (o n)")
        sp.dma_start(slot, self.k.dram["l2f"][j]).then_inc(self.p.mark(f"load{j}"), 16)

    def sp(self, sp):
        k = self.k
        for name in ("L1a", "L1f"):
            if name in k.layers:
                sp.wait_ge(*k.layers[name].y.drained("y"))
        sp.dma_start(k.area("pack0", 0, C_L2F["all"]), k.dram["l2f_gate"]).then_inc(self.p.mark("load_pack"), 16)
        for j in range(self.SLOTS):
            self.load_expert(sp, j)
        if "L2a" in k.layers:
            sp.wait_ge(*k.layers["L2a"].y.filled("y"))
        sp.dma_start(self.bias, k.dram["l2f_bias"]).then_inc(self.p.mark("load_bias"), 16)
        for j in range(self.SLOTS, E8):
            sp.wait_ge(*self.p.filled(f"e{j - self.SLOTS}"))
            self.load_expert(sp, j)

    def pe(self, pe):
        k, p = self.k, self.p
        self.ln_pe(pe, p)
        pe.wait_ge(*p.drained("ln"))
        pe.wait_ge(*p.loaded("load_pack"))
        pe.wait_ge(*p.room("g"))
        self.project(pe, k.ps(6), self.wg, E8).then_inc(p.fill("g"), 1)
        for j in range(E8):
            pe.wait_ge(*p.loaded(f"load{j}"))
            pe.wait_ge(*p.room(f"e{j}"))
            self.project(pe, k.ps(j % 4), self.slots[j % self.SLOTS], D).then_inc(p.fill(f"e{j}"), 1)
            if j == 3:
                pe.wait_ge(*p.done("sel"))
                pe.wait_ge(*p.room("selT"))
                pe.transpose(k.ps(5)[0:E8, 0:P], self.sel, k.ident).then_inc(p.fill("selT"), 1)
        pe.wait_ge(*p.drained("selT"))
        pe.wait_ge(*p.loaded("load_bias"))
        pe.wait_ge(*p.room("y"))
        pe.matmul(k.ps(7), self.selT, self.bias, start=True, stop=True).then_inc(p.fill("y"), 1)

    def act(self, act):
        k, p = self.k, self.p
        self.ln_act(act, p)
        act.wait_ge(*p.done("shift"))
        act.activation(self.e, self.e, ACT.Exp, accum_out=self.sum).then_inc(p.mark("exp"), 1)
        act.wait_ge(*p.filled("selT"))
        act.activation(self.selT, k.ps(5)[0:E8, 0:P], ACT.Copy).then_inc(p.drain("selT"), 1)

    def dve(self, v):
        k, p = self.k, self.p
        self.ln_dve(v, p)
        v.wait_ge(*p.loaded("load_pack"))
        v.wait_ge(*p.filled("g"))
        v.tensor_tensor(self.g, k.ps(6)[:, 0:E8], self.bg, ALU.add).then_inc(p.drain("g"), 1)
        v.wait_ge(*p.drained("g"))
        k.link(v.reduce_max(self.m, self.g, AX_X))
        v.tensor_scalar(self.e, self.g, self.m, None, ALU.subtract).then_inc(p.mark("shift"), 1)
        v.wait_ge(*p.done("exp"))
        k.link(v.reciprocal(self.inv, self.sum))
        k.link(v.tensor_scalar(self.g, self.e, self.inv, None, ALU.mult))
        k.link(v.reduce_max(self.m, self.g, AX_X))
        k.link(v.tensor_scalar(self.e, self.g, self.m, None, ALU.is_equal))
        k.link(v.tensor_tensor(self.e, self.e, self.rank, ALU.mult))
        k.link(v.reduce_max(self.top, self.e, AX_X))
        v.tensor_scalar(self.sel, self.e, self.top, None, ALU.is_equal).then_inc(p.mark("sel"), 1)
        v.wait_ge(*p.done("sel"))
        for j in range(E8):
            v.wait_ge(*p.filled(f"e{j}"))
            v.scalar_tensor_tensor(out=k.x, in0=k.ps(j % 4), scalar=self.sel[:, j:j + 1], in1=k.x, op0=ALU.mult,
                                   op1=ALU.add).then_inc(p.drain(f"e{j}"), 1)
            v.wait_ge(*p.drained(f"e{j}"))
        v.wait_ge(*p.filled("y"))
        self.add_output(v, p)


class L3Attn(Layer):
    SLOTS = 4

    def __init__(self, k):
        super().__init__(k)
        ev = [("load_v", "load_values")] + [(f"load{g}", f"load_expert{g % self.SLOTS}") for g in range(GROUPS)]
        ev += [(f"pair{g}", "row_pairs") for g in range(GROUPS)] + [(f"sum{g}", "row_sums") for g in range(GROUPS)]
        self.y = self.p = Phase(k, ev + LN_EVENTS + [("v0", "5"), ("v1", "6"), ("part0", "l3a_part"), ("part1", "l3a_part"), ("part2", "l3a_part"), ("part3", "l3a_part"),
                                     ("part4", "l3a_part"), ("part5", "l3a_part"), ("part6", "l3a_part"), ("y", "7")])
        w, p0, a = k.area("weights"), k.area("pack0"), k.area("work")
        self.wv = w[:, 5120:9216].rearrange("p (o n) -> p o n", o=DC)
        self.slots = [w[:, 9216:11264], w[:, 11264:13312], p0[:, 0:2048], p0[:, 2048:4096]]
        self.pairs = [a[:, 1024 * j:1024 * j + 1024] for j in range(2)]
        self.sums = [a[:, 2048 + 512 * j:2560 + 512 * j] for j in range(4)]
        self.vT = a[:, 4096:5120]

    def load_rows(self, sp, g):
        sp.dma_start(self.slots[g % self.SLOTS], self.k.dram["l3a_out"][g]).then_inc(self.p.mark(f"load{g}"), 16)

    def sp(self, sp):
        k, p = self.k, self.p
        if "L2f" in k.layers:
            sp.wait_ge(*k.layers["L2f"].y.drained("y"))
        sp.dma_start(k.area("weights", 5120, 9216), k.dram["l3a_v"]).then_inc(p.mark("load_v"), 16)
        for g in range(self.SLOTS):
            self.load_rows(sp, g)
        for g in range(self.SLOTS, GROUPS):
            sp.wait_ge(*p.done(f"pair{g - self.SLOTS}"))
            self.load_rows(sp, g)

    def pe(self, pe):
        k, p = self.k, self.p
        self.ln_pe(pe, p)
        pe.wait_ge(*p.drained("ln"))
        pe.wait_ge(*p.loaded("load_v"))
        for j in range(2):
            pe.wait_ge(*p.room(f"v{j}"))
            for c in range(4):
                g = 4 * j + c
                for o in range(DC):
                    last = pe.matmul(k.ps(5 + j)[:, c * P:(c + 1) * P], self.wv[:, o, g * P:(g + 1) * P], k.xnT[:, o, :], start=o == 0, stop=o == DC - 1)
            last.then_inc(p.fill(f"v{j}"), 1)
        pe.wait_ge(*p.room("y"))
        for g in range(GROUPS):
            if g % 4 == 0:
                pe.wait_ge(*p.drained(f"v{g // 4}"))
            pe.wait_ge(*p.done(f"sum{g}"))
            ins = pe.matmul(k.ps(7), self.vT[:, g * P:(g + 1) * P], self.sums[g % 4], start=g == 0, stop=g == GROUPS - 1)
            ins.then_inc(p.mark(f"part{g}") if g < GROUPS - 1 else p.fill("y"), 1)

    def act(self, act):
        k, p = self.k, self.p
        self.ln_act(act, p)
        for j in range(2):
            act.wait_ge(*p.filled(f"v{j}"))
            act.activation(self.vT[:, 512 * j:512 * j + 512], k.ps(5 + j), ACT.Copy).then_inc(p.drain(f"v{j}"), 1)

    def dve(self, v):
        k, p = self.k, self.p
        self.ln_dve(v, p)
        for g in range(GROUPS):
            slot, pair = self.slots[g % self.SLOTS], self.pairs[g % 2]
            v.wait_ge(*p.loaded(f"load{g}"))
            v.tensor_tensor(pair, slot[:, 0:1024], slot[:, 1024:2048], ALU.add).then_inc(p.mark(f"pair{g}"), 1)
            v.wait_ge(*p.done(f"pair{g}"))
            if g >= 4:
                v.wait_ge(*p.done(f"part{g - 4}"))
            v.tensor_tensor(self.sums[g % 4], pair[:, 0:512], pair[:, 512:1024], ALU.add).then_inc(p.mark(f"sum{g}"), 1)
        v.wait_ge(*p.filled("y"))
        self.add_output(v, p)


class L3Ffn(Layer):

    def __init__(self, k):
        super().__init__(k)
        self.y = self.p = Phase(k, [("load_pack", "load_pack1"), ("load_mask", "load_fmask"), ("load_f", "load_fourier"), ("w", "decoders"), ("m", "6")] + LN_EVENTS + [
            ("e", "5"), ("e_out", "encoded"), ("eT", "4"), ("y", "7")])
        pack_ = k.area("pack1")
        self.w, self.enc = (pack_[:, C_L3F[n]].rearrange("p (o n) -> p o n", o=DC) for n in ("w", "enc"))
        self.coef, self.bias = pack_[:, C_L3F["coef"]], pack_[:, C_L3F["bias"]]
        self.fourier = k.area("weights", 0, 2048).rearrange("p (o n) -> p o n", o=DC)
        a = k.area("work", 5120)
        self.mask_words, self.mask = a[:, 0:120].bitcast(mybir.dt.int32), a[:, 0:120].bitcast(U8)
        self.maskf, self.dec, self.e = a[:, 128:608], a[:, 608:768], a[:, 768:808]
        self.m, self.eT = a[0:R3, 1024:1536], a[0:R3, 1536:1664]

    def sp(self, sp):
        k = self.k
        for name in ("L2a", "L3x"):
            if name in k.layers:
                sp.wait_ge(*k.layers[name].y.drained("y"))
        sp.dma_start(k.area("pack1", 0, C_L3F["all"]), k.dram["l3f"]).then_inc(self.p.mark("load_pack"), 16)
        sp.dma_start(self.mask_words, k.dram["l3f_mask"]).then_inc(self.p.mark("load_mask"), 16)
        sp.dma_start(k.area("weights", 0, 2048), k.dram["fourier"]).then_inc(self.p.mark("load_f"), 16)

    def pe(self, pe):
        k, p = self.k, self.p
        pe.wait_ge(*p.done("w"))
        pe.wait_ge(*p.loaded("load_f"))
        pe.wait_ge(*p.room("m"))
        dec = self.dec.rearrange("p (o r) -> p o r", o=DC)
        for o in range(DC):
            last = pe.matmul(k.ps(6)[0:R3, :], dec[:, o, :], self.fourier[:, o, :], start=o == 0, stop=o == DC - 1)
        last.then_inc(p.fill("m"), 1)
        self.ln_pe(pe, p)
        pe.wait_ge(*p.drained("ln"))
        pe.wait_ge(*p.room("e"))
        pe.wait_ge(*p.loaded("load_pack"))
        self.project(pe, k.ps(5), self.enc, R3).then_inc(p.fill("e"), 1)
        pe.wait_ge(*p.room("y"))
        self.project(pe, k.ps(7), self.w, D, stop=False)
        pe.wait_ge(*p.drained("e"))
        pe.transpose(k.ps(4)[0:R3, 0:P], self.e, k.ident).then_inc(p.fill("eT"), 1)
        pe.wait_ge(*p.drained("eT"))
        pe.wait_ge(*p.drained("m"))
        pe.matmul(k.ps(7), self.eT, self.m, start=False, stop=True).then_inc(p.fill("y"), 1)

    def act(self, act):
        k, p = self.k, self.p
        act.wait_ge(*p.filled("m"))
        act.activation(self.m, k.ps(6)[0:R3, :], ACT.Copy, scale=0.5).then_inc(p.drain("m"), 1)
        self.ln_act(act, p)
        act.wait_ge(*p.filled("e"))
        act.activation(self.e, k.ps(5)[:, 0:R3], ACT.Copy).then_inc(p.drain("e"), 1)
        act.wait_ge(*p.filled("eT"))
        act.activation(self.eT, k.ps(4)[0:R3, 0:P], ACT.Copy).then_inc(p.drain("eT"), 1)

    def dve(self, v):
        k, p = self.k, self.p
        v.wait_ge(*p.loaded("load_mask"))
        v.wait_ge(*p.loaded("load_pack"))
        k.link(v.tensor_copy(self.maskf, self.mask))
        k.link(v.tensor_tensor(self.maskf, self.maskf, self.coef, ALU.mult))
        masked = self.maskf.rearrange("p (o e r) -> p o e r", o=DC, e=3)
        dec = self.dec.rearrange("p (o r) -> p o r", o=DC)
        k.link(v.tensor_tensor(dec, masked[:, :, 0, :], masked[:, :, 1, :], ALU.add))
        v.tensor_tensor(dec, dec, masked[:, :, 2, :], ALU.add).then_inc(p.mark("w"), 1)
        self.ln_dve(v, p)
        k.link(v.tensor_tensor(k.x, k.x, self.bias, ALU.add))
        v.wait_ge(*p.filled("y"))
        self.add_output(v, p)


LAYERS = ("L0x", "L0a", "L0f", "L1x", "L1a", "L1f", "L2x", "L2a", "L2f", "L3x", "L3a", "L3f")


def build(nc, dram, out):
    with ExitStack() as ctx:
        k = Program(nc, ctx, dram)
        start = Phase(k, [("load_const", "load_const"), ("load_x", "load_x"), ("zeros", "zeros"), ("store", "store")])
        make = {"L0x": lambda: L0Xattn(k), "L0a": lambda: SelfAttention(k), "L0f": lambda: L0Ffn(k),
                "L1x": lambda: L1Xattn(k), "L1a": lambda: Scan(k), "L1f": lambda: L1Ffn(k),
                "L2x": lambda: CrossAttention(k, "l2x", True), "L2a": lambda: L2Attn(k), "L2f": lambda: L2Ffn(k),
                "L3x": lambda: CrossAttention(k, "l3x", False), "L3a": lambda: L3Attn(k),
                "L3f": lambda: L3Ffn(k)}
        k.layers = {}
        for name in LAYERS:
            k.layers[name] = make[name]()
        layers = list(k.layers.values())
        block = ctx.enter_context(nc.Block())

        @block.sync
        def _(sp):
            sp.dma_start(k.x, dram["x"]).then_inc(start.mark("load_x"), 16)
            sp.dma_start(k.mem[:, AREA["ident"].start:AREA["minus_half"].stop], dram["const"]).then_inc(start.mark("load_const"), 16)
            for layer in layers:
                layer.sp(sp)
            sp.wait_ge(*layers[-1].y.drained("y"))
            sp.dma_start(out, k.x).then_inc(start.mark("store"), 16)
            sp.wait_ge(*start.loaded("store"))

        @block.gpsimd
        def _(pool):
            pool.wait_ge(*start.loaded("load_const"))
            for layer in layers:
                layer.pool(pool)

        @block.tensor
        def _(pe):
            pe.wait_ge(*start.loaded("load_const"))
            pe.wait_ge(*start.done("zeros"))
            for layer in layers:
                layer.pe(pe)

        @block.scalar
        def _(act):
            k.act_chain = Chain(act, k.sem("scalar_step"))
            k.act_link = k.act_chain.link
            for layer in layers:
                layer.act(act)

        @block.vector
        def _(v):
            k.chain = Chain(v, k.sem("vector_step"))
            k.link = k.chain.link
            v.memset(k.zeros, 0.0).then_inc(start.mark("zeros"), 1)
            for b in range(8):
                v.memset(k.ps(b), 0.0).then_inc(k.sem(f"drained_{b}"), 1)
            v.wait_ge(*start.loaded("load_x"))
            v.wait_ge(*start.loaded("load_const"))
            for layer in layers:
                layer.dve(v)


def tiles(a):
    n = a.shape[1]
    return a.reshape(-1, P, n).transpose(1, 0, 2).reshape(P, -1)


def rows(a, n=P):
    return np.broadcast_to(a.reshape(1, -1), (n, a.size))


def cols(a):
    return a.reshape(-1, P).T


def pack(*parts):
    return np.ascontiguousarray(np.concatenate(parts, axis=1))


def rope_table(positions, inv_freq):
    ang = positions[:, None].astype(np.float32) * inv_freq[None, :].astype(np.float32)
    return np.cos(ang.astype(np.float64)).astype(np.float32), np.sin(ang.astype(np.float64)).astype(np.float32)


def group_weights(wq, wk, wv, wo, d=P):
    out = []
    for g in range(GROUPS):
        q = tiles(wq[:, g * 512:(g + 1) * 512])
        kv = tiles(np.concatenate([wk[:, g * P:(g + 1) * P], wv[:, g * P:(g + 1) * P]], axis=1))
        out.append(np.concatenate([q, kv, tiles(wo[g * 512:(g + 1) * 512])], axis=1))
    return np.stack(out)


def layout(i):
    half = HALF
    pos = np.arange(P)
    inv0 = (10000.0 ** (-np.arange(half, dtype=np.float32) / half).astype(np.float64)).astype(np.float32)
    c0, s0 = rope_table(pos, inv0)
    a = {"x": i["x"][0],
         "const": pack(np.eye(P, dtype=np.float32), np.where(np.tri(P, dtype=bool), 0.0, NEG).astype(np.float32),
                       np.full((P, 16), -0.5, np.float32)),
         "ctxT": tiles(i["ctx_4096"][0].T), "ctx": tiles(i["ctx_4096"][0])}
    a["l0x"] = pack(tiles(i["L0_xattn_Wq"].T), tiles(i["L0_xattn_Wk"]), rows(i["L0_xattn_bq"]), rows(i["L0_xattn_bk"]))
    a["l0a"] = group_weights(i["L0_attn_wq"], i["L0_attn_wk"], i["L0_attn_wv"], i["L0_attn_wo"])
    a["rope_self"] = pack(c0, s0, -s0)
    a["l0f"] = pack(tiles(i["L0_ffn_W"].T), tiles(i["L0_ffn_lora_A"].reshape(P, D).T),
                    i["L0_ffn_lora_B"].transpose(0, 2, 1).reshape(P, D), rows(i["L0_ffn_bias"]),
                    np.repeat(i["L0_ffn_lora_weights"], 16)[:, None])
    a["l1x"] = pack(tiles(i["L1_xattn_Wq_w"].T), tiles(i["L1_xattn_Wk_w"].T), rows(i["L1_xattn_Wq_b"]), rows(i["L1_xattn_Wk_b"]),
                    rows(i["L1_xattn_fn_w"]), cols(i["L1_xattn_fn_w"]), cols(i["L1_xattn_qn_w"]), cols(i["L1_xattn_kn_w"]))

    inner = GROUPS * GROUP_D
    wt = i["L1_attn_in_proj_w"].T
    xw, bw, cw = inner, 2 * inner, 2 * inner + GROUPS * P
    conv = np.concatenate([i["L1_attn_conv_w"][:, 0, :], i["L1_attn_conv_b"][:, None]], axis=1)
    outw = i["L1_attn_out_proj_w"].T
    groups, convs, table = [], [], []
    for g in range(GROUPS):
        own = np.concatenate([np.arange(g * GROUP_D, (g + 1) * GROUP_D), inner + np.arange(g * P, (g + 1) * P),
                              inner + GROUPS * P + np.arange(g * P, (g + 1) * P)])
        groups.append(np.concatenate([tiles(wt[:, xw + own]), tiles(wt[:, g * GROUP_D:(g + 1) * GROUP_D]),
                                      tiles(outw[g * GROUP_D:(g + 1) * GROUP_D])], axis=1))
        convs.append(tiles(conv[own]))
        table.append(np.concatenate([cols(i["L1_attn_norm_w"][g * GROUP_D:(g + 1) * GROUP_D]), np.zeros((P, 32), np.float32),
                                     rows(i["L1_attn_D"][g * HG:(g + 1) * HG])], axis=1))
    a["l1a"] = np.stack(groups)
    a["l1a_small"] = pack(tiles(wt[:, cw + GROUPS * P:]), *convs, *table, rows(i["L1_attn_dt_bias"]),
                          -np.arange(1, P + 1, dtype=np.float32)[:, None], np.triu(np.ones((P, P), np.float32)))
    a["l1f"] = pack(tiles(i["L1_ffn_W_base"].T), tiles(i["L1_ffn_A_w"].reshape(P, D).T),
                    tiles(np.concatenate([i["L1_ffn_W_gate"].T, i["L1_ffn_W_thr"][:, None]], axis=1)),
                    i["L1_ffn_B_w"].transpose(0, 2, 1).reshape(P, D), rows(i["L1_ffn_b_base"]), rows(i["L1_ffn_b_thr"]))

    inv2 = (1.0 / (10000.0 ** (np.arange(0, P, 2, dtype=np.float32) / P).astype(np.float64)).astype(np.float32)).astype(np.float32)
    ck, sk = rope_table(np.arange(KEYS), inv2)
    a["rope_keys"] = pack(tiles(ck), tiles(sk))
    a["l2x"] = group_weights(i["L2_xattn_wq"], i["L2_xattn_wk"], i["L2_xattn_wv"], i["L2_xattn_wo"])
    a["mask2"], a["mask3"] = i["mask_BxSxS2_ff0"][0], i["mask_1x1xSxS2_ff0"][0, 0]
    inv16 = (1.0 / (10000.0 ** (np.arange(0, HD2, 2, dtype=np.float32) / HD2).astype(np.float64)).astype(np.float32)).astype(np.float32)
    c16, s16 = rope_table(pos, inv16)
    a["l2a"] = pack(tiles(i["L2_attn_wq"].T), tiles(np.concatenate([i["L2_attn_wk"].T, i["L2_attn_wv"].T], axis=1)),
                    tiles(i["L2_attn_wo"].T), c16, s16)
    a["l2f_gate"] = pack(tiles(i["L2_ffn_gate_w"].T), rows(i["L2_ffn_gate_b"]), rows(np.arange(E8, 0, -1).astype(np.float32)))
    a["l2f_bias"] = i["L2_ffn_expert_b"]
    a["l2f"] = np.stack([tiles(w.T) for w in i["L2_ffn_expert_w"]])
    a["l3x"] = group_weights(i["L3_xattn_Wq"].T, i["L3_xattn_Wk"].T, i["L3_xattn_Wv"].T, i["L3_xattn_Wo"].T)
    a["l3x_norm"] = pack(i["L3_xattn_q_norm_w"][:, None], i["L3_xattn_k_norm_w"][:, None])

    qkv = i["L3_attn_weight_qkv"].reshape(GROUPS, PER_GROUP + 2, P, D)
    a["l3a_v"] = tiles(qkv[:, PER_GROUP + 1].reshape(GROUPS * P, D).T)
    a["l3a_out"] = np.stack([tiles(w) for w in i["L3_attn_weight_proj"].T.reshape(GROUPS, PER_GROUP * P, D)])

    coefs = np.concatenate([i["L3_ffn_coefs0"], i["L3_ffn_coefs1"]], axis=2)
    masks = np.concatenate([i["L3_ffn_mask0"], i["L3_ffn_mask1"]], axis=2)
    by_row = lambda c: tiles(c.transpose(1, 0, 2).reshape(D, -1))
    a["l3f"] = pack(tiles(i["L3_ffn_W_base"].T), tiles(np.concatenate([i["L3_ffn_enc0"], i["L3_ffn_enc1"]], axis=0).T),
                    by_row(coefs), rows(i["L3_ffn_b_base"]))
    a["l3f_mask"] = np.ascontiguousarray(by_row(masks)).view(np.int32)
    a["fourier"] = tiles(fourier_basis())
    return a


def fourier_basis():
    n = np.arange(D, dtype=np.float64)
    f = np.arange(1, (D - 1) // 2 + 1, dtype=np.float64)
    basis = np.empty((D, D))
    basis[0] = D ** -0.5
    basis[1:D - 1:2] = (2.0 / D) ** 0.5 * np.cos(2 * np.pi * np.outer(f, n) / D)
    basis[2:D:2] = (2.0 / D) ** 0.5 * np.sin(2 * np.pi * np.outer(f, n) / D)
    basis[D - 1] = D ** -0.5 * (-1.0) ** n
    return basis.astype(np.float32)


def kernel(**inputs):
    import concourse.bacc as bacc
    from concourse.bass_utils import run_bass_kernel_spmd

    nc = bacc.Bacc("TRN2", target_bir_lowering=False, num_devices=1)
    arrays = {f"in_{n}": np.ascontiguousarray(a) for n, a in layout({n: np.asarray(a) for n, a in inputs.items()}).items()}
    dram = {n[3:]: nc.dram_tensor(n, a.shape, mybir.dt.from_np(a.dtype), kind="ExternalInput").ap() for n, a in arrays.items()}
    dram["cs"] = nc.dram_tensor("scan_cs", (GROUPS, HG * P), F32).ap()
    out = nc.dram_tensor("out_x", (P, D), F32, kind="ExternalOutput").ap()
    build(nc, dram, out)
    result = run_bass_kernel_spmd(nc, [arrays], core_ids=[0])
    return result.results[0]["out_x"].reshape(1, P, D)
```

```python
from contextlib import ExitStack

import numpy as np

import concourse.bass as bass
from concourse import mybir

F32 = mybir.dt.float32
U8 = mybir.dt.uint8
ACT = mybir.ActivationFunctionType
ALU = mybir.AluOpType
AX_X = mybir.AxisListType.X

P = 128
D = 512
DC = D // P
KEYS = 2048
KT = KEYS // P
GROUPS = 8
PER_GROUP = 4
NEG = -1.0e30
NEG_MAX = -3.0e38


class Phase:

    def __init__(self, prog, events, times=1):
        self.prog, self.at, self.per = prog, {}, {}
        for name, sem in events:
            self.per[sem] = self.per.get(sem, 0) + 1
            self.at[name] = (sem, self.per[sem])
        self.base = dict(prog.counts)
        for sem, n in self.per.items():
            prog.counts[sem] = prog.counts.get(sem, 0) + n * times

    def value(self, name, i=0):
        sem, k = self.at[name]
        return self.base.get(sem, 0) + k + i * self.per[sem]

    def filled(self, name, i=0):
        return self.prog.sem("filled_" + self.at[name][0]), self.value(name, i)

    def drained(self, name, i=0):
        return self.prog.sem("drained_" + self.at[name][0]), self.value(name, i) + 1

    def room(self, name, i=0):
        return self.prog.sem("drained_" + self.at[name][0]), self.value(name, i)

    def fill(self, name):
        return self.prog.sem("filled_" + self.at[name][0])

    def drain(self, name):
        return self.prog.sem("drained_" + self.at[name][0])

    def done(self, name, i=0):
        return self.prog.sem(self.at[name][0]), self.value(name, i)

    def mark(self, name):
        return self.prog.sem(self.at[name][0])

    def loaded(self, name, i=0):
        return self.prog.sem(self.at[name][0]), self.value(name, i) * 16

    def before(self, sem, i=0, kind=""):
        return self.prog.sem(kind + sem), self.base.get(sem, 0) + (kind == "drained_") + i * self.per.get(sem, 0)


class Chain:

    def __init__(self, eng, sem):
        self.eng, self.sem, self.n, self.i, self.per = eng, sem, 0, None, 0

    def link(self, ins):
        self.n += 1
        ins.then_inc(self.sem, 1)
        self.eng.wait_ge(self.sem, self.n if self.i is None else self.n + self.i * self.per)

    def loop(self, i, per):
        self.i, self.per, self.start = i, per, self.n

    def end(self, times):
        assert self.n - self.start == self.per, f"{self.n - self.start} links an iteration"
        self.n, self.i = self.start + self.per * times, None


def columns(*parts):
    out, at = {}, 0
    for name, n in parts:
        out[name] = slice(at, at + n)
        at += n
    out["all"] = at
    return out


HALF = P // 2
C_CONST = columns(("ident", P), ("causal", P), ("minus_half", 16))
C_L0X = columns(("wq", DC * D), ("wk", DC * D), ("bq", D), ("bk", D))
C_L0F = columns(("w", DC * D), ("a", DC * P), ("b", D), ("bias", D), ("coef", 1))
C_L1X = columns(("wq", DC * D), ("wk", DC * D), ("bq", D), ("bk", D), ("fn_row", D),
                ("fn", DC), ("qn", DC), ("kn", DC))
E8 = 8
C_L1F = columns(("w", DC * D), ("a", DC * P), ("gate", DC * (E8 + 1)), ("b", D), ("bias", D), ("bthr", 1))
HD2 = 16
C_L2A = columns(("wq", DC * D), ("wkv", DC * 256), ("wo", DC * D), ("cos", 8), ("sin", 8))
C_L2F = columns(("gate", DC * E8), ("bgate", E8), ("rank", E8))
R3 = 40
C_L3F = columns(("w", DC * D), ("enc", DC * R3), ("coef", DC * 3 * R3), ("bias", D))
C_ROPE_Q = columns(("cos", HALF), ("sin", HALF), ("nsin", HALF))
C_QKV = columns(("q", DC * D), ("kv", DC * 256))


AREA = columns(("ctxT", DC * KEYS), ("ctx", KT * D), ("weights", 13312), ("pack0", 5760), ("pack1", 5760),
               ("work", 9728), ("x", D), ("xn", D), ("xnT", D), ("ident", P), ("causal", P),
               ("minus_half", 16), ("zeros", P), ("small", 128))


class Program:

    def __init__(self, nc, ctx, dram):
        self.nc, self.dram, self.counts, self.sems = nc, dram, {}, {}
        self.ctx = ctx
        self.mem = ctx.enter_context(nc.sbuf_tensor("mem", [P, AREA["all"]], F32))
        self.bank = [ctx.enter_context(nc.psum_tensor(f"bank{b}", [P, 512], F32)) for b in range(4, 8)]
        self.wide = ctx.enter_context(nc.psum_tensor("wide", [P, 4 * 512], F32))
        self.x, self.xn, self.ident = self.area("x"), self.area("xn"), self.area("ident")
        self.zeros = self.area("zeros")
        self.causal, self.minus_half = self.area("causal"), self.area("minus_half")
        self.xnT = self.area("xnT").rearrange("p (o t) -> p o t", o=DC)
        self.ctxT = self.area("ctxT").rearrange("p (o s) -> p o s", o=DC)
        self.ctxN = self.area("ctx").rearrange("p (t d) -> p t d", t=KT)
        small = self.area("small")
        self.stats, self.mv, self.var, self.rstd = small[:, 0:6], small[:, 6:8], small[:, 8:9], small[:, 9:10]
        self.small = small[:, 16:128]

    def area(self, name, a=0, b=None):
        s = AREA[name]
        return self.mem[:, s.start + a:(s.start + b if b is not None else s.stop)]

    def ps(self, b):
        return self.wide[:, 512 * b:512 * b + 512] if b < 4 else self.bank[b - 4][:, :]

    def sem(self, name):
        if name not in self.sems:
            self.sems[name] = self.ctx.enter_context(self.nc.semaphore(name))
        return self.sems[name]


def heads(ap, h):
    return ap.rearrange("p (h n) -> p h n", h=h)


def per_head(ap, n):
    return ap.unsqueeze(2).broadcast_to([ap.shape[0], ap.shape[1], n])


def every_head(ap, h):
    return ap.unsqueeze(1).broadcast_to([ap.shape[0], h, ap.shape[1]])


LN_EVENTS = [("ln_var", "ln_var"), ("ln_rstd", "ln_rstd"), ("ln_xn", "ln_xn"), ("ln", "4")]


class Layer:
    def __init__(self, k):
        self.k = k

    def sp(self, sp):
        pass

    def pool(self, pool):
        self.ln_pool(pool, self.p)

    def ln_dve(self, v, ph):
        k = self.k
        k.link(v.bn_stats(k.stats, k.x))
        k.link(v.bn_aggr(k.mv, k.stats))
        v.tensor_scalar(k.var, k.mv[:, 1:2], 1e-5, None, ALU.add).then_inc(ph.mark("ln_var"), 1)
        v.wait_ge(*ph.done("ln_rstd"))
        v.tensor_scalar(k.xn, k.x, k.mv[:, 0:1], k.rstd, ALU.subtract, ALU.mult).then_inc(ph.mark("ln_xn"), 1)

    def add_output(self, v, ph):
        k = self.k
        v.tensor_tensor(k.x, k.ps(7), k.x, ALU.add).then_inc(ph.drain("y"), 1)
        v.wait_ge(*ph.drained("y"))

    def ln_pool(self, pool, ph):
        k = self.k
        pool.wait_ge(*ph.done("ln_var"))
        pool.tensor_tensor(k.rstd, k.var, k.minus_half[:, 0:1], ALU.pow).then_inc(ph.mark("ln_rstd"), 1)

    def ln_pe(self, pe, ph):
        k = self.k
        pe.wait_ge(*ph.done("ln_xn"))
        pe.wait_ge(*ph.room("ln"))
        self.turn(pe, k.ps(4), k.xn, DC).then_inc(ph.fill("ln"), 1)

    def ln_act(self, act, ph):
        k = self.k
        act.wait_ge(*ph.filled("ln"))
        act.activation(k.xnT, heads(k.ps(4), DC), ACT.Copy).then_inc(ph.drain("ln"), 1)

    def turn(self, pe, out, src, n):
        for j in range(n):
            last = pe.transpose(out[:, j * P:(j + 1) * P], src[:, j * P:(j + 1) * P], self.k.ident)
        return last

    def project(self, pe, out, w, n, start=True, stop=True, src=None):
        src = self.k.xnT if src is None else src
        for o in range(DC):
            last = pe.matmul(out[:, 0:n], src[:, o, :], w[:, o, :], start=start and o == 0, stop=stop and o == DC - 1)
        return last

    def softmax_turn_pe(self, pe, ph, probs, names):
        for j, name in enumerate(names):
            pe.wait_ge(*ph.room(name))
            self.turn(pe, self.k.ps(int(ph.at[name][0])), probs[:, j * 512:(j + 1) * 512], 4).then_inc(ph.fill(name), 1)


class L0Xattn(Layer):
    TURNS = ["t0", "t1", "t2", "t3"]

    def __init__(self, k):
        super().__init__(k)
        self.y = self.p = Phase(k, [("load_pack", "load_pack0"), ("load_ctxT", "load_ctxT"), ("load_ctx", "load_ctx")] + LN_EVENTS + [
            ("q", "5"), ("qT", "4"), ("q2", "5"), ("q2T", "4"), ("s", "0"), ("shift", "shift"),
            ("t0", "4"), ("t1", "5"), ("t2", "4"), ("t3", "5"), ("y", "7")])
        pack = k.area("pack0")
        self.wq, self.wk = (pack[:, C_L0X[n]].rearrange("p (o n) -> p o n", o=DC) for n in ("wq", "wk"))
        self.bq, self.bk = pack[:, C_L0X["bq"]], pack[:, C_L0X["bk"]]
        w = k.area("work")
        self.q, self.qT, self.q2, self.q2T = w[:, 0:512], heads(w[:, 512:1024], DC), w[:, 1024:1536], heads(w[:, 1536:2048], DC)
        self.junk = w[:, 2048:2560]
        self.probs, self.probsT = w[:, 2560:4608], heads(w[:, 4608:6656], KT)
        self.c, self.m, self.b, self.sum, self.inv = (k.small[:, j:j + 1] for j in range(5))
        self.scale = float(D) ** -0.5

    def sp(self, sp):
        k = self.k
        sp.dma_start(k.area("pack0", 0, C_L0X["all"]), k.dram["l0x"]).then_inc(self.p.mark("load_pack"), 16)
        sp.dma_start(k.area("ctxT"), k.dram["ctxT"]).then_inc(self.p.mark("load_ctxT"), 16)
        sp.dma_start(k.area("ctx"), k.dram["ctx"]).then_inc(self.p.mark("load_ctx"), 16)

    def pe(self, pe):
        k, p = self.k, self.p
        self.ln_pe(pe, p)
        pe.wait_ge(*p.drained("ln"))
        pe.wait_ge(*p.loaded("load_pack"))
        pe.wait_ge(*p.room("q"))
        self.project(pe, k.ps(5), self.wq, D).then_inc(p.fill("q"), 1)
        pe.wait_ge(*p.drained("q"))
        self.turn(pe, k.ps(4), self.q, DC).then_inc(p.fill("qT"), 1)
        pe.wait_ge(*p.drained("qT"))
        self.project(pe, k.ps(5), self.wk, D, src=self.qT).then_inc(p.fill("q2"), 1)
        pe.wait_ge(*p.drained("q2"))
        self.turn(pe, k.ps(4), self.q2, DC).then_inc(p.fill("q2T"), 1)
        pe.wait_ge(*p.drained("q2T"))
        pe.wait_ge(*p.loaded("load_ctxT"))
        pe.wait_ge(*p.room("s"))
        for c in range(4):
            last = self.project(pe, k.ps(c), k.ctxT[:, :, c * 512:(c + 1) * 512], 512, src=self.q2T)
        last.then_inc(p.fill("s"), 1)
        pe.wait_ge(*p.drained("s"))
        self.softmax_turn_pe(pe, p, self.probs, self.TURNS)
        pe.wait_ge(*p.loaded("load_ctx"))
        pe.wait_ge(*p.room("y"))
        for t in range(KT):
            if t % 4 == 0:
                pe.wait_ge(*p.drained(self.TURNS[t // 4]))
            last = pe.matmul(k.ps(7), self.probsT[:, t, :], k.ctxN[:, t, :], start=t == 0, stop=t == KT - 1)
        last.then_inc(p.fill("y"), 1)

    def act(self, act):
        k, p = self.k, self.p
        self.ln_act(act, p)
        for name, out in (("qT", self.qT), ("q2T", self.q2T)):
            act.wait_ge(*p.filled(name))
            act.activation(out, heads(k.ps(4), DC), ACT.Copy).then_inc(p.drain(name), 1)
        act.wait_ge(*p.done("shift"))
        act.activation(self.probs, k.wide[:, :], ACT.Exp, bias=self.b, scale=self.scale, accum_out=self.sum).then_inc(p.drain("s"), 1)
        for j in (1, 3):
            name = self.TURNS[j]
            act.wait_ge(*p.filled(name))
            act.activation(self.probsT[:, 4 * j:4 * j + 4, :], heads(k.ps(5), 4), ACT.Copy).then_inc(p.drain(name), 1)
        if "L1x" in k.layers:
            k.layers["L1x"].act_context(act)

    def dve(self, v):
        k, p = self.k, self.p
        self.ln_dve(v, p)
        v.wait_ge(*p.loaded("load_pack"))
        v.wait_ge(*p.filled("q"))
        v.tensor_tensor(self.q, k.ps(5), self.bq, ALU.add).then_inc(p.drain("q"), 1)
        v.wait_ge(*p.drained("q"))
        k.link(v.tensor_tensor_reduce(out=self.junk, in0=self.q, in1=self.bk, scale=1.0, scalar=0.0,
                                      op0=ALU.mult, op1=ALU.add, accum_out=self.c))
        v.wait_ge(*p.filled("q2"))
        v.tensor_copy(self.q2, k.ps(5)).then_inc(p.drain("q2"), 1)
        v.wait_ge(*p.filled("s"))
        k.link(v.reduce_max(self.m, k.wide[:, :], AX_X))
        k.link(v.tensor_scalar(self.m, self.m, self.c, None, ALU.add))
        v.tensor_scalar(self.b, self.c, self.m, self.scale, ALU.subtract, ALU.mult).then_inc(p.mark("shift"), 1)
        for j in (0, 2):
            name = self.TURNS[j]
            v.wait_ge(*p.filled(name))
            v.tensor_copy(self.probsT[:, 4 * j:4 * j + 4, :], heads(k.ps(4), 4)).then_inc(p.drain(name), 1)
        v.wait_ge(*p.drained("s"))
        k.link(v.reciprocal(self.inv, self.sum))
        v.wait_ge(*p.filled("y"))
        v.scalar_tensor_tensor(out=k.x, in0=k.ps(7), scalar=self.inv, in1=k.x, op0=ALU.mult, op1=ALU.add).then_inc(p.drain("y"), 1)
        v.wait_ge(*p.drained("y"))


class L0Ffn(Layer):
    def __init__(self, k):
        super().__init__(k)
        self.y = self.p = Phase(k, [("load_pack", "load_pack1")] + LN_EVENTS + [
            ("h", "5"), ("hT", "4"), ("y", "7")])
        pack = k.area("pack1")
        self.w, self.a = (pack[:, C_L0F[n]].rearrange("p (o n) -> p o n", o=DC) for n in ("w", "a"))
        self.b, self.bias, self.coef = (pack[:, C_L0F[n]] for n in ("b", "bias", "coef"))
        w = k.area("work")
        self.h, self.hT, self.coef2 = w[:, 0:P], w[:, P:2 * P], k.small[:, 0:1]

    def sp(self, sp):
        k = self.k
        sp.dma_start(k.area("pack1", 0, C_L0F["all"]), k.dram["l0f"]).then_inc(self.p.mark("load_pack"), 16)

    def pe(self, pe):
        k, p = self.k, self.p
        self.ln_pe(pe, p)
        pe.wait_ge(*p.drained("ln"))
        pe.wait_ge(*p.loaded("load_pack"))
        pe.wait_ge(*p.room("h"))
        self.project(pe, k.ps(5), self.a, P).then_inc(p.fill("h"), 1)
        pe.wait_ge(*p.room("y"))
        self.project(pe, k.ps(7), self.w, D, stop=False)
        pe.wait_ge(*p.drained("h"))
        self.turn(pe, k.ps(4), self.h, 1).then_inc(p.fill("hT"), 1)
        pe.wait_ge(*p.drained("hT"))
        pe.matmul(k.ps(7), self.hT, self.b, start=False, stop=True).then_inc(p.fill("y"), 1)

    def act(self, act):
        k, p = self.k, self.p
        self.ln_act(act, p)
        act.wait_ge(*p.filled("h"))
        act.activation(self.h, k.ps(5)[:, 0:P], ACT.Copy).then_inc(p.drain("h"), 1)

    def dve(self, v):
        k, p = self.k, self.p
        self.ln_dve(v, p)
        v.wait_ge(*p.loaded("load_pack"))
        k.link(v.tensor_scalar(self.coef2, self.coef, 2.0, None, ALU.mult))
        v.wait_ge(*p.filled("hT"))
        v.tensor_scalar(self.hT, k.ps(4)[:, 0:P], self.coef2, None, ALU.mult).then_inc(p.drain("hT"), 1)
        k.link(v.tensor_tensor(k.x, k.x, self.bias, ALU.add))
        v.wait_ge(*p.filled("y"))
        self.add_output(v, p)


class SelfAttention(Layer):
    PROJECT = [("load_qkv", "load_qkv"), ("q", "0"), ("kv", "1"), ("v", "v_ready"), ("qT", "4"), ("kT", "5")]
    ATTEND = [("load_wo", "load_wo"), ("s", "2"), ("shift", "shift"), ("exp", "exp"), ("norm", "norm"),
              ("pT", "3"), ("oT", "6")]

    def __init__(self, k):
        super().__init__(k)
        self.first = self.p = Phase(k, [("load_rope", "load_rope")] + LN_EVENTS + self.PROJECT)
        self.body = Phase(k, self.ATTEND + [("part", "part_done")] + self.PROJECT, GROUPS - 1)
        self.y = self.last = Phase(k, self.ATTEND + [("y", "7")])
        m = k.area("weights", 0, 5120)
        self.wqkv, self.wo = m[:, 0:3072], m[:, 3072:5120].rearrange("p (h n) -> p h n", h=PER_GROUP)
        self.wq = self.wqkv[:, C_QKV["q"]].rearrange("p (o n) -> p o n", o=DC)
        self.wkv = self.wqkv[:, C_QKV["kv"]].rearrange("p (o n) -> p o n", o=DC)
        w = k.area("work")
        take = iter(range(0, 9728, 512))
        nxt = lambda: w[:, (a := next(take)):a + 512]
        self.qn, self.qT, self.tmp, self.probs, self.probsT, self.oT, kk = (nxt() for _ in range(7))
        self.tabs = k.area("pack1", 5000, 5000 + C_ROPE_Q["all"])
        self.kn, self.kT, self.v, self.tmpk = (kk[:, j * P:(j + 1) * P] for j in range(4))
        self.max, self.sum, self.inv = (k.small[:, 4 * j:4 * j + 4] for j in range(3))
        self.scale = float(P) ** -0.5

    def sp(self, sp):
        k = self.k
        sp.dma_start(self.tabs[:, 0:C_ROPE_Q["all"]], k.dram["rope_self"]).then_inc(self.first.mark("load_rope"), 16)
        src = k.dram["l0a"]

        def load(g, qkv):
            a, b = (0, 3072) if qkv else (3072, 5120)
            row = src[g] if isinstance(g, int) else src[bass.ds(g, 1), :, :].rearrange("a p n -> p (a n)")
            return sp.dma_start(self.wqkv if qkv else self.wo.rearrange("p h n -> p (h n)"), row[:, a:b])

        load(0, True).then_inc(self.first.mark("load_qkv"), 16)
        load(0, False).then_inc(self.body.mark("load_wo"), 16)
        sp.wait_ge(*self.first.filled("kv"))
        load(1, True).then_inc(self.body.mark("load_qkv"), 16)
        with sp.Fori(0, GROUPS - 2) as g:
            sp.wait_ge(*self.body.filled("kv", g))
            load(g + 2, True).then_inc(self.body.mark("load_qkv"), 16)
            sp.wait_ge(*self.body.done("part", g))
            load(g + 1, False).then_inc(self.body.mark("load_wo"), 16)
        sp.wait_ge(*self.body.done("part", GROUPS - 2))
        load(GROUPS - 1, False).then_inc(self.body.mark("load_wo"), 16)

    def pe_queries(self, pe, ph, g=0):
        k = self.k
        pe.wait_ge(*ph.loaded("load_qkv", g))
        pe.wait_ge(*ph.room("q", g))
        self.project(pe, k.ps(0), self.wq, D).then_inc(ph.fill("q"), 1)

    def pe_keys(self, pe, ph, g=0):
        k = self.k
        pe.wait_ge(*ph.room("kv", g))
        if not self.first_group(ph):
            pe.wait_ge(*ph.before("v_ready", g))
        self.project(pe, k.ps(1), self.wkv, 256).then_inc(ph.fill("kv"), 1)

    def first_group(self, ph):
        return ph is self.first

    def pe_queries_T(self, pe, ph, g=0):
        pe.wait_ge(*ph.drained("q", g))
        pe.wait_ge(*ph.room("qT", g))
        self.turn(pe, self.k.ps(4), self.qn, PER_GROUP).then_inc(ph.fill("qT"), 1)

    def pe_keys_T(self, pe, ph, g=0):
        pe.wait_ge(*ph.drained("kv", g))
        pe.wait_ge(*ph.room("kT", g))
        self.turn(pe, self.k.ps(5), self.kn, 1).then_inc(ph.fill("kT"), 1)

    def pe_scores(self, pe, ph, g=0):
        k = self.k
        pe.wait_ge(*ph.before("4", g, "drained_"))
        pe.wait_ge(*ph.before("5", g, "drained_"))
        pe.wait_ge(*ph.room("s", g))
        for h in range(PER_GROUP):
            last = pe.matmul(k.ps(2)[:, h * P:(h + 1) * P], self.qT[:, h * P:(h + 1) * P], self.kT, start=True, stop=True)
        last.then_inc(ph.fill("s"), 1)

    def pe_probs(self, pe, ph, g=0):
        pe.wait_ge(*ph.done("norm", g))
        pe.wait_ge(*ph.room("pT", g))
        self.turn(pe, self.k.ps(3), self.probs, PER_GROUP).then_inc(ph.fill("pT"), 1)

    def pe_attend(self, pe, ph, g=0):
        pe.wait_ge(*ph.drained("pT", g))
        pe.wait_ge(*ph.before("v_ready", g))
        pe.wait_ge(*ph.room("oT", g))
        pe.matmul(self.k.ps(6), self.v, self.probsT, start=True, stop=True).then_inc(ph.fill("oT"), 1)

    def pe_out(self, pe, ph, g=0, stop=False):
        pe.wait_ge(*ph.drained("oT", g))
        pe.wait_ge(*ph.loaded("load_wo", g))
        for h in range(PER_GROUP):
            if h == 2 and ph is self.body:
                self.pe_keys_T(pe, ph, g)
            last = pe.matmul(self.k.ps(7), self.oT[:, h * P:(h + 1) * P], self.wo[:, h, :], start=False,
                             stop=stop and h == PER_GROUP - 1, skip_group_check=True)
        return last

    def pe(self, pe):
        k = self.k
        self.ln_pe(pe, self.first)
        pe.wait_ge(*self.last.room("y"))
        pe.matmul(k.ps(7), k.zeros, k.xn, start=True, stop=False, skip_group_check=True)
        pe.wait_ge(*self.first.drained("ln"))
        self.pe_queries(pe, self.first)
        self.pe_keys(pe, self.first)
        self.pe_queries_T(pe, self.first)
        self.pe_keys_T(pe, self.first)
        with pe.Fori(0, GROUPS - 1) as g:
            self.pe_scores(pe, self.body, g)
            self.pe_queries(pe, self.body, g)
            self.pe_probs(pe, self.body, g)
            self.pe_attend_and_keys(pe, self.body, g)
            self.pe_queries_T(pe, self.body, g)
            self.pe_out(pe, self.body, g).then_inc(self.body.mark("part"), 1)
        self.pe_scores(pe, self.last)
        self.pe_probs(pe, self.last)
        self.pe_attend(pe, self.last)
        self.pe_out(pe, self.last, stop=True).then_inc(self.last.fill("y"), 1)

    def pe_attend_and_keys(self, pe, ph, g):
        self.pe_keys(pe, ph, g)
        self.pe_attend(pe, ph, g)

    def act_values(self, act, ph, g=0):
        act.wait_ge(*ph.drained("kv", g))
        if not self.first_group(ph):
            act.wait_ge(*ph.filled("oT", g))
        act.activation(self.v, self.k.ps(1)[:, P:2 * P], ACT.Copy).then_inc(ph.mark("v"), 1)

    def act_queries_T(self, act, ph, g=0):
        act.wait_ge(*ph.filled("qT", g))
        act.activation(self.qT, self.k.ps(4), ACT.Copy).then_inc(ph.drain("qT"), 1)

    def act_exp(self, act, ph, g=0):
        act.wait_ge(*ph.done("shift", g))
        act.activation(self.probs, self.probs, ACT.Exp).then_inc(ph.mark("exp"), 1)

    def act_probs_T(self, act, ph, g=0):
        act.wait_ge(*ph.filled("pT", g))
        act.activation(self.probsT, self.k.ps(3), ACT.Copy).then_inc(ph.drain("pT"), 1)

    def act(self, act):
        self.ln_act(act, self.first)
        self.act_values(act, self.first)
        self.act_queries_T(act, self.first)
        with act.Fori(0, GROUPS - 1) as g:
            self.act_exp(act, self.body, g)
            self.act_probs_T(act, self.body, g)
            self.act_values(act, self.body, g)
            self.act_queries_T(act, self.body, g)
        self.act_exp(act, self.last)
        self.act_probs_T(act, self.last)

    def dve_rope(self, v, src, out, tmp, n):
        k = self.k
        cos, sin, nsin = (self.tabs[:, C_ROPE_Q[c]] for c in ("cos", "sin", "nsin"))
        halves = lambda ap: ap.rearrange("p (h n) -> p h n", n=HALF)
        both = lambda ap: ap.rearrange("p (h s n) -> p h s n", s=2, n=HALF)
        v.tensor_tensor(both(tmp)[:, :, 0, :], both(src)[:, :, 1, :], every_head(nsin, n), ALU.mult)
        v.tensor_tensor(both(tmp)[:, :, 1, :], both(src)[:, :, 0, :], every_head(sin, n), ALU.mult)
        k.link(v.tensor_tensor(halves(out), halves(src), every_head(cos, 2 * n), ALU.mult))
        return v.tensor_tensor(out, out, tmp, ALU.add)

    def dve_queries(self, v, ph, g=0):
        v.wait_ge(*ph.filled("q", g))
        self.dve_rope(v, self.k.ps(0), self.qn, self.tmp, PER_GROUP).then_inc(ph.drain("q"), 1)

    def dve_keys(self, v, ph, g=0):
        v.wait_ge(*ph.filled("kv", g))
        src = self.k.ps(1)[:, 0:P]
        self.dve_rope(v, src, self.kn, self.tmpk, 1).then_inc(ph.drain("kv"), 1)
        v.wait_ge(*ph.filled("kT", g))
        v.tensor_copy(self.kT, self.k.ps(5)[:, 0:P]).then_inc(ph.drain("kT"), 1)

    def dve_softmax_shift(self, v, ph, g=0):
        k = self.k
        v.wait_ge(*ph.filled("s", g))
        v.scalar_tensor_tensor(out=heads(self.probs, PER_GROUP), in0=heads(k.ps(2), PER_GROUP), scalar=self.scale,
                               in1=every_head(k.causal, PER_GROUP), op0=ALU.mult, op1=ALU.add).then_inc(ph.drain("s"), 1)
        v.wait_ge(*ph.drained("s", g))
        k.link(v.reduce_max(self.max, heads(self.probs, PER_GROUP), AX_X))
        v.tensor_tensor(heads(self.probs, PER_GROUP), heads(self.probs, PER_GROUP), per_head(self.max, P),
                        ALU.subtract).then_inc(ph.mark("shift"), 1)

    def dve_softmax_norm(self, v, ph, g=0):
        k = self.k
        v.wait_ge(*ph.done("exp", g))
        k.link(v.reduce_sum(self.sum, heads(self.probs, PER_GROUP), AX_X))
        k.link(v.reciprocal(self.inv, self.sum))
        v.tensor_tensor(heads(self.probs, PER_GROUP), heads(self.probs, PER_GROUP), per_head(self.inv, P),
                        ALU.mult).then_inc(ph.mark("norm"), 1)

    def dve_out_T(self, v, ph, g=0):
        v.wait_ge(*ph.filled("oT", g))
        v.tensor_copy(self.oT, self.k.ps(6)).then_inc(ph.drain("oT"), 1)

    def dve(self, v):
        k = self.k
        self.ln_dve(v, self.first)
        v.wait_ge(*self.first.loaded("load_rope"))
        self.dve_queries(v, self.first)
        self.dve_keys(v, self.first)
        with v.Fori(0, GROUPS - 1) as g:
            k.chain.loop(g, 5)
            self.dve_softmax_shift(v, self.body, g)
            self.dve_softmax_norm(v, self.body, g)
            self.dve_queries(v, self.body, g)
            self.dve_out_and_keys(v, self.body, g)
        k.chain.end(GROUPS - 1)
        self.dve_softmax_shift(v, self.last)
        self.dve_softmax_norm(v, self.last)
        self.dve_out_T(v, self.last)
        v.wait_ge(*self.last.filled("y"))
        self.add_output(v, self.last)

    def dve_out_and_keys(self, v, ph, g):
        self.dve_out_T(v, ph, g)
        self.dve_keys(v, ph, g)


class L1Xattn(Layer):
    TURNS = ["t0", "t1", "t2", "t3"]
    BATCHES = KT // 4

    def __init__(self, k):
        super().__init__(k)
        keys = []
        for b in range(self.BATCHES):
            for t in range(4 * b, 4 * b + 4):
                keys += [(f"k{t}", "45"[t % 2])] + (LN_EVENTS if t == 1 else [])
            keys += [(f"ssq{b}", "k_squares"), (f"kvar{b}", "k_var"), (f"krs{b}", "k_rstd"), (f"kn{b}", "k_normed")]
            if b == 0:
                keys += [("q", "6"), ("q_var", "k_var"), ("q_rs", "k_rstd"), ("qn", "k_normed"), ("qT", "6")]
            keys += [(f"kT{b}{c}", str(c)) for c in range(DC)]
            keys += [(f"kst{t}", "k_row") for t in range(4 * b, 4 * b + 4)]
        self.y = self.p = Phase(k, [("load_pack", "load_pack0"), ("f_ssq", "ctx_squares"), ("f_var", "k_var"), ("f_rs", "k_rstd")]
                                + keys + [("wk", "wk_scaled"), ("s", "0"), ("shift", "shift"),
                                ("t0", "4"), ("t1", "5"), ("t2", "4"), ("t3", "5"), ("y", "7")])
        pack_ = k.area("pack0")
        self.wq, self.wk = (pack_[:, C_L1X[n]].rearrange("p (o n) -> p o n", o=DC) for n in ("wq", "wk"))
        self.bq, self.bk, self.fn_row, self.fn, self.qnw, self.knw = (pack_[:, C_L1X[n]] for n in ("bq", "bk", "fn_row", "fn", "qn", "kn"))
        self.keysT = k.area("work", 0, 8192).rearrange("p (o s) -> p o s", o=DC)
        self.q, self.qT = k.area("work", 8192, 8704), k.area("work", 8704, 9216)
        self.junk = k.area("work", 9216, 9728)
        stage = k.area("weights", 9216)
        self.stage = [stage[:, j * 2048:(j + 1) * 2048] for j in range(2)]
        self.probs, self.probsT = self.stage[0], heads(self.stage[1], KT)
        s = k.small
        self.rf, self.k_ssq, self.rk = (s[:, 16 * j:16 * j + 16] for j in range(3))
        self.f_ssq = s[:, 80:96]
        self.q_ssq, self.rq, self.m, self.sum, self.inv = (s[:, 64 + j:65 + j] for j in range(5))
        self.qk = s[:, 72:76]
        self.scale = float(D) ** -0.5

    def sp(self, sp):
        k = self.k
        if "L0x" in k.layers:
            sp.wait_ge(*k.layers["L0x"].y.drained("y"))
        sp.dma_start(k.area("pack0", 0, C_L1X["all"]), k.dram["l1x"]).then_inc(self.p.mark("load_pack"), 16)
        if "L0x" not in k.layers:
            load_context(sp, k)

    def pool(self, pool):
        k, p = self.k, self.p

        def power(var, out, dst, src):
            pool.wait_ge(*p.done(var))
            pool.tensor_tensor(dst, src, k.minus_half[:, 0:dst.shape[1]], ALU.pow).then_inc(p.mark(out), 1)

        power("f_var", "f_rs", self.rf, self.f_ssq)
        self.ln_pool(pool, p)
        for b in range(self.BATCHES):
            power(f"kvar{b}", f"krs{b}", self.rk[:, 4 * b:4 * b + 4], self.k_ssq[:, 4 * b:4 * b + 4])
            if b == 0:
                power("q_var", "q_rs", self.rq, self.q_ssq)

    def pe(self, pe):
        k, p = self.k, self.p
        pe.wait_ge(*p.done("wk"))
        pe.wait_ge(*context_loaded(k))
        for b in range(self.BATCHES + 1):
            if b < self.BATCHES:
                for t in range(4 * b, 4 * b + 4):
                    pe.wait_ge(*p.room(f"k{t}"))
                    self.project(pe, k.ps(4 + t % 2), self.wk, D, src=k.ctxT[:, :, t * P:(t + 1) * P]).then_inc(p.fill(f"k{t}"), 1)
                    if t == 1:
                        self.ln_pe(pe, p)
            if b == 0:
                pe.wait_ge(*p.drained("ln"))
                pe.wait_ge(*p.room("q"))
                self.project(pe, k.ps(6), self.wq, D).then_inc(p.fill("q"), 1)
            if b == 1:
                pe.wait_ge(*p.done("qn"))
                self.turn(pe, k.ps(6), self.q, DC).then_inc(p.fill("qT"), 1)
            if b >= 1:
                pe.wait_ge(*p.done(f"kn{b - 1}"))
                rows_ = self.stage[(b - 1) % 2].rearrange("p (t n) -> p t n", t=4)
                for c in range(DC):
                    pe.wait_ge(*p.room(f"kT{b - 1}{c}"))
                    for t in range(4):
                        last = pe.transpose(k.ps(c)[:, t * P:(t + 1) * P], rows_[:, t, c * P:(c + 1) * P], k.ident)
                    last.then_inc(p.fill(f"kT{b - 1}{c}"), 1)
        pe.wait_ge(*p.drained("qT"))
        for c in range(DC):
            pe.wait_ge(*p.drained(f"kT{self.BATCHES - 1}{c}"))
        qT = heads(self.qT, DC)
        for c in range(4):
            last = self.project(pe, k.ps(c), self.keysT[:, :, c * 512:(c + 1) * 512], 512, src=qT)
        last.then_inc(p.fill("s"), 1)
        pe.wait_ge(*p.drained("s"))
        self.softmax_turn_pe(pe, p, self.probs, self.TURNS)
        pe.wait_ge(*p.room("y"))
        for t in range(KT):
            if t % 4 == 0:
                pe.wait_ge(*p.drained(self.TURNS[t // 4]))
            last = pe.matmul(k.ps(7), self.probsT[:, t, :], k.ctxN[:, t, :], start=t == 0, stop=t == KT - 1)
        last.then_inc(p.fill("y"), 1)

    def act_context(self, act):
        k, p = self.k, self.p
        act.wait_ge(*context_rows_loaded(k))
        for t in range(KT):
            ins = act.activation(self.junk, k.ctxN[:, t, :], ACT.Square, accum_out=self.f_ssq[:, t:t + 1])
            if t < KT - 1:
                k.act_link(ins)
        ins.then_inc(p.mark("f_ssq"), 1)

    def act(self, act):
        k, p = self.k, self.p
        if "L0x" not in k.layers:
            self.act_context(act)
        act.wait_ge(*p.done("f_ssq"))
        for b in range(self.BATCHES + 1):
            if b < self.BATCHES:
                for t in range(4 * b, 4 * b + 4):
                    if t == 2:
                        self.ln_act(act, p)
                    act.wait_ge(*p.done(f"kst{t}"))
                    row = self.stage[b % 2][:, (t % 4) * 512:(t % 4 + 1) * 512]
                    ins = act.activation(self.junk, row, ACT.Square, accum_out=self.k_ssq[:, t:t + 1])
                    if t % 4 < 3:
                        k.act_link(ins)
                ins.then_inc(p.mark(f"ssq{b}"), 1)
                act.wait_ge(*p.done(f"ssq{b}"))
            if b >= 1:
                self.keys_out(act.activation, act, b - 1, (1, 3), ACT.Copy)
        act.wait_ge(*p.done("shift"))
        act.activation(self.probs, k.wide[:, :], ACT.Exp, bias=self.m, scale=self.scale, accum_out=self.sum).then_inc(p.drain("s"), 1)

    def keys_out(self, copy, eng, b, chunks, *func):
        for c in chunks:
            eng.wait_ge(*self.p.filled(f"kT{b}{c}"))
            copy(self.keysT[:, c, b * 512:(b + 1) * 512], self.k.ps(c), *func).then_inc(self.p.drain(f"kT{b}{c}"), 1)

    def dve(self, v):
        k, p = self.k, self.p
        v.wait_ge(*p.loaded("load_pack"))
        for o in range(DC):
            last = v.tensor_scalar(self.wk[:, o, :], self.wk[:, o, :], self.fn[:, o:o + 1], None, ALU.mult)
        last.then_inc(p.mark("wk"), 1)
        k.link(v.tensor_tensor(self.qk, self.qnw, self.knw, ALU.mult))
        v.wait_ge(*p.done("f_ssq"))
        v.tensor_scalar(self.f_ssq, self.f_ssq, 1.0 / D, 1e-6, ALU.mult, ALU.add).then_inc(p.mark("f_var"), 1)
        self.ln_dve(v, p)
        v.wait_ge(*p.done("f_rs"))
        for b in range(self.BATCHES + 1):
            if b < self.BATCHES:
                for t in range(4 * b, 4 * b + 4):
                    v.wait_ge(*p.filled(f"k{t}"))
                    row = self.stage[b % 2][:, (t % 4) * 512:(t % 4 + 1) * 512]
                    v.scalar_tensor_tensor(out=row, in0=k.ps(4 + t % 2), scalar=self.rf[:, t:t + 1], in1=self.bk,
                                           op0=ALU.mult, op1=ALU.add).then_inc(p.drain(f"k{t}"), 1)
                    v.wait_ge(*p.drained(f"k{t}"))
                    v.engine_nop().then_inc(p.mark(f"kst{t}"), 1)
                v.wait_ge(*p.done(f"ssq{b}"))
                four = slice(4 * b, 4 * b + 4)
                v.tensor_scalar(self.k_ssq[:, four], self.k_ssq[:, four], 1.0 / D, 1e-6, ALU.mult, ALU.add).then_inc(p.mark(f"kvar{b}"), 1)
                v.wait_ge(*p.done(f"krs{b}"))
                v.tensor_tensor(heads(self.stage[b % 2], 4), heads(self.stage[b % 2], 4), per_head(self.rk[:, four], 512),
                                ALU.mult).then_inc(p.mark(f"kn{b}"), 1)
            if b == 0:
                self.dve_queries(v)
            if b == 1:
                v.wait_ge(*p.filled("qT"))
                v.tensor_tensor(heads(self.qT, DC), heads(k.ps(6), DC), per_head(self.qk, P), ALU.mult).then_inc(p.drain("qT"), 1)
            if b >= 1:
                self.keys_out(v.tensor_copy, v, b - 1, (0, 2))
        v.wait_ge(*p.filled("s"))
        k.link(v.reduce_max(self.m, k.wide[:, :], AX_X))
        v.tensor_scalar(self.m, self.m, -self.scale, None, ALU.mult).then_inc(p.mark("shift"), 1)
        self.dve_output(v)

    def dve_queries(self, v):
        k, p = self.k, self.p
        v.wait_ge(*p.filled("q"))
        v.tensor_tensor(self.q, k.ps(6), self.bq, ALU.add).then_inc(p.drain("q"), 1)
        v.wait_ge(*p.drained("q"))
        k.link(v.tensor_tensor_reduce(out=self.qT, in0=self.q, in1=self.q, scale=1.0, scalar=0.0,
                                      op0=ALU.mult, op1=ALU.add, accum_out=self.q_ssq))
        v.tensor_scalar(self.q_ssq, self.q_ssq, 1.0 / D, 1e-6, ALU.mult, ALU.add).then_inc(p.mark("q_var"), 1)
        v.wait_ge(*p.done("q_rs"))
        v.tensor_scalar(self.q, self.q, self.rq, None, ALU.mult).then_inc(p.mark("qn"), 1)

    def dve_output(self, v):
        k, p = self.k, self.p
        for j, name in enumerate(self.TURNS):
            v.wait_ge(*p.filled(name))
            v.tensor_tensor(self.probsT[:, 4 * j:4 * j + 4, :], heads(k.ps(4 + j % 2), 4), per_head(self.rf[:, 4 * j:4 * j + 4], P),
                            ALU.mult).then_inc(p.drain(name), 1)
        v.wait_ge(*p.drained("s"))
        k.link(v.reciprocal(self.inv, self.sum))
        v.wait_ge(*p.filled("y"))
        k.link(v.scalar_tensor_tensor(out=self.q, in0=k.ps(7), scalar=self.inv, in1=self.fn_row, op0=ALU.mult, op1=ALU.mult))
        v.tensor_tensor(k.x, k.x, self.q, ALU.add).then_inc(p.drain("y"), 1)
        v.wait_ge(*p.drained("y"))


def load_context(sp, k, rows_too=True):
    k.context = Phase(k, [("load_ctxT", "load_ctxT"), ("load_ctx", "load_ctx")])
    sp.dma_start(k.area("ctxT"), k.dram["ctxT"]).then_inc(k.context.mark("load_ctxT"), 16)
    if rows_too:
        sp.dma_start(k.area("ctx"), k.dram["ctx"]).then_inc(k.context.mark("load_ctx"), 16)


def context_loaded(k):
    return k.sem("load_ctxT"), 16


def context_rows_loaded(k):
    return k.sem("load_ctx"), 16


XT, HG = 8, 16
CHANNELS = XT + 2
GROUP_D = XT * P
PAD = 3
C_SCAN = columns(("xbc", DC * CHANNELS * P), ("gate", DC * GROUP_D), ("out", XT * D))
C_SCAN_S = columns(("dtw", DC * P), ("conv", GROUPS * CHANNELS * 5), ("table", GROUPS * 56), ("dtb", P), ("minus_a", 1), ("mask", P))


class Scan(Layer):
    PROJECT = [("load_xbc", "load_xbc"), ("bc", "0"), ("x0", "1"), ("x1", "2"), ("load_gate", "load_gate"), ("g0", "3"), ("g1", "4"),
               ("tg0", "gate_tanh"), ("tg1", "gate_tanh"), ("conv", "conv"), ("th", "conv_tanh"), ("sx", "channels")]
    MIX = [("load_cs", "load_cs"), ("cs_g", "group_cs"), ("rel", "relative_cs"), ("diff", "decay_diff"), ("decay", "decay"), ("xs0", "5"), ("xs1", "6"), ("s", "4"),
           ("mix", "mix"), ("y0", "5"), ("y1", "6"), ("yg", "gated"), ("ssq", "gated_squares"),
           ("yvar", "gated_var"), ("yrs", "gated_rstd"), ("yn", "normed")]
    OUT = [("yT0", "0"), ("yT1", "1"), ("load_out", "load_out")]

    def __init__(self, k):
        super().__init__(k)
        self.first = self.p = Phase(k, [("load_small", "load_pack1"), ("pad", "conv_pad")] + LN_EVENTS + [("dt", "5"), ("later", "later_mask"), ("absdt", "abs_dt"), ("expdt", "exp_dt"),
                                    ("lndt", "ln_dt"), ("dtn", "dt_ready"), ("dtT", "4"), ("csT", "csT_ready"), ("store_cs", "store_cs"), ("cs", "4")] + self.PROJECT)
        self.body = Phase(k, self.MIX + self.PROJECT + self.OUT + [("part", "scan_part")], GROUPS - 1)
        self.last = Phase(k, self.MIX + self.OUT + [("y", "7")])
        self.y = self.last
        w = k.area("weights")
        self.wx = w[:, C_SCAN["xbc"]].rearrange("p (o n) -> p o n", o=DC)
        self.wg = w[:, C_SCAN["gate"]].rearrange("p (o n) -> p o n", o=DC)
        self.wout = w[:, C_SCAN["out"]].rearrange("p (t n) -> p t n", t=XT)
        small = k.area("pack1")
        self.dtw, self.convw, self.table, self.dtb, self.minus_a, self.mask = (
            small[:, C_SCAN_S[n]] for n in ("dtw", "conv", "table", "dtb", "minus_a", "mask"))
        self.dtw = self.dtw.rearrange("p (o n) -> p o n", o=DC)
        self.tab = self.table.rearrange("p (g n) -> p g n", g=GROUPS)
        c = k.area("ctx")
        self.decay, self.mixer = c[:, 0:2048], c[:, 2048:4096]
        self.xc = c[:, 4096:4096 + CHANNELS * (P + PAD)].rearrange("p (t n) -> p t n", t=CHANNELS)
        self.conv = c[:, 5440:5440 + CHANNELS * P].rearrange("p (t n) -> p t n", t=CHANNELS)
        self.tanh = c[:, 6720:6720 + CHANNELS * P].rearrange("p (t n) -> p t n", t=CHANNELS)
        a = k.area("work")
        self.sx = a[:, 0:1280].rearrange("p (t n) -> p t n", t=CHANNELS)
        self.xdt, self.xd, self.tg, self.gate, self.yv, self.yT = (a[:, 1280 + 1024 * j:1280 + 1024 * (j + 1)] for j in range(6))
        rest = a[:, 7424:9728]
        self.masked, self.dtv, self.dta, self.dte, self.dt, self.da, self.csT, self.ones = (rest[:, P * j:P * (j + 1)] for j in range(8))
        self.table_g = rest[:, 1024:1024 + 56]
        self.normw, self.cs_g, self.dt_g, self.d_g = self.table_g[:, 0:8], self.table_g[:, 8:24], self.table_g[:, 24:40], self.table_g[:, 40:56]
        self.conv_g = rest[:, 1088:1088 + 50]
        self.ssq, self.rs = k.small[:, 0:1], k.small[:, 1:2]
        self.decay_cs = k.small[:, 16:32]
        self.later = c[:, 8000:8000 + P]
        self.squares = self.mixer[:, 0:GROUP_D]

    def load(self, sp, part, g):
        k = self.k
        src = k.dram["l1a"]
        row = src[g] if isinstance(g, int) else src[bass.ds(g, 1), :, :].rearrange("a p n -> p (a n)")
        return sp.dma_start(k.area("weights")[:, C_SCAN[part]], row[:, C_SCAN[part]])

    def load_cs(self, sp, g):
        rows_ = self.k.dram["cs"]
        row = rows_[g] if isinstance(g, int) else rows_[bass.ds(g, 1), :].rearrange("a n -> (a n)")
        return sp.dma_start(self.decay, row.partition_broadcast(P))

    def sp(self, sp):
        k, b = self.k, self.body
        for name, event, kind in (("L0f", "y", "drained"), ("L0a", "y", "drained")):
            if name in k.layers:
                sp.wait_ge(*k.layers[name].y.drained("y"))
        sp.dma_start(k.area("pack1", 0, C_SCAN_S["all"]), k.dram["l1a_small"]).then_inc(self.first.mark("load_small"), 16)
        self.load(sp, "xbc", 0).then_inc(self.first.mark("load_xbc"), 16)
        self.load(sp, "gate", 0).then_inc(self.first.mark("load_gate"), 16)
        if "L1x" in k.layers:
            sp.wait_ge(*k.layers["L1x"].y.filled("y"))
        self.load(sp, "out", 0).then_inc(b.mark("load_out"), 16)
        sp.wait_ge(*self.first.done("csT"))
        sp.dma_start(k.dram["cs"].rearrange("g (h l) -> (g h) l", h=HG), self.csT).then_inc(self.first.mark("store_cs"), 16)
        sp.wait_ge(*self.first.loaded("store_cs"))
        self.load_cs(sp, 0).then_inc(b.mark("load_cs"), 16)
        sp.wait_ge(*b.before("2", 0, "filled_"))
        self.load(sp, "xbc", 1).then_inc(b.mark("load_xbc"), 16)
        sp.wait_ge(*b.before("4", 0, "filled_"))
        self.load(sp, "gate", 1).then_inc(b.mark("load_gate"), 16)

        def iteration(g, more):
            sp.wait_ge(*b.done("mix", g))
            self.load_cs(sp, g + 1).then_inc(b.mark("load_cs"), 16)
            if more:
                sp.wait_ge(*b.filled("x1", g))
                self.load(sp, "xbc", g + 2).then_inc(b.mark("load_xbc"), 16)
            if more:
                sp.wait_ge(*b.filled("g1", g))
                self.load(sp, "gate", g + 2).then_inc(b.mark("load_gate"), 16)
            sp.wait_ge(*b.done("part", g))
            self.load(sp, "out", g + 1).then_inc(b.mark("load_out"), 16)

        with sp.Fori(0, GROUPS - 2) as g:
            iteration(g, True)
        iteration(GROUPS - 2, False)

    def pool(self, pool):
        k = self.k
        self.ln_pool(pool, self.first)

        def rstd(ph, g=0):
            pool.wait_ge(*ph.done("yvar", g))
            pool.tensor_tensor(self.rs, self.ssq, k.minus_half[:, 0:1], ALU.pow).then_inc(ph.mark("yrs"), 1)

        pool.wait_ge(*self.first.drained("cs"))
        pool.wait_ge(*self.first.done("later"))
        self.pool_relative(pool, self.body, 0, 0)
        self.pool_mask(pool, self.body, 0)
        with pool.Fori(0, GROUPS - 1) as g:
            self.pool_relative(pool, self.body, g + 1, g + 1)
            rstd(self.body, g)
            self.pool_mask(pool, self.body, g + 1)
        rstd(self.last)

    def pool_relative(self, pool, ph, g, group):
        pool.wait_ge(*ph.loaded("load_cs", g))
        src = self.table[:, 8:24] if isinstance(group, int) else self.table[:, bass.ds(group * 56 + 8, 16)]
        pool.tensor_copy(self.decay_cs, src).then_inc(ph.mark("cs_g"), 1)
        pool.wait_ge(*ph.done("cs_g", g))
        decay = heads(self.decay, HG)
        pool.tensor_tensor(decay, decay, per_head(self.decay_cs, P), ALU.subtract).then_inc(ph.mark("rel"), 1)

    def pool_mask(self, pool, ph, g):
        decay = heads(self.decay, HG)
        pool.wait_ge(*ph.done("rel", g))
        pool.tensor_tensor(decay, decay, every_head(self.later, HG), ALU.add).then_inc(ph.mark("diff"), 1)

    def pe_channels(self, pe, ph, g=0):
        k = self.k
        pe.wait_ge(*ph.loaded("load_xbc", g))
        for name, tiles_ in (("bc", range(XT, XT + 2)), ("x0", range(0, 4)), ("x1", range(4, 8))):
            pe.wait_ge(*ph.room(name, g))
            out = k.ps(int(ph.at[name][0]))
            for j, t in enumerate(tiles_):
                for o in range(DC):
                    last = pe.matmul(out[:, j * P:(j + 1) * P], self.wx[:, o, t * P:(t + 1) * P], k.xnT[:, o, :], start=o == 0, stop=o == DC - 1)
            last.then_inc(ph.fill(name), 1)

    def pe_gate(self, pe, ph, g=0):
        k = self.k
        pe.wait_ge(*ph.loaded("load_gate", g))
        for j, name in enumerate(("g0", "g1")):
            pe.wait_ge(*ph.room(name, g))
            self.project(pe, k.ps(int(ph.at[name][0])), self.wg[:, :, j * 512:(j + 1) * 512], 512).then_inc(ph.fill(name), 1)

    def pe_rows(self, pe, ph, g=0):
        k = self.k
        pe.wait_ge(*ph.before("channels", g))
        for j, name in enumerate(("xs0", "xs1")):
            pe.wait_ge(*ph.room(name, g))
            for t in range(4):
                last = pe.transpose(k.ps(5 + j)[:, t * P:(t + 1) * P], self.sx[:, 4 * j + t, :], k.ident)
            last.then_inc(ph.fill(name), 1)

    def pe_cb(self, pe, ph, g=0):
        k = self.k
        pe.wait_ge(*ph.room("s", g))
        pe.matmul(k.ps(4)[:, 0:P], self.sx[:, XT, :], self.sx[:, XT + 1, :], start=True, stop=True).then_inc(ph.fill("s"), 1)

    def pe_mix(self, pe, ph, g=0):
        k = self.k
        pe.wait_ge(*ph.done("mix", g))
        for j, name in enumerate(("y0", "y1")):
            pe.wait_ge(*ph.room(name, g))
            for h in range(8 * j, 8 * j + 8):
                last = pe.matmul(k.ps(5 + j)[:, (h % 8) * 64:(h % 8 + 1) * 64], self.mixer[:, h * P:(h + 1) * P],
                                 self.xdt[:, h * 64:(h + 1) * 64], start=True, stop=True)
            last.then_inc(ph.fill(name), 1)

    def pe_turn(self, pe, ph, g=0):
        k = self.k
        pe.wait_ge(*ph.done("yn", g))
        for j, name in enumerate(("yT0", "yT1")):
            pe.wait_ge(*ph.room(name, g))
            self.turn(pe, k.ps(j), self.yv[:, 512 * j:512 * j + 512], 4).then_inc(ph.fill(name), 1)

    def pe_out(self, pe, ph, g=0, stop=False):
        k = self.k
        pe.wait_ge(*ph.loaded("load_out", g))
        for t in range(XT):
            if t == 4 and ph is self.body:
                self.pe_rows(pe, ph, g + 1)
            if t % 4 == 0:
                pe.wait_ge(*ph.drained(f"yT{t // 4}", g))
            last = pe.matmul(k.ps(7), self.yT[:, t * P:(t + 1) * P], self.wout[:, t, :], start=False, stop=stop and t == XT - 1, skip_group_check=True)
        return last

    def pe(self, pe):
        k, f = self.k, self.first
        self.ln_pe(pe, f)
        pe.wait_ge(*self.last.room("y"))
        pe.matmul(k.ps(7), k.zeros, k.xn, start=True, stop=False, skip_group_check=True)
        pe.wait_ge(*f.drained("ln"))
        pe.wait_ge(*f.loaded("load_small"))
        pe.wait_ge(*f.room("dt"))
        self.project(pe, k.ps(5), self.dtw, P).then_inc(f.fill("dt"), 1)
        self.pe_channels(pe, f)
        pe.wait_ge(*f.done("dtn"))
        self.turn(pe, k.ps(4), self.dt, 1).then_inc(f.fill("dtT"), 1)
        pe.wait_ge(*f.done("csT"))
        self.turn(pe, k.ps(4), self.csT, 1).then_inc(f.fill("cs"), 1)
        self.pe_gate(pe, f)
        self.pe_rows(pe, self.body, 0)
        with pe.Fori(0, GROUPS - 1) as g:
            self.pe_cb(pe, self.body, g)
            self.pe_channels(pe, self.body, g)
            self.pe_mix(pe, self.body, g)
            self.pe_gate(pe, self.body, g)
            self.pe_turn(pe, self.body, g)
            self.pe_out(pe, self.body, g).then_inc(self.body.mark("part"), 1)
        self.pe_cb(pe, self.last)
        self.pe_mix(pe, self.last)
        self.pe_turn(pe, self.last)
        self.pe_out(pe, self.last, stop=True).then_inc(self.last.fill("y"), 1)

    def act_channels(self, act, ph, g=0):
        k = self.k
        if ph is not self.first:
            act.wait_ge(*ph.before("conv", g))
        for name, a, b in (("bc", XT, XT + 2), ("x0", 0, 4), ("x1", 4, 8)):
            act.wait_ge(*ph.filled(name, g))
            src = k.ps(int(ph.at[name][0]))[:, 0:(b - a) * P]
            act.activation(self.xc[:, a:b, PAD:PAD + P], heads(src, b - a), ACT.Copy).then_inc(ph.drain(name), 1)

    def act_tanh(self, act, ph, g=0):
        act.wait_ge(*ph.done("conv", g))
        act.activation(self.tanh, self.conv, ACT.Tanh, scale=0.5).then_inc(ph.mark("th"), 1)

    def act_gate(self, act, ph, g=0):
        for j, name in enumerate(("g0", "g1")):
            act.wait_ge(*ph.filled(name, g))
            if ph is not self.first:
                act.wait_ge(*ph.before(str(3 + j), g, "drained_"))
            act.activation(self.tg[:, 512 * j:512 * j + 512], self.k.ps(3 + j), ACT.Tanh, scale=0.5).then_inc(ph.mark(f"tg{j}"), 1)

    def act_decay(self, act, ph, g=0):
        act.wait_ge(*ph.done("diff", g))
        act.activation(self.decay, self.decay, ACT.Exp).then_inc(ph.mark("decay"), 1)

    def act_square(self, act, ph, g=0):
        act.wait_ge(*ph.done("yg", g))
        act.activation(self.squares, self.yv, ACT.Square, accum_out=self.ssq).then_inc(ph.mark("ssq"), 1)

    def act(self, act):
        f = self.first
        self.ln_act(act, f)
        act.wait_ge(*f.done("pad"))
        self.act_channels(act, f)
        act.wait_ge(*f.done("absdt"))
        act.activation(self.dte, self.dta, ACT.Exp, scale=-1.0).then_inc(f.mark("expdt"), 1)
        act.wait_ge(*f.done("expdt"))
        act.activation(self.dte, self.dte, ACT.Ln, bias=1.0).then_inc(f.mark("lndt"), 1)
        self.act_tanh(act, f)
        self.act_gate(act, f)
        self.act_decay(act, self.body, 0)
        with act.Fori(0, GROUPS - 1) as g:
            self.act_channels(act, self.body, g)
            self.act_square(act, self.body, g)
            self.act_tanh(act, self.body, g)
            self.act_gate(act, self.body, g)
            self.act_decay(act, self.body, g + 1)
        self.act_square(act, self.last)

    def dve_taps(self, v, ph, name, g=0, between=None):
        k = self.k
        tiles_ = {"bc": range(XT, XT + 2), "x0": range(0, 4), "x1": range(4, 8)}[name]
        w = lambda t, j: self.conv_g[:, 5 * t + j:5 * t + j + 1]
        v.wait_ge(*ph.drained(name, g))
        for j in range(4):
            if between and j in between:
                between[j]()
            for t in tiles_:
                src, out = self.xc[:, t, PAD - j:PAD - j + P], self.conv[:, t, :]
                if j == 0:
                    last = v.tensor_scalar(out, src, w(t, 3), w(t, 4), ALU.mult, ALU.add)
                else:
                    last = v.scalar_tensor_tensor(out=out, in0=src, scalar=w(t, 3 - j), in1=out, op0=ALU.mult, op1=ALU.add)
            if j < 3:
                k.link(last)
        return last

    def dve_conv_first(self, v, ph, g=0, group=0):
        n = CHANNELS * 5
        self.k.link(v.tensor_copy(self.conv_g, self.convw[:, bass.ds(group * n, n)] if ph is not self.first else self.convw[:, 0:n]))
        self.dve_taps(v, ph, "bc", g)
        self.dve_taps(v, ph, "x0", g)

    def dve_conv_last(self, v, ph, g=0, between=None):
        self.dve_taps(v, ph, "x1", g, between).then_inc(ph.mark("conv"), 1)

    def dve_silu(self, v, ph, g=0):
        v.wait_ge(*ph.done("th", g))
        v.wait_ge(*ph.done("conv", g))
        flat = lambda ap: ap.rearrange("p t n -> p (t n)")
        v.scalar_tensor_tensor(out=flat(self.sx), in0=flat(self.tanh), scalar=1.0, in1=flat(self.conv), op0=ALU.add,
                               op1=ALU.mult).then_inc(ph.mark("sx"), 1)

    def dve_gate(self, v, ph, g=0):
        for j, name in enumerate(("g0", "g1")):
            v.wait_ge(*ph.done(f"tg{j}", g))
            s = slice(512 * j, 512 * j + 512)
            v.scalar_tensor_tensor(out=self.gate[:, s], in0=self.tg[:, s], scalar=1.0, in1=self.k.ps(3 + j), op0=ALU.add,
                                   op1=ALU.mult).then_inc(ph.drain(name), 1)

    def dve_table(self, v, ph, g=0, group=0):
        n = 56
        src = self.table[:, (GROUPS - 1) * n:] if isinstance(group, int) else self.table[:, bass.ds(group * n, n)]
        v.wait_ge(*ph.before("4", g, "drained_"))
        self.k.link(v.tensor_copy(self.table_g, src))

    def dve_rows(self, v, ph, g=0):
        k = self.k
        for j, name in enumerate(("xs0", "xs1")):
            v.wait_ge(*ph.filled(name, g))
            s = slice(512 * j, 512 * j + 512)
            h = slice(8 * j, 8 * j + 8)
            v.tensor_tensor(heads(self.xdt[:, s], 8), heads(k.ps(5 + j), 8), per_head(self.dt_g[:, h], 64), ALU.mult)
            v.tensor_tensor(heads(self.xd[:, s], 8), heads(k.ps(5 + j), 8), per_head(self.d_g[:, h], 64), ALU.mult).then_inc(ph.drain(name), 1)
        v.wait_ge(*ph.filled("s", g))
        v.scalar_tensor_tensor(out=self.masked, in0=k.ps(4)[:, 0:P], scalar=0.25, in1=self.mask, op0=ALU.mult, op1=ALU.mult).then_inc(ph.drain("s"), 1)
        v.wait_ge(*ph.drained("s", g))
        v.wait_ge(*ph.done("decay", g))
        v.tensor_tensor(heads(self.mixer, HG), heads(self.decay, HG), every_head(self.masked, HG), ALU.mult).then_inc(ph.mark("mix"), 1)

    def dve_gated(self, v, ph, g=0):
        k = self.k
        v.wait_ge(*ph.before("channels", g))
        for j, name in enumerate(("y0", "y1")):
            v.wait_ge(*ph.filled(name, g))
            s = slice(512 * j, 512 * j + 512)
            last = v.tensor_tensor(self.yv[:, s], k.ps(5 + j), self.xd[:, s], ALU.add)
            last.then_inc(ph.drain(name), 1)
        v.wait_ge(*ph.drained("y1", g))
        v.wait_ge(*ph.drained("y0", g))
        v.tensor_tensor(self.yv, self.yv, self.gate, ALU.mult).then_inc(ph.mark("yg"), 1)

    def dve_norm_var(self, v, ph, g=0):
        v.wait_ge(*ph.done("ssq", g))
        v.tensor_scalar(self.ssq, self.ssq, 0.25 / GROUP_D, 1e-5, ALU.mult, ALU.add).then_inc(ph.mark("yvar"), 1)

    def dve_norm(self, v, ph, g=0):
        v.wait_ge(*ph.done("yrs", g))
        v.tensor_scalar(self.yv, self.yv, self.rs, 0.5, ALU.mult, ALU.mult).then_inc(ph.mark("yn"), 1)

    def dve_out_T(self, v, ph, g=0):
        for j, name in enumerate(("yT0", "yT1")):
            v.wait_ge(*ph.filled(name, g))
            v.tensor_tensor(heads(self.yT[:, 512 * j:512 * j + 512], 4), heads(self.k.ps(j), 4), per_head(self.normw[:, 4 * j:4 * j + 4], P),
                            ALU.mult).then_inc(ph.drain(name), 1)

    def dve(self, v):
        k, f = self.k, self.first
        self.ln_dve(v, f)
        v.memset(self.xc[:, :, 0:PAD], 0.0).then_inc(f.mark("pad"), 1)
        v.memset(self.ones, 1.0)
        v.wait_ge(*f.loaded("load_small"))
        v.tensor_scalar(self.later, self.mask, -1.0, -NEG, ALU.add, ALU.mult).then_inc(f.mark("later"), 1)
        v.wait_ge(*f.filled("dt"))
        v.tensor_tensor(self.dtv, k.ps(5)[:, 0:P], self.dtb, ALU.add).then_inc(f.drain("dt"), 1)
        v.wait_ge(*f.drained("dt"))
        k.link(v.tensor_scalar(self.dta, self.dtv, -1.0, None, ALU.mult))
        v.tensor_tensor(self.dta, self.dta, self.dtv, ALU.max).then_inc(f.mark("absdt"), 1)
        k.link(v.tensor_scalar(self.dtv, self.dtv, 0.0, None, ALU.max))
        v.wait_ge(*f.done("lndt"))
        k.link(v.tensor_tensor(self.dt, self.dtv, self.dte, ALU.add))
        v.tensor_scalar(self.dt, self.dt, 0.001, 100.0, ALU.max, ALU.min).then_inc(f.mark("dtn"), 1)
        v.wait_ge(*f.done("dtn"))
        half = lambda part: self.tab[:, :, part]
        v.tensor_scalar(half(slice(24, 40)), self.dt.rearrange("p (g n) -> p g n", g=GROUPS), 0.5, None, ALU.mult)
        v.tensor_scalar(half(slice(40, 56)), half(slice(40, 56)), 0.5, None, ALU.mult)
        v.wait_ge(*f.filled("dtT"))
        v.tensor_scalar(self.da, k.ps(4)[:, 0:P], self.minus_a, None, ALU.mult).then_inc(f.drain("dtT"), 1)
        v.wait_ge(*f.drained("dtT"))
        v.tensor_tensor_scan(self.csT, self.ones, self.da, 0.0, ALU.mult, ALU.add).then_inc(f.mark("csT"), 1)
        v.wait_ge(*f.filled("cs"))
        v.tensor_copy(half(slice(8, 24)), heads(k.ps(4)[:, 0:P], GROUPS)).then_inc(f.drain("cs"), 1)
        v.wait_ge(*f.drained("cs"))
        self.dve_conv_first(v, f)
        self.dve_conv_last(v, f)
        self.dve_silu(v, f)
        self.dve_gate(v, f)
        with v.Fori(0, GROUPS - 1) as g:
            k.chain.loop(g, 11)
            self.dve_table(v, self.body, g, g)
            self.dve_rows(v, self.body, g)
            self.dve_conv_first(v, self.body, g, g + 1)
            self.dve_gated(v, self.body, g)
            self.dve_conv_last(v, self.body, g, {2: lambda: self.dve_norm_var(v, self.body, g), 3: lambda: self.dve_norm(v, self.body, g)})
            self.dve_out_T(v, self.body, g)
            self.dve_silu(v, self.body, g)
            self.dve_gate(v, self.body, g)
        k.chain.end(GROUPS - 1)
        self.dve_table(v, self.last)
        self.dve_rows(v, self.last)
        self.dve_gated(v, self.last)
        self.dve_norm_var(v, self.last)
        self.dve_norm(v, self.last)
        self.dve_out_T(v, self.last)
        v.wait_ge(*self.last.filled("y"))
        self.add_output(v, self.last)


class L1Ffn(Layer):
    def __init__(self, k):
        super().__init__(k)
        self.y = self.p = Phase(k, [("load_pack", "load_pack0")] + LN_EVENTS + [
            ("g", "6"), ("h", "5"), ("shift", "shift"), ("thr", "threshold_exp"), ("exp", "exp"), ("hw", "hidden"), ("hT", "4"), ("y", "7")])
        pack_ = k.area("pack0")
        self.w, self.a, self.wg = (pack_[:, C_L1F[n]].rearrange("p (o n) -> p o n", o=DC) for n in ("w", "a", "gate"))
        self.b, self.bias, self.bthr = (pack_[:, C_L1F[n]] for n in ("b", "bias", "bthr"))
        w = k.area("work")
        self.h, self.hT = w[:, 0:P], w[:, P:2 * P]
        s = k.small
        self.g, self.e, self.w8, self.t8 = s[:, 0:9], s[:, 16:24], s[:, 24:32], s[:, 32:40]
        self.m, self.sum, self.inv, self.te, self.th, self.ws = (s[:, 48 + j:49 + j] for j in range(6))

    def sp(self, sp):
        k = self.k
        if "L1x" in k.layers:
            sp.wait_ge(*k.layers["L1x"].y.drained("y"))
        sp.dma_start(k.area("pack0", 0, C_L1F["all"]), k.dram["l1f"]).then_inc(self.p.mark("load_pack"), 16)

    def pe(self, pe):
        k, p = self.k, self.p
        self.ln_pe(pe, p)
        pe.wait_ge(*p.drained("ln"))
        pe.wait_ge(*p.loaded("load_pack"))
        pe.wait_ge(*p.room("g"))
        self.project(pe, k.ps(6), self.wg, E8 + 1).then_inc(p.fill("g"), 1)
        pe.wait_ge(*p.room("h"))
        self.project(pe, k.ps(5), self.a, P).then_inc(p.fill("h"), 1)
        pe.wait_ge(*p.room("y"))
        self.project(pe, k.ps(7), self.w, D, stop=False)
        pe.wait_ge(*p.drained("h"))
        self.turn(pe, k.ps(4), self.h, 1).then_inc(p.fill("hT"), 1)
        pe.wait_ge(*p.drained("hT"))
        pe.matmul(k.ps(7), self.hT, self.b, start=False, stop=True).then_inc(p.fill("y"), 1)

    def act(self, act):
        k, p = self.k, self.p
        self.ln_act(act, p)
        act.wait_ge(*p.done("shift"))
        act.activation(self.te, self.g[:, 8:9], ACT.Exp, scale=-1.0)
        act.activation(self.e, self.e, ACT.Exp, accum_out=self.sum).then_inc(p.mark("exp"), 1)
        act.wait_ge(*p.filled("hT"))
        act.activation(self.hT, k.ps(4)[:, 0:P], ACT.Copy).then_inc(p.drain("hT"), 1)

    def dve(self, v):
        k, p = self.k, self.p
        self.ln_dve(v, p)
        v.wait_ge(*p.loaded("load_pack"))
        v.wait_ge(*p.filled("g"))
        v.tensor_copy(self.g, k.ps(6)[:, 0:9]).then_inc(p.drain("g"), 1)
        v.wait_ge(*p.drained("g"))
        v.tensor_scalar(self.g[:, 8:9], self.g[:, 8:9], self.bthr, None, ALU.add)
        k.link(v.reduce_max(self.m, self.g[:, 0:8], AX_X))
        v.tensor_scalar(self.e, self.g[:, 0:8], self.m, None, ALU.subtract).then_inc(p.mark("shift"), 1)
        v.wait_ge(*p.done("exp"))
        k.link(v.tensor_scalar(self.te, self.te, 1.0, None, ALU.add))
        k.link(v.reciprocal(self.th, self.te))
        k.link(v.reciprocal(self.inv, self.sum))
        k.link(v.tensor_scalar(self.th, self.th, 0.125, None, ALU.mult))
        k.link(v.tensor_scalar(self.w8, self.e, self.inv, self.th, ALU.mult, ALU.subtract))
        k.link(v.tensor_scalar(self.w8, self.w8, 0.0, None, ALU.max))
        k.link(v.reduce_sum(self.ws, self.w8, AX_X))
        k.link(v.tensor_scalar(self.m, self.ws, 0.0, None, ALU.is_equal))
        k.link(v.tensor_tensor(self.ws, self.ws, self.m, ALU.add))
        k.link(v.reciprocal(self.inv, self.ws))
        k.link(v.tensor_scalar(self.w8, self.w8, self.inv, 2.0, ALU.mult, ALU.mult))
        v.wait_ge(*p.filled("h"))
        v.tensor_tensor(heads(self.h, E8), heads(k.ps(5)[:, 0:P], E8), per_head(self.w8, 16), ALU.mult).then_inc(p.drain("h"), 1)
        k.link(v.tensor_tensor(k.x, k.x, self.bias, ALU.add))
        v.wait_ge(*p.filled("y"))
        self.add_output(v, p)


C_ROPE_K = columns(("cos", KT * HALF), ("sin", KT * HALF))


class CrossAttention(Layer):
    BLOCKS = range(KT // 4)

    def __init__(self, k, source, rope):
        super().__init__(k)
        self.source, self.rope = source, rope
        scores = [("load_v", "load_v")]
        for b in self.BLOCKS:
            scores += [(f"s{t}", str(t % 4)) for t in range(4 * b, 4 * b + 4)] + [(f"v{b}", "45"[b % 2])]
        scores += [("max", "key_max"), ("mT", "6"), ("mB", "6")]
        scores += [(f"shift{b}", "shift_pool" if self.by_pool(b) else "shift") for b in self.BLOCKS]
        scores += [(f"exp{b}", "exp") for b in self.BLOCKS]
        project = [("load_q", "load_q"), ("q", "4"), ("load_k", "load_k")] + [(f"k{b}", str(b)) for b in self.BLOCKS]
        if not rope:
            project += [("q_sq", "q_squares"), ("q_var", "q_var"), ("q_rs", "q_rstd")]
            for b in self.BLOCKS:
                project += [(f"k_sq{b}", "k_squares"), (f"k_var{b}", "k_var"), (f"k_rs{b}", "k_rstd")]
        project += [(f"kT{b}", "54"[b % 2]) for b in self.BLOCKS] + [("qT", "6")]
        attend = [("o0", "2"), ("o1", "3"), ("oT", "6"), ("load_wo", "load_wo")]
        self.first = self.p = Phase(k, [("load_mask", "load_mask"), ("load_tab", "load_rope"), ("ones", "ones_column")] + LN_EVENTS + project)
        self.body = Phase(k, scores + project + attend + [("part", "part_done")], GROUPS - 1)
        self.last = self.y = Phase(k, scores + attend + [("y", "7")])
        w = k.area("weights", 0, 5120)
        self.wq = w[:, 0:2048].rearrange("p (o n) -> p o n", o=DC)
        wkv = w[:, 2048:3072].rearrange("p (o n) -> p o n", o=DC)
        self.wk, self.wv = wkv[:, :, 0:P], wkv[:, :, P:2 * P]
        self.wo = w[:, 3072:5120].rearrange("p (h n) -> p h n", h=PER_GROUP)
        self.probsT, a, b = k.area("ctx"), k.area("work"), k.area("pack0")
        self.keysT, self.mask, self.tab, self.keys = (a[:, 2048 * j:2048 * j + 2048] for j in range(4))
        self.qn, self.qT, self.tmp = a[:, 8192:8704], a[:, 8704:9216], a[:, 9216:9728]
        e = k.area("weights", 5120, 5120 + 5648) if rope else k.area("pack1", 0, 5648)
        self.values = e[:, 0:KT * (P + 1)].rearrange("p (t n) -> p t n", t=KT)
        self.most, self.mrow, self.tmpk, self.on = e[:, 2064:4112], e[:, 4112:4624], e[:, 4624:5136], e[:, 5136:5648]
        self.oT = b[:, 4096:4608]
        self.qw, self.kw = self.tab[:, 0:1], self.tab[:, 1:2]
        s = k.small
        self.inv, self.q_ssq, self.rq, self.m = (s[:, 4 * j:4 * j + 4] for j in range(4))
        self.k_ssq, self.rk = s[:, 16:32], s[:, 32:48]
        self.scale = float(P) ** -0.5

    def by_pool(self, b):
        return b in (1, 2) if self.rope else b == 2

    def load(self, sp, part, g):
        src = self.k.dram[self.source]
        row = src[g] if isinstance(g, int) else src[bass.ds(g, 1), :, :].rearrange("a p n -> p (a n)")
        if part in ("k", "v"):
            kv = row[:, 2048:3072].rearrange("p (o n) -> p o n", o=DC)
            return sp.dma_start(self.wk if part == "k" else self.wv, kv[:, :, 0:P] if part == "k" else kv[:, :, P:2 * P])
        a, b = {"q": (0, 2048), "wo": (3072, 5120)}[part]
        return sp.dma_start(self.k.area("weights", a, b), row[:, a:b])

    def sp(self, sp):
        k, f, b = self.k, self.first, self.body
        for name in (("L1x", "L1a", "L1f") if self.rope else ("L2x", "L2a", "L2f")):
            if name in k.layers:
                sp.wait_ge(*k.layers[name].y.drained("y"))
        if "L0x" not in k.layers and (self.rope or "L2x" not in k.layers):
            load_context(sp, k, False)
        self.load(sp, "k", 0).then_inc(f.mark("load_k"), 16)
        self.load(sp, "q", 0).then_inc(f.mark("load_q"), 16)
        tab = self.tab if self.rope else self.tab[:, 0:2]
        sp.dma_start(tab, k.dram["rope_keys" if self.rope else "l3x_norm"]).then_inc(f.mark("load_tab"), 16)
        self.load(sp, "v", 0).then_inc(b.mark("load_v"), 16)
        sp.dma_start(self.mask, k.dram["mask2" if self.rope else "mask3"]).then_inc(f.mark("load_mask"), 16)
        self.load(sp, "wo", 0).then_inc(b.mark("load_wo"), 16)
        sp.wait_ge(*f.filled("q"))
        self.load(sp, "q", 1).then_inc(b.mark("load_q"), 16)
        sp.wait_ge(*f.filled("k3"))
        self.load(sp, "k", 1).then_inc(b.mark("load_k"), 16)

        def iteration(g, more):
            sp.wait_ge(*b.filled("v3", g))
            self.load(sp, "v", g + 1).then_inc(b.mark("load_v"), 16)
            if more:
                sp.wait_ge(*b.filled("q", g))
                self.load(sp, "q", g + 2).then_inc(b.mark("load_q"), 16)
                sp.wait_ge(*b.filled("k3", g))
                self.load(sp, "k", g + 2).then_inc(b.mark("load_k"), 16)
            sp.wait_ge(*b.done("part", g))
            self.load(sp, "wo", g + 1).then_inc(b.mark("load_wo"), 16)

        with sp.Fori(0, GROUPS - 2) as g:
            iteration(g, True)
        iteration(GROUPS - 2, False)

    def pool(self, pool):
        k = self.k
        self.ln_pool(pool, self.first)

        def power(ph, var, out, dst, src, g):
            pool.wait_ge(*ph.done(var, g))
            pool.tensor_tensor(dst, src, k.minus_half[:, 0:dst.shape[1]], ALU.pow).then_inc(ph.mark(out), 1)

        def norms(ph, g=0, both=True):
            if both:
                power(ph, "q_var", "q_rs", self.rq, self.q_ssq, g)
            for b in self.BLOCKS:
                if both and b == 1:
                    shifts(ph, g)
                s = slice(4 * b, 4 * b + 4)
                power(ph, f"k_var{b}", f"k_rs{b}", self.rk[:, s], self.k_ssq[:, s], g)
            if not both:
                power(ph, "q_var", "q_rs", self.rq, self.q_ssq, g)

        def shifts(ph, g=0):
            for b in self.BLOCKS:
                if self.by_pool(b):
                    pool.wait_ge(*ph.drained("mB", g))
                    self.shift(pool, b).then_inc(ph.mark(f"shift{b}"), 1)

        if self.rope:
            with pool.Fori(0, GROUPS - 1) as g:
                shifts(self.body, g)
            shifts(self.last)
        else:
            norms(self.first, 0, False)
            with pool.Fori(0, GROUPS - 1) as g:
                norms(self.body, g)
            shifts(self.last)

    def shift(self, eng, b):
        block = self.probsT[:, 2048 * b:2048 * b + 2048].rearrange("p (t n) -> p t n", t=4)
        return eng.tensor_tensor(block, block, every_head(self.mrow, 4), ALU.subtract)

    def pe_block_scores(self, pe, ph, b, g=0):
        for t in range(4 * b, 4 * b + 4):
            pe.wait_ge(*ph.room(f"s{t}", g))
            pe.matmul(self.k.ps(t % 4), self.keysT[:, t * P:(t + 1) * P], self.qT, start=True, stop=True).then_inc(ph.fill(f"s{t}"), 1)

    def pe_block_values(self, pe, ph, b, g=0):
        if b == 0:
            pe.wait_ge(*ph.loaded("load_v", g))
        pe.wait_ge(*ph.room(f"v{b}", g))
        self.four_tiles(pe, self.k.ps(4 + b % 2), self.wv, b).then_inc(ph.fill(f"v{b}"), 1)

    def pe_scores(self, pe, ph, g=0):
        for b in self.BLOCKS[1:]:
            self.pe_block_scores(pe, ph, b, g)
            self.pe_block_values(pe, ph, b, g)

    def four_tiles(self, pe, bank, w, b):
        for j in range(4):
            t = 4 * b + j
            last = self.project(pe, bank[:, j * P:(j + 1) * P], w, P, src=self.k.ctxT[:, :, t * P:(t + 1) * P])
        return last

    def pe_max(self, pe, ph, name, g=0):
        k = self.k
        if name == "mT":
            pe.wait_ge(*ph.done("max", g))
            pe.wait_ge(*ph.room("mT", g))
            self.turn(pe, k.ps(6), self.most, PER_GROUP).then_inc(ph.fill("mT"), 1)
            return
        pe.wait_ge(*ph.drained("mT", g))
        for h in range(PER_GROUP):
            last = pe.transpose(k.ps(6)[:, h * P:(h + 1) * P], self.m[:, h:h + 1].broadcast_to([P, P]), k.ident)
        last.then_inc(ph.fill("mB"), 1)

    def pe_queries(self, pe, ph, g=0):
        pe.wait_ge(*ph.loaded("load_q", g))
        pe.wait_ge(*ph.room("q", g))
        self.project(pe, self.k.ps(4), self.wq, D).then_inc(ph.fill("q"), 1)

    def pe_project(self, pe, ph, g=0):
        self.pe_queries(pe, ph, g)
        self.pe_max(pe, ph, "mT", g)
        pe.wait_ge(*ph.loaded("load_k", g))
        for b in self.BLOCKS:
            self.pe_keys(pe, ph, b, g)
            if b == 0:
                self.pe_max(pe, ph, "mB", g)
        self.pe_turn(pe, ph, g)

    def pe_keys(self, pe, ph, b, g=0):
        pe.wait_ge(*ph.room(f"k{b}", g))
        self.four_tiles(pe, self.k.ps(b), self.wk, b).then_inc(ph.fill(f"k{b}"), 1)

    def pe_turn(self, pe, ph, g=0):
        k = self.k
        for b in self.BLOCKS:
            pe.wait_ge(*ph.drained(f"k{b}", g))
            pe.wait_ge(*ph.room(f"kT{b}", g))
            self.turn(pe, k.ps(5 - b % 2), self.keys[:, 512 * b:512 * b + 512], 4).then_inc(ph.fill(f"kT{b}"), 1)
        pe.wait_ge(*ph.drained("q", g))
        pe.wait_ge(*ph.room("qT", g))
        self.turn(pe, k.ps(6), self.qn, PER_GROUP).then_inc(ph.fill("qT"), 1)

    def pe_attend(self, pe, ph, g=0):
        k = self.k
        pe.wait_ge(*ph.drained("v2", g))
        pe.wait_ge(*ph.drained("v3", g))
        for h in range(PER_GROUP):
            if h % 2 == 0:
                pe.wait_ge(*ph.room(f"o{h // 2}", g))
            for t in range(KT):
                if h == 0 and t % 4 == 0:
                    pe.wait_ge(*ph.done(f"exp{t // 4}", g))
                c = t * 512 + h * P
                last = pe.matmul(k.ps(2 + h // 2)[:, h % 2 * (P + 1):(h % 2 + 1) * (P + 1)], self.probsT[:, c:c + P], self.values[:, t, :],
                                 start=t == 0, stop=t == KT - 1)
            if h % 2 == 1:
                last.then_inc(ph.fill(f"o{h // 2}"), 1)

    def pe_heads_T(self, pe, ph, g=0):
        k = self.k
        pe.wait_ge(*ph.drained("o0", g))
        pe.wait_ge(*ph.drained("o1", g))
        pe.wait_ge(*ph.room("oT", g))
        self.turn(pe, k.ps(6), self.on, PER_GROUP).then_inc(ph.fill("oT"), 1)

    def pe_out(self, pe, ph, g=0, stop=False):
        pe.wait_ge(*ph.drained("oT", g))
        pe.wait_ge(*ph.loaded("load_wo", g))
        for h in range(PER_GROUP):
            last = pe.matmul(self.k.ps(7), self.oT[:, h * P:(h + 1) * P], self.wo[:, h, :], start=False,
                             stop=stop and h == PER_GROUP - 1, skip_group_check=True)
        return last

    def pe(self, pe):
        k, f = self.k, self.first
        pe.wait_ge(*context_loaded(k))
        pe.wait_ge(*f.loaded("load_k"))
        for b in self.BLOCKS:
            self.pe_keys(pe, f, b)
            if b == 0:
                self.ln_pe(pe, f)
        pe.wait_ge(*self.last.room("y"))
        pe.matmul(k.ps(7), k.zeros, k.xn, start=True, stop=False, skip_group_check=True)
        pe.wait_ge(*f.drained("ln"))
        self.pe_queries(pe, f)
        self.pe_turn(pe, f)
        pe.wait_ge(*f.done("ones"))
        for b in "456":
            pe.wait_ge(*self.body.before(b, 0, "drained_"))
        self.pe_block_scores(pe, self.body, 0)
        self.pe_block_values(pe, self.body, 0)
        with pe.Fori(0, GROUPS - 1) as g:
            self.pe_scores(pe, self.body, g)
            self.pe_project(pe, self.body, g)
            self.pe_attend(pe, self.body, g)
            for name in ("kT2", "kT3", "qT"):
                pe.wait_ge(*self.body.drained(name, g))
            self.pe_block_scores(pe, self.body, 0, g + 1)
            self.pe_heads_T(pe, self.body, g)
            self.pe_block_values(pe, self.body, 0, g + 1)
            self.pe_out(pe, self.body, g).then_inc(self.body.mark("part"), 1)
        self.pe_scores(pe, self.last)
        for name in ("mT", "mB"):
            self.pe_max(pe, self.last, name)
        self.pe_attend(pe, self.last)
        self.pe_heads_T(pe, self.last)
        self.pe_out(pe, self.last, stop=True).then_inc(self.last.fill("y"), 1)

    def act_values(self, act, ph, g=0):
        for b in self.BLOCKS:
            act.wait_ge(*ph.filled(f"v{b}", g))
            act.activation(self.values[:, 4 * b:4 * b + 4, 0:P], heads(self.k.ps(4 + b % 2), 4), ACT.Copy).then_inc(ph.drain(f"v{b}"), 1)

    def act_exp(self, act, ph, b, g=0):
        act.wait_ge(*ph.done(f"shift{b}", g))
        block = self.probsT[:, 2048 * b:2048 * b + 2048]
        act.activation(block, block, ACT.Exp).then_inc(ph.mark(f"exp{b}"), 1)

    def act_squares(self, act, ph, b, g=0):
        if self.rope:
            return
        act.wait_ge(*ph.filled(f"k{b}", g))
        if b > 0:
            act.wait_ge(*ph.done(f"k_sq{b - 1}", g))
        for j in range(4):
            s = slice(j * P, (j + 1) * P)
            last = act.activation(self.tmpk[:, s], self.k.ps(b)[:, s], ACT.Square, accum_out=self.k_ssq[:, 4 * b + j:4 * b + j + 1])
        last.then_inc(ph.mark(f"k_sq{b}"), 1)

    def act_keys_T(self, act, ph, b, g=0):
        act.wait_ge(*ph.filled(f"kT{b}", g))
        act.activation(self.keysT[:, 512 * b:512 * b + 512], self.k.ps(5 - b % 2), ACT.Copy,
                       scale=1.0 if self.rope else self.kw).then_inc(ph.drain(f"kT{b}"), 1)

    def act_query_squares(self, act, ph, g=0):
        if not self.rope:
            act.wait_ge(*ph.filled("q", g))
            act.activation(self.tmp, self.k.ps(4), ACT.Square).then_inc(ph.mark("q_sq"), 1)

    def act_project(self, act, ph, g=0):
        both = ph is not self.first
        if both:
            self.act_query_squares(act, ph, g)
        for b in self.BLOCKS:
            self.act_squares(act, ph, b, g)
            if both and b < 2:
                self.act_exp(act, ph, b, g)
            if not both and b == 0:
                self.ln_act(act, ph)
        if not both:
            self.act_query_squares(act, ph, g)
        for b in self.BLOCKS:
            if both and b == 2:
                self.act_exp(act, ph, 2, g)
            self.act_keys_T(act, ph, b, g)
        act.wait_ge(*ph.filled("qT", g))
        act.activation(self.qT, self.k.ps(6), ACT.Copy, scale=self.scale if self.rope else self.qw).then_inc(ph.drain("qT"), 1)
        if both:
            self.act_exp(act, ph, 3, g)

    def act_heads_T(self, act, ph, g=0):
        act.wait_ge(*ph.filled("oT", g))
        act.activation(self.oT, self.k.ps(6), ACT.Copy).then_inc(ph.drain("oT"), 1)

    def act(self, act):
        act.wait_ge(*self.first.loaded("load_tab"))
        if not self.rope:
            act.wait_ge(*self.first.done("ones"))
        self.act_project(act, self.first)
        with act.Fori(0, GROUPS - 1) as g:
            self.act_values(act, self.body, g)
            self.act_project(act, self.body, g)
            self.act_heads_T(act, self.body, g)
        self.act_values(act, self.last)
        for b in self.BLOCKS:
            self.act_exp(act, self.last, b)
        self.act_heads_T(act, self.last)

    def rotate(self, v, src, out, tmp, cos, sin):
        k = self.k
        both = lambda ap: ap.rearrange("p h (s n) -> p h s n", s=2)
        v.scalar_tensor_tensor(out=both(tmp)[:, :, 0, :], in0=both(src)[:, :, 1, :], scalar=-1.0, in1=sin, op0=ALU.mult, op1=ALU.mult)
        v.tensor_tensor(both(tmp)[:, :, 1, :], both(src)[:, :, 0, :], sin, ALU.mult)
        v.tensor_tensor(both(out)[:, :, 0, :], both(src)[:, :, 0, :], cos, ALU.mult)
        k.link(v.tensor_tensor(both(out)[:, :, 1, :], both(src)[:, :, 1, :], cos, ALU.mult))
        return v.tensor_tensor(out, out, tmp, ALU.add)

    def tables(self, t, n):
        cos, sin = self.tab[:, C_ROPE_K["cos"]], self.tab[:, C_ROPE_K["sin"]]
        return tuple(ap[:, t * HALF:(t + n) * HALF].rearrange("p (t n) -> p t n", n=HALF) for ap in (cos, sin))

    def dve_scores(self, v, ph, g=0):
        k = self.k
        for b in self.BLOCKS:
            for t in range(4 * b, 4 * b + 4):
                v.wait_ge(*ph.filled(f"s{t}", g))
                v.tensor_tensor(heads(self.probsT[:, t * 512:(t + 1) * 512], PER_GROUP), heads(k.ps(t % 4), PER_GROUP),
                                every_head(self.mask[:, t * P:(t + 1) * P], PER_GROUP), ALU.add).then_inc(ph.drain(f"s{t}"), 1)
            v.wait_ge(*ph.drained(f"s{4 * b + 3}", g))
            if b >= 1:
                before = self.probsT[:, 0:2048] if b == 1 else self.most
                k.link(v.scalar_tensor_tensor(out=self.most, in0=before, scalar=NEG_MAX, in1=self.probsT[:, 2048 * b:2048 * b + 2048],
                                              op0=ALU.max, op1=ALU.max))
        k.link(v.tensor_tensor(self.most[:, 0:1024], self.most[:, 0:1024], self.most[:, 1024:2048], ALU.max))
        v.tensor_tensor(self.most[:, 0:512], self.most[:, 0:512], self.most[:, 512:1024], ALU.max).then_inc(ph.mark("max"), 1)

    def dve_max(self, v, ph, name, g=0):
        k = self.k
        v.wait_ge(*ph.filled(name, g))
        if name == "mT":
            v.reduce_max(self.m, heads(k.ps(6), PER_GROUP), AX_X).then_inc(ph.drain("mT"), 1)
        else:
            v.tensor_copy(self.mrow, k.ps(6)).then_inc(ph.drain("mB"), 1)

    def dve_shift(self, v, ph, b, g=0):
        if not self.by_pool(b):
            v.wait_ge(*ph.drained("mB", g))
            self.shift(v, b).then_inc(ph.mark(f"shift{b}"), 1)

    def dve_queries(self, v, ph, g=0):
        k = self.k
        if self.rope:
            v.wait_ge(*ph.filled("q", g))
            cos, sin = (every_head(c[:, 0, :], PER_GROUP) for c in self.tables(0, 1))
            self.rotate(v, heads(k.ps(4), 4), heads(self.qn, 4), heads(self.tmp, 4), cos, sin).then_inc(ph.drain("q"), 1)
            return
        v.wait_ge(*ph.done("q_sq", g))
        k.link(v.reduce_sum(self.q_ssq, heads(self.tmp, PER_GROUP), AX_X))
        v.tensor_scalar(self.q_ssq, self.q_ssq, 1.0 / P, 1e-5, ALU.mult, ALU.add).then_inc(ph.mark("q_var"), 1)
        v.wait_ge(*ph.done("q_rs", g))
        v.tensor_tensor(heads(self.qn, PER_GROUP), heads(k.ps(4), PER_GROUP), per_head(self.rq, P), ALU.mult).then_inc(ph.drain("q"), 1)

    def dve_keys_var(self, v, ph, b, g=0):
        if not self.rope:
            s = slice(4 * b, 4 * b + 4)
            v.wait_ge(*ph.done(f"k_sq{b}", g))
            v.tensor_scalar(self.k_ssq[:, s], self.k_ssq[:, s], 1.0 / P, 1e-5, ALU.mult, ALU.add).then_inc(ph.mark(f"k_var{b}"), 1)

    def dve_keys(self, v, ph, b, g=0, var=True):
        k = self.k
        src, out = heads(k.ps(b), 4), heads(self.keys[:, 512 * b:512 * b + 512], 4)
        if self.rope:
            v.wait_ge(*ph.filled(f"k{b}", g))
            self.rotate(v, src, out, heads(self.tmpk, 4), *self.tables(4 * b, 4)).then_inc(ph.drain(f"k{b}"), 1)
            v.wait_ge(*ph.drained(f"k{b}", g))
            return
        if var:
            self.dve_keys_var(v, ph, b, g)
        s = slice(4 * b, 4 * b + 4)
        v.wait_ge(*ph.done(f"k_rs{b}", g))
        v.tensor_tensor(out, src, per_head(self.rk[:, s], P), ALU.mult).then_inc(ph.drain(f"k{b}"), 1)

    def dve_attend(self, v, ph, g=0):
        k = self.k
        for j in range(2):
            out = k.ps(2 + j)[:, 0:2 * (P + 1)].rearrange("p (h n) -> p h n", h=2)
            inv = self.inv[:, 2 * j:2 * j + 2]
            v.wait_ge(*ph.filled(f"o{j}", g))
            k.link(v.reciprocal(inv.unsqueeze(2), out[:, :, P:P + 1]))
            v.tensor_tensor(heads(self.on[:, 256 * j:256 * j + 256], 2), out[:, :, 0:P], per_head(inv, P), ALU.mult).then_inc(ph.drain(f"o{j}"), 1)

    def dve(self, v):
        k, f, b = self.k, self.first, self.body
        self.ln_dve(v, f)
        v.wait_ge(*f.loaded("load_tab"))
        if not self.rope:
            k.link(v.tensor_scalar(self.qw, self.qw, self.scale, None, ALU.mult))
        v.memset(self.values[:, :, P:P + 1], 1.0).then_inc(f.mark("ones"), 1)
        for j in self.BLOCKS:
            self.dve_keys(v, f, j)
        self.dve_queries(v, f)
        v.wait_ge(*f.loaded("load_mask"))
        with v.Fori(0, GROUPS - 1) as g:
            k.chain.loop(g, 11 if self.rope else 7)
            self.dve_scores(v, b, g)
            self.dve_max(v, b, "mT", g)
            self.dve_queries(v, b, g)
            self.dve_max(v, b, "mB", g)
            self.dve_shift(v, b, 0, g)
            self.dve_keys(v, b, 0, g)
            if self.rope:
                for j in (1, 2, 3):
                    self.dve_keys(v, b, j, g)
                self.dve_shift(v, b, 3, g)
            else:
                self.dve_shift(v, b, 1, g)
                self.dve_shift(v, b, 3, g)
                self.dve_keys_var(v, b, 1, g)
                self.dve_keys_var(v, b, 2, g)
                self.dve_keys(v, b, 1, g, False)
                self.dve_keys(v, b, 2, g, False)
                self.dve_keys(v, b, 3, g)
            self.dve_attend(v, b, g)
        k.chain.end(GROUPS - 1)
        self.dve_scores(v, self.last)
        for name in ("mT", "mB"):
            self.dve_max(v, self.last, name)
        for j in self.BLOCKS:
            self.dve_shift(v, self.last, j)
        self.dve_attend(v, self.last)
        v.wait_ge(*self.last.filled("y"))
        self.add_output(v, self.last)


class L2Attn(Layer):

    def __init__(self, k):
        super().__init__(k)
        ev = [("load_pack", "load_pack1")] + LN_EVENTS + [("q", "0"), ("kv", "1"), ("v", "v_ready")]
        ev += [(f"kT{j}", "3") for j in range(2)]
        for g in range(GROUPS):
            ev += [(f"qT{g}", "45"[g % 2])]
        for g in range(GROUPS):
            ev += [(f"s{g}", "01"[g % 2]), (f"shift{g}", "shift"), (f"exp{g}", "exp"), (f"pT{g}", "23"[g % 2])]
        self.y = self.p = Phase(k, ev + [("o", "6"), ("oT", "4"), ("y", "7")])
        pack_ = k.area("pack1")
        self.wq, self.wkv = (pack_[:, C_L2A[n]].rearrange("p (o n) -> p o n", o=DC) for n in ("wq", "wkv"))
        self.wo = pack_[:, C_L2A["wo"]].rearrange("p (o n) -> p o n", o=DC)
        self.cos, self.sin = pack_[:, C_L2A["cos"]], pack_[:, C_L2A["sin"]]
        w = k.area("work")
        self.qn, self.tmp, self.kn, self.tmpk, self.v = w[:, 0:512], w[:, 512:1024], w[:, 1024:1152], w[:, 1152:1280], w[:, 1280:1408]
        self.qT, self.kT = w[0:HD2, 1536:5632], w[0:HD2, 5632:6656]
        self.probs = [w[:, 6656:7168], w[:, 7168:7680]]
        self.pT = [w[:, 7680:8192], w[:, 8192:8704]]
        self.on, self.oT = w[:, 8704:9216], w[:, 9216:9728]
        self.max, self.sum, self.inv = k.small[:, 0:4], k.small[:, 16:48], k.small[:, 48:80]

    def sp(self, sp):
        k = self.k
        if "L1a" in k.layers:
            sp.wait_ge(*k.layers["L1a"].y.drained("y"))
        sp.dma_start(k.area("pack1", 0, C_L2A["all"]), k.dram["l2a"]).then_inc(self.p.mark("load_pack"), 16)

    def pe(self, pe):
        k, p = self.k, self.p
        self.ln_pe(pe, p)
        pe.wait_ge(*p.drained("ln"))
        pe.wait_ge(*p.loaded("load_pack"))
        pe.wait_ge(*p.room("q"))
        self.project(pe, k.ps(0), self.wq, D).then_inc(p.fill("q"), 1)
        pe.wait_ge(*p.room("kv"))
        self.project(pe, k.ps(1), self.wkv, 256).then_inc(p.fill("kv"), 1)
        pe.wait_ge(*p.drained("q"))

        def turn16(name, bank, src, first):
            pe.wait_ge(*p.room(name))
            for j in range(4):
                c = (first + j) * HD2
                last = pe.transpose(k.ps(bank)[0:HD2, j * P:(j + 1) * P], src[:, c:c + HD2], k.ident)
            last.then_inc(p.fill(name), 1)

        for g in range(2):
            turn16(f"qT{g}", 4 + g % 2, self.qn, 4 * g)
        pe.wait_ge(*p.drained("kv"))
        for j in range(2):
            turn16(f"kT{j}", 3, self.kn, 4 * j)
        pe.wait_ge(*p.done("v"))
        pe.wait_ge(*p.drained("kT1"))
        pe.wait_ge(*p.room("o"))

        def scores(g):
            pe.wait_ge(*p.drained(f"qT{g}"))
            pe.wait_ge(*p.room(f"s{g}"))
            for h in range(4):
                c = 4 * g + h
                last = pe.matmul(k.ps(g % 2)[:, h * P:(h + 1) * P], self.qT[:, c * P:(c + 1) * P], self.kT[:, g * P:(g + 1) * P], start=True, stop=True)
            last.then_inc(p.fill(f"s{g}"), 1)

        def attend(g):
            pe.wait_ge(*p.drained(f"pT{g}"))
            for h in range(4):
                c = 4 * g + h
                last = pe.matmul(k.ps(6)[:, c * HD2:(c + 1) * HD2], self.pT[g % 2][:, h * P:(h + 1) * P], self.v[:, g * HD2:(g + 1) * HD2], start=True, stop=True)
            if g == GROUPS - 1:
                last.then_inc(p.fill("o"), 1)

        scores(0)
        for g in range(GROUPS + 1):
            if g + 1 < GROUPS:
                scores(g + 1)
            if g + 2 < GROUPS:
                turn16(f"qT{g + 2}", 4 + g % 2, self.qn, 4 * (g + 2))
            if g < GROUPS:
                pe.wait_ge(*p.done(f"exp{g}"))
                pe.wait_ge(*p.room(f"pT{g}"))
                self.turn(pe, k.ps(2 + g % 2), self.probs[g % 2], 4).then_inc(p.fill(f"pT{g}"), 1)
            if g >= 1:
                attend(g - 1)
        pe.wait_ge(*p.drained("o"))
        pe.wait_ge(*p.room("oT"))
        self.turn(pe, k.ps(4), self.on, DC).then_inc(p.fill("oT"), 1)
        pe.wait_ge(*p.drained("oT"))
        pe.wait_ge(*p.room("y"))
        self.project(pe, k.ps(7), self.wo, D, src=heads(self.oT, DC)).then_inc(p.fill("y"), 1)

    def act(self, act):
        k, p = self.k, self.p
        self.ln_act(act, p)

        def queries_T(g):
            act.wait_ge(*p.filled(f"qT{g}"))
            act.activation(self.qT[:, 512 * g:512 * g + 512], k.ps(4 + g % 2)[0:HD2, :], ACT.Copy).then_inc(p.drain(f"qT{g}"), 1)

        queries_T(0)
        queries_T(1)
        for j in range(2):
            act.wait_ge(*p.filled(f"kT{j}"))
            act.activation(self.kT[:, 512 * j:512 * j + 512], k.ps(3)[0:HD2, :], ACT.Copy).then_inc(p.drain(f"kT{j}"), 1)
        for g in range(GROUPS + 1):
            if g < GROUPS:
                act.wait_ge(*p.done(f"shift{g}"))
                act.activation(self.probs[g % 2], self.probs[g % 2], ACT.Exp).then_inc(p.mark(f"exp{g}"), 1)
            if g + 2 < GROUPS:
                queries_T(g + 2)
            if g >= 1:
                act.wait_ge(*p.filled(f"pT{g - 1}"))
                act.activation(self.pT[(g - 1) % 2], k.ps(2 + (g - 1) % 2), ACT.Copy).then_inc(p.drain(f"pT{g - 1}"), 1)

    def rotate(self, v, src, out, tmp, n):
        both = lambda ap: ap.rearrange("p (h s n) -> p h s n", s=2, n=8)
        cos, sin = every_head(self.cos, n), every_head(self.sin, n)
        v.scalar_tensor_tensor(out=both(tmp)[:, :, 0, :], in0=both(src)[:, :, 1, :], scalar=-1.0, in1=sin, op0=ALU.mult, op1=ALU.mult)
        v.tensor_tensor(both(tmp)[:, :, 1, :], both(src)[:, :, 0, :], sin, ALU.mult)
        v.tensor_tensor(both(out)[:, :, 0, :], both(src)[:, :, 0, :], cos, ALU.mult)
        self.k.link(v.tensor_tensor(both(out)[:, :, 1, :], both(src)[:, :, 1, :], cos, ALU.mult))
        return v.tensor_tensor(out, out, tmp, ALU.add)

    def dve(self, v):
        k, p = self.k, self.p
        self.ln_dve(v, p)
        v.wait_ge(*p.loaded("load_pack"))
        v.wait_ge(*p.filled("q"))
        self.rotate(v, k.ps(0), self.qn, self.tmp, 32).then_inc(p.drain("q"), 1)
        v.wait_ge(*p.filled("kv"))
        v.tensor_copy(self.v, k.ps(1)[:, P:2 * P]).then_inc(p.mark("v"), 1)
        self.rotate(v, k.ps(1)[:, 0:P], self.kn, self.tmpk, 8).then_inc(p.drain("kv"), 1)

        def shift(g):
            pr = heads(self.probs[g % 2], 4)
            v.wait_ge(*p.filled(f"s{g}"))
            v.scalar_tensor_tensor(out=pr, in0=heads(k.ps(g % 2), 4), scalar=float(HD2) ** -0.5, in1=every_head(k.causal, 4),
                                   op0=ALU.mult, op1=ALU.add).then_inc(p.drain(f"s{g}"), 1)
            v.wait_ge(*p.drained(f"s{g}"))
            k.link(v.reduce_max(self.max, pr, AX_X))
            v.tensor_tensor(pr, pr, per_head(self.max, P), ALU.subtract).then_inc(p.mark(f"shift{g}"), 1)

        def total(g):
            v.wait_ge(*p.done(f"exp{g}"))
            k.link(v.reduce_sum(self.sum[:, 4 * g:4 * g + 4], heads(self.probs[g % 2], 4), AX_X))

        for g in range(GROUPS + 1):
            if g < GROUPS:
                shift(g)
            if g >= 1:
                total(g - 1)
        k.link(v.reciprocal(self.inv, self.sum))
        v.wait_ge(*p.filled("o"))
        v.tensor_tensor(heads(self.on, 32), heads(k.ps(6), 32), per_head(self.inv, HD2), ALU.mult).then_inc(p.drain("o"), 1)
        v.wait_ge(*p.filled("oT"))
        v.tensor_copy(self.oT, k.ps(4)).then_inc(p.drain("oT"), 1)
        v.wait_ge(*p.filled("y"))
        self.add_output(v, p)


class L2Ffn(Layer):
    SLOTS = 4

    def __init__(self, k):
        super().__init__(k)
        ev = [("load_pack", "load_pack0"), ("load_bias", "load_bias")] + [(f"load{j}", f"load_expert{j % self.SLOTS}") for j in range(E8)]
        ev += LN_EVENTS + [("g", "6"), ("shift", "shift"), ("exp", "exp"), ("sel", "chosen"), ("selT", "5")]
        ev += [(f"e{j}", str(j % 4)) for j in range(E8)] + [("y", "7")]
        self.y = self.p = Phase(k, ev)
        pack_ = k.area("pack0")
        self.wg = pack_[:, C_L2F["gate"]].rearrange("p (o n) -> p o n", o=DC)
        self.bg, self.rank = pack_[:, C_L2F["bgate"]], pack_[:, C_L2F["rank"]]
        self.bias, self.selT = k.area("work", 0, 512)[0:E8, :], k.area("work", 512, 640)[0:E8, :]
        self.slots = [k.area("weights", 5120 + 2048 * j, 5120 + 2048 * (j + 1)).rearrange("p (o n) -> p o n", o=DC) for j in range(self.SLOTS)]
        s = k.small
        self.g, self.e, self.sel = s[:, 0:8], s[:, 8:16], s[:, 16:24]
        self.m, self.sum, self.inv, self.top = (s[:, 32 + j:33 + j] for j in range(4))

    def load_expert(self, sp, j):
        slot = self.slots[j % self.SLOTS].rearrange("p o n -> p (o n)")
        sp.dma_start(slot, self.k.dram["l2f"][j]).then_inc(self.p.mark(f"load{j}"), 16)

    def sp(self, sp):
        k = self.k
        for name in ("L1a", "L1f", "L2x"):
            if name in k.layers:
                sp.wait_ge(*k.layers[name].y.drained("y"))
        sp.dma_start(k.area("pack0", 0, C_L2F["all"]), k.dram["l2f_gate"]).then_inc(self.p.mark("load_pack"), 16)
        for j in range(self.SLOTS):
            self.load_expert(sp, j)
        if "L2a" in k.layers:
            sp.wait_ge(*k.layers["L2a"].y.filled("y"))
        sp.dma_start(self.bias, k.dram["l2f_bias"]).then_inc(self.p.mark("load_bias"), 16)
        for j in range(self.SLOTS, E8):
            sp.wait_ge(*self.p.filled(f"e{j - self.SLOTS}"))
            self.load_expert(sp, j)

    def pe(self, pe):
        k, p = self.k, self.p
        self.ln_pe(pe, p)
        pe.wait_ge(*p.drained("ln"))
        pe.wait_ge(*p.loaded("load_pack"))
        pe.wait_ge(*p.room("g"))
        self.project(pe, k.ps(6), self.wg, E8).then_inc(p.fill("g"), 1)
        for j in range(E8):
            pe.wait_ge(*p.loaded(f"load{j}"))
            pe.wait_ge(*p.room(f"e{j}"))
            self.project(pe, k.ps(j % 4), self.slots[j % self.SLOTS], D).then_inc(p.fill(f"e{j}"), 1)
            if j == 3:
                pe.wait_ge(*p.done("sel"))
                pe.wait_ge(*p.room("selT"))
                pe.transpose(k.ps(5)[0:E8, 0:P], self.sel, k.ident).then_inc(p.fill("selT"), 1)
        pe.wait_ge(*p.drained("selT"))
        pe.wait_ge(*p.loaded("load_bias"))
        pe.wait_ge(*p.room("y"))
        pe.matmul(k.ps(7), self.selT, self.bias, start=True, stop=True).then_inc(p.fill("y"), 1)

    def act(self, act):
        k, p = self.k, self.p
        self.ln_act(act, p)
        act.wait_ge(*p.done("shift"))
        act.activation(self.e, self.e, ACT.Exp, accum_out=self.sum).then_inc(p.mark("exp"), 1)
        act.wait_ge(*p.filled("selT"))
        act.activation(self.selT, k.ps(5)[0:E8, 0:P], ACT.Copy).then_inc(p.drain("selT"), 1)

    def dve(self, v):
        k, p = self.k, self.p
        self.ln_dve(v, p)
        v.wait_ge(*p.loaded("load_pack"))
        v.wait_ge(*p.filled("g"))
        v.tensor_tensor(self.g, k.ps(6)[:, 0:E8], self.bg, ALU.add).then_inc(p.drain("g"), 1)
        v.wait_ge(*p.drained("g"))
        k.link(v.reduce_max(self.m, self.g, AX_X))
        v.tensor_scalar(self.e, self.g, self.m, None, ALU.subtract).then_inc(p.mark("shift"), 1)
        v.wait_ge(*p.done("exp"))
        k.link(v.reciprocal(self.inv, self.sum))
        k.link(v.tensor_scalar(self.g, self.e, self.inv, None, ALU.mult))
        k.link(v.reduce_max(self.m, self.g, AX_X))
        k.link(v.tensor_scalar(self.e, self.g, self.m, None, ALU.is_equal))
        k.link(v.tensor_tensor(self.e, self.e, self.rank, ALU.mult))
        k.link(v.reduce_max(self.top, self.e, AX_X))
        v.tensor_scalar(self.sel, self.e, self.top, None, ALU.is_equal).then_inc(p.mark("sel"), 1)
        v.wait_ge(*p.done("sel"))
        for j in range(E8):
            v.wait_ge(*p.filled(f"e{j}"))
            v.scalar_tensor_tensor(out=k.x, in0=k.ps(j % 4), scalar=self.sel[:, j:j + 1], in1=k.x, op0=ALU.mult,
                                   op1=ALU.add).then_inc(p.drain(f"e{j}"), 1)
            v.wait_ge(*p.drained(f"e{j}"))
        v.wait_ge(*p.filled("y"))
        self.add_output(v, p)


class L3Attn(Layer):
    SLOTS = 4

    def __init__(self, k):
        super().__init__(k)
        ev = [("load_v", "load_values")] + [(f"load{g}", f"load_expert{g % self.SLOTS}") for g in range(GROUPS)]
        ev += [(f"pair{g}", "row_pairs") for g in range(GROUPS)] + [(f"sum{g}", "row_sums") for g in range(GROUPS)]
        self.y = self.p = Phase(k, ev + LN_EVENTS + [("v0", "5"), ("v1", "6"), ("part0", "l3a_part"), ("part1", "l3a_part"), ("part2", "l3a_part"), ("part3", "l3a_part"),
                                     ("part4", "l3a_part"), ("part5", "l3a_part"), ("part6", "l3a_part"), ("y", "7")])
        w, p0, a = k.area("weights"), k.area("pack0"), k.area("work")
        self.wv = w[:, 5120:9216].rearrange("p (o n) -> p o n", o=DC)
        self.slots = [w[:, 9216:11264], w[:, 11264:13312], p0[:, 0:2048], p0[:, 2048:4096]]
        self.pairs = [a[:, 1024 * j:1024 * j + 1024] for j in range(2)]
        self.sums = [a[:, 2048 + 512 * j:2560 + 512 * j] for j in range(4)]
        self.vT = a[:, 4096:5120]

    def load_rows(self, sp, g):
        sp.dma_start(self.slots[g % self.SLOTS], self.k.dram["l3a_out"][g]).then_inc(self.p.mark(f"load{g}"), 16)

    def sp(self, sp):
        k, p = self.k, self.p
        if "L2f" in k.layers:
            sp.wait_ge(*k.layers["L2f"].y.drained("y"))
        sp.dma_start(k.area("weights", 5120, 9216), k.dram["l3a_v"]).then_inc(p.mark("load_v"), 16)
        for g in range(self.SLOTS):
            self.load_rows(sp, g)
        for g in range(self.SLOTS, GROUPS):
            sp.wait_ge(*p.done(f"pair{g - self.SLOTS}"))
            self.load_rows(sp, g)

    def pe(self, pe):
        k, p = self.k, self.p
        self.ln_pe(pe, p)
        pe.wait_ge(*p.drained("ln"))
        pe.wait_ge(*p.loaded("load_v"))
        for j in range(2):
            pe.wait_ge(*p.room(f"v{j}"))
            for c in range(4):
                g = 4 * j + c
                for o in range(DC):
                    last = pe.matmul(k.ps(5 + j)[:, c * P:(c + 1) * P], self.wv[:, o, g * P:(g + 1) * P], k.xnT[:, o, :], start=o == 0, stop=o == DC - 1)
            last.then_inc(p.fill(f"v{j}"), 1)
        pe.wait_ge(*p.room("y"))
        for g in range(GROUPS):
            if g % 4 == 0:
                pe.wait_ge(*p.drained(f"v{g // 4}"))
            pe.wait_ge(*p.done(f"sum{g}"))
            ins = pe.matmul(k.ps(7), self.vT[:, g * P:(g + 1) * P], self.sums[g % 4], start=g == 0, stop=g == GROUPS - 1)
            ins.then_inc(p.mark(f"part{g}") if g < GROUPS - 1 else p.fill("y"), 1)

    def act(self, act):
        k, p = self.k, self.p
        self.ln_act(act, p)
        for j in range(2):
            act.wait_ge(*p.filled(f"v{j}"))
            act.activation(self.vT[:, 512 * j:512 * j + 512], k.ps(5 + j), ACT.Copy).then_inc(p.drain(f"v{j}"), 1)

    def dve(self, v):
        k, p = self.k, self.p
        self.ln_dve(v, p)
        for g in range(GROUPS):
            slot, pair = self.slots[g % self.SLOTS], self.pairs[g % 2]
            v.wait_ge(*p.loaded(f"load{g}"))
            v.tensor_tensor(pair, slot[:, 0:1024], slot[:, 1024:2048], ALU.add).then_inc(p.mark(f"pair{g}"), 1)
            v.wait_ge(*p.done(f"pair{g}"))
            if g >= 4:
                v.wait_ge(*p.done(f"part{g - 4}"))
            v.tensor_tensor(self.sums[g % 4], pair[:, 0:512], pair[:, 512:1024], ALU.add).then_inc(p.mark(f"sum{g}"), 1)
        v.wait_ge(*p.filled("y"))
        self.add_output(v, p)


class L3Ffn(Layer):

    def __init__(self, k):
        super().__init__(k)
        self.y = self.p = Phase(k, [("load_pack", "load_pack1"), ("load_mask", "load_fmask"), ("load_f", "load_fourier"), ("w", "decoders"), ("m", "6")] + LN_EVENTS + [
            ("e", "5"), ("e_out", "encoded"), ("eT", "4"), ("y", "7")])
        pack_ = k.area("pack1")
        self.w, self.enc = (pack_[:, C_L3F[n]].rearrange("p (o n) -> p o n", o=DC) for n in ("w", "enc"))
        self.coef, self.bias = pack_[:, C_L3F["coef"]], pack_[:, C_L3F["bias"]]
        self.fourier = k.area("weights", 0, 2048).rearrange("p (o n) -> p o n", o=DC)
        a = k.area("work", 5120)
        self.mask_words, self.mask = a[:, 0:120].bitcast(mybir.dt.int32), a[:, 0:120].bitcast(U8)
        self.maskf, self.dec, self.e = a[:, 128:608], a[:, 608:768], a[:, 768:808]
        self.m, self.eT = a[0:R3, 1024:1536], a[0:R3, 1536:1664]

    def sp(self, sp):
        k = self.k
        for name in ("L2a", "L3x"):
            if name in k.layers:
                sp.wait_ge(*k.layers[name].y.drained("y"))
        sp.dma_start(k.area("pack1", 0, C_L3F["all"]), k.dram["l3f"]).then_inc(self.p.mark("load_pack"), 16)
        sp.dma_start(self.mask_words, k.dram["l3f_mask"]).then_inc(self.p.mark("load_mask"), 16)
        sp.dma_start(k.area("weights", 0, 2048), k.dram["fourier"]).then_inc(self.p.mark("load_f"), 16)

    def pe(self, pe):
        k, p = self.k, self.p
        pe.wait_ge(*p.done("w"))
        pe.wait_ge(*p.loaded("load_f"))
        pe.wait_ge(*p.room("m"))
        dec = self.dec.rearrange("p (o r) -> p o r", o=DC)
        for o in range(DC):
            last = pe.matmul(k.ps(6)[0:R3, :], dec[:, o, :], self.fourier[:, o, :], start=o == 0, stop=o == DC - 1)
        last.then_inc(p.fill("m"), 1)
        self.ln_pe(pe, p)
        pe.wait_ge(*p.drained("ln"))
        pe.wait_ge(*p.room("e"))
        pe.wait_ge(*p.loaded("load_pack"))
        self.project(pe, k.ps(5), self.enc, R3).then_inc(p.fill("e"), 1)
        pe.wait_ge(*p.room("y"))
        self.project(pe, k.ps(7), self.w, D, stop=False)
        pe.wait_ge(*p.drained("e"))
        pe.transpose(k.ps(4)[0:R3, 0:P], self.e, k.ident).then_inc(p.fill("eT"), 1)
        pe.wait_ge(*p.drained("eT"))
        pe.wait_ge(*p.drained("m"))
        pe.matmul(k.ps(7), self.eT, self.m, start=False, stop=True).then_inc(p.fill("y"), 1)

    def act(self, act):
        k, p = self.k, self.p
        act.wait_ge(*p.filled("m"))
        act.activation(self.m, k.ps(6)[0:R3, :], ACT.Copy, scale=0.5).then_inc(p.drain("m"), 1)
        self.ln_act(act, p)
        act.wait_ge(*p.filled("e"))
        act.activation(self.e, k.ps(5)[:, 0:R3], ACT.Copy).then_inc(p.drain("e"), 1)
        act.wait_ge(*p.filled("eT"))
        act.activation(self.eT, k.ps(4)[0:R3, 0:P], ACT.Copy).then_inc(p.drain("eT"), 1)

    def dve(self, v):
        k, p = self.k, self.p
        v.wait_ge(*p.loaded("load_mask"))
        v.wait_ge(*p.loaded("load_pack"))
        k.link(v.tensor_copy(self.maskf, self.mask))
        k.link(v.tensor_tensor(self.maskf, self.maskf, self.coef, ALU.mult))
        masked = self.maskf.rearrange("p (o e r) -> p o e r", o=DC, e=3)
        dec = self.dec.rearrange("p (o r) -> p o r", o=DC)
        k.link(v.tensor_tensor(dec, masked[:, :, 0, :], masked[:, :, 1, :], ALU.add))
        v.tensor_tensor(dec, dec, masked[:, :, 2, :], ALU.add).then_inc(p.mark("w"), 1)
        self.ln_dve(v, p)
        k.link(v.tensor_tensor(k.x, k.x, self.bias, ALU.add))
        v.wait_ge(*p.filled("y"))
        self.add_output(v, p)


LAYERS = ("L0x", "L0a", "L0f", "L1x", "L1a", "L1f", "L2x", "L2a", "L2f", "L3x", "L3a", "L3f")


def build(nc, dram, out):
    with ExitStack() as ctx:
        k = Program(nc, ctx, dram)
        start = Phase(k, [("load_const", "load_const"), ("load_x", "load_x"), ("zeros", "zeros"), ("store", "store")])
        make = {"L0x": lambda: L0Xattn(k), "L0a": lambda: SelfAttention(k), "L0f": lambda: L0Ffn(k),
                "L1x": lambda: L1Xattn(k), "L1a": lambda: Scan(k), "L1f": lambda: L1Ffn(k),
                "L2x": lambda: CrossAttention(k, "l2x", True), "L2a": lambda: L2Attn(k), "L2f": lambda: L2Ffn(k),
                "L3x": lambda: CrossAttention(k, "l3x", False), "L3a": lambda: L3Attn(k),
                "L3f": lambda: L3Ffn(k)}
        k.layers = {}
        for name in LAYERS:
            k.layers[name] = make[name]()
        layers = list(k.layers.values())
        block = ctx.enter_context(nc.Block())

        @block.sync
        def _(sp):
            sp.dma_start(k.x, dram["x"]).then_inc(start.mark("load_x"), 16)
            sp.dma_start(k.mem[:, AREA["ident"].start:AREA["minus_half"].stop], dram["const"]).then_inc(start.mark("load_const"), 16)
            for layer in layers:
                layer.sp(sp)
            sp.wait_ge(*layers[-1].y.drained("y"))
            sp.dma_start(out, k.x).then_inc(start.mark("store"), 16)
            sp.wait_ge(*start.loaded("store"))

        @block.gpsimd
        def _(pool):
            pool.wait_ge(*start.loaded("load_const"))
            for layer in layers:
                layer.pool(pool)

        @block.tensor
        def _(pe):
            pe.wait_ge(*start.loaded("load_const"))
            pe.wait_ge(*start.done("zeros"))
            for layer in layers:
                layer.pe(pe)

        @block.scalar
        def _(act):
            k.act_chain = Chain(act, k.sem("scalar_step"))
            k.act_link = k.act_chain.link
            for layer in layers:
                layer.act(act)

        @block.vector
        def _(v):
            k.chain = Chain(v, k.sem("vector_step"))
            k.link = k.chain.link
            v.memset(k.zeros, 0.0).then_inc(start.mark("zeros"), 1)
            for b in range(8):
                v.memset(k.ps(b), 0.0).then_inc(k.sem(f"drained_{b}"), 1)
            v.wait_ge(*start.loaded("load_x"))
            v.wait_ge(*start.loaded("load_const"))
            for layer in layers:
                layer.dve(v)


def tiles(a):
    n = a.shape[1]
    return a.reshape(-1, P, n).transpose(1, 0, 2).reshape(P, -1)


def rows(a, n=P):
    return np.broadcast_to(a.reshape(1, -1), (n, a.size))


def cols(a):
    return a.reshape(-1, P).T


def pack(*parts):
    return np.ascontiguousarray(np.concatenate(parts, axis=1))


def rope_table(positions, inv_freq):
    ang = positions[:, None].astype(np.float32) * inv_freq[None, :].astype(np.float32)
    return np.cos(ang.astype(np.float64)).astype(np.float32), np.sin(ang.astype(np.float64)).astype(np.float32)


def group_weights(wq, wk, wv, wo, d=P):
    out = []
    for g in range(GROUPS):
        q = tiles(wq[:, g * 512:(g + 1) * 512])
        kv = tiles(np.concatenate([wk[:, g * P:(g + 1) * P], wv[:, g * P:(g + 1) * P]], axis=1))
        out.append(np.concatenate([q, kv, tiles(wo[g * 512:(g + 1) * 512])], axis=1))
    return np.stack(out)


def layout(i):
    half = HALF
    pos = np.arange(P)
    inv0 = (10000.0 ** (-np.arange(half, dtype=np.float32) / half).astype(np.float64)).astype(np.float32)
    c0, s0 = rope_table(pos, inv0)
    a = {"x": i["x"][0],
         "const": pack(np.eye(P, dtype=np.float32), np.where(np.tri(P, dtype=bool), 0.0, NEG).astype(np.float32),
                       np.full((P, 16), -0.5, np.float32)),
         "ctxT": tiles(i["ctx_4096"][0].T), "ctx": tiles(i["ctx_4096"][0])}
    a["l0x"] = pack(tiles(i["L0_xattn_Wq"].T), tiles(i["L0_xattn_Wk"]), rows(i["L0_xattn_bq"]), rows(i["L0_xattn_bk"]))
    a["l0a"] = group_weights(i["L0_attn_wq"], i["L0_attn_wk"], i["L0_attn_wv"], i["L0_attn_wo"])
    a["rope_self"] = pack(c0, s0, -s0)
    a["l0f"] = pack(tiles(i["L0_ffn_W"].T), tiles(i["L0_ffn_lora_A"].reshape(P, D).T),
                    i["L0_ffn_lora_B"].transpose(0, 2, 1).reshape(P, D), rows(i["L0_ffn_bias"]),
                    np.repeat(i["L0_ffn_lora_weights"], 16)[:, None])
    a["l1x"] = pack(tiles(i["L1_xattn_Wq_w"].T), tiles(i["L1_xattn_Wk_w"].T), rows(i["L1_xattn_Wq_b"]), rows(i["L1_xattn_Wk_b"]),
                    rows(i["L1_xattn_fn_w"]), cols(i["L1_xattn_fn_w"]), cols(i["L1_xattn_qn_w"]), cols(i["L1_xattn_kn_w"]))

    inner = GROUPS * GROUP_D
    wt = i["L1_attn_in_proj_w"].T
    xw, bw, cw = inner, 2 * inner, 2 * inner + GROUPS * P
    conv = np.concatenate([i["L1_attn_conv_w"][:, 0, :], i["L1_attn_conv_b"][:, None]], axis=1)
    outw = i["L1_attn_out_proj_w"].T
    groups, convs, table = [], [], []
    for g in range(GROUPS):
        own = np.concatenate([np.arange(g * GROUP_D, (g + 1) * GROUP_D), inner + np.arange(g * P, (g + 1) * P),
                              inner + GROUPS * P + np.arange(g * P, (g + 1) * P)])
        groups.append(np.concatenate([tiles(wt[:, xw + own]), tiles(wt[:, g * GROUP_D:(g + 1) * GROUP_D]),
                                      tiles(outw[g * GROUP_D:(g + 1) * GROUP_D])], axis=1))
        convs.append(tiles(conv[own]))
        table.append(np.concatenate([cols(i["L1_attn_norm_w"][g * GROUP_D:(g + 1) * GROUP_D]), np.zeros((P, 32), np.float32),
                                     rows(i["L1_attn_D"][g * HG:(g + 1) * HG])], axis=1))
    a["l1a"] = np.stack(groups)
    a["l1a_small"] = pack(tiles(wt[:, cw + GROUPS * P:]), *convs, *table, rows(i["L1_attn_dt_bias"]),
                          -np.arange(1, P + 1, dtype=np.float32)[:, None], np.triu(np.ones((P, P), np.float32)))
    a["l1f"] = pack(tiles(i["L1_ffn_W_base"].T), tiles(i["L1_ffn_A_w"].reshape(P, D).T),
                    tiles(np.concatenate([i["L1_ffn_W_gate"].T, i["L1_ffn_W_thr"][:, None]], axis=1)),
                    i["L1_ffn_B_w"].transpose(0, 2, 1).reshape(P, D), rows(i["L1_ffn_b_base"]), rows(i["L1_ffn_b_thr"]))

    inv2 = (1.0 / (10000.0 ** (np.arange(0, P, 2, dtype=np.float32) / P).astype(np.float64)).astype(np.float32)).astype(np.float32)
    ck, sk = rope_table(np.arange(KEYS), inv2)
    a["rope_keys"] = pack(tiles(ck), tiles(sk))
    a["l2x"] = group_weights(i["L2_xattn_wq"], i["L2_xattn_wk"], i["L2_xattn_wv"], i["L2_xattn_wo"])
    a["mask2"], a["mask3"] = tiles(i["mask_BxSxS2_ff0"][0].T), tiles(i["mask_1x1xSxS2_ff0"][0, 0].T)
    inv16 = (1.0 / (10000.0 ** (np.arange(0, HD2, 2, dtype=np.float32) / HD2).astype(np.float64)).astype(np.float32)).astype(np.float32)
    c16, s16 = rope_table(pos, inv16)
    a["l2a"] = pack(tiles(i["L2_attn_wq"].T), tiles(np.concatenate([i["L2_attn_wk"].T, i["L2_attn_wv"].T], axis=1)),
                    tiles(i["L2_attn_wo"].T), c16, s16)
    a["l2f_gate"] = pack(tiles(i["L2_ffn_gate_w"].T), rows(i["L2_ffn_gate_b"]), rows(np.arange(E8, 0, -1).astype(np.float32)))
    a["l2f_bias"] = i["L2_ffn_expert_b"]
    a["l2f"] = np.stack([tiles(w.T) for w in i["L2_ffn_expert_w"]])
    a["l3x"] = group_weights(i["L3_xattn_Wq"].T, i["L3_xattn_Wk"].T, i["L3_xattn_Wv"].T, i["L3_xattn_Wo"].T)
    a["l3x_norm"] = pack(i["L3_xattn_q_norm_w"][:, None], i["L3_xattn_k_norm_w"][:, None])

    qkv = i["L3_attn_weight_qkv"].reshape(GROUPS, PER_GROUP + 2, P, D)
    a["l3a_v"] = tiles(qkv[:, PER_GROUP + 1].reshape(GROUPS * P, D).T)
    a["l3a_out"] = np.stack([tiles(w) for w in i["L3_attn_weight_proj"].T.reshape(GROUPS, PER_GROUP * P, D)])

    coefs = np.concatenate([i["L3_ffn_coefs0"], i["L3_ffn_coefs1"]], axis=2)
    masks = np.concatenate([i["L3_ffn_mask0"], i["L3_ffn_mask1"]], axis=2)
    by_row = lambda c: tiles(c.transpose(1, 0, 2).reshape(D, -1))
    a["l3f"] = pack(tiles(i["L3_ffn_W_base"].T), tiles(np.concatenate([i["L3_ffn_enc0"], i["L3_ffn_enc1"]], axis=0).T),
                    by_row(coefs), rows(i["L3_ffn_b_base"]))
    a["l3f_mask"] = np.ascontiguousarray(by_row(masks)).view(np.int32)
    a["fourier"] = tiles(fourier_basis())
    return a


def fourier_basis():
    n = np.arange(D, dtype=np.float64)
    f = np.arange(1, (D - 1) // 2 + 1, dtype=np.float64)
    basis = np.empty((D, D))
    basis[0] = D ** -0.5
    basis[1:D - 1:2] = (2.0 / D) ** 0.5 * np.cos(2 * np.pi * np.outer(f, n) / D)
    basis[2:D:2] = (2.0 / D) ** 0.5 * np.sin(2 * np.pi * np.outer(f, n) / D)
    basis[D - 1] = D ** -0.5 * (-1.0) ** n
    return basis.astype(np.float32)


def kernel(**inputs):
    import concourse.bacc as bacc
    from concourse.bass_utils import run_bass_kernel_spmd

    nc = bacc.Bacc("TRN2", target_bir_lowering=False, num_devices=1)
    arrays = {f"in_{n}": np.ascontiguousarray(a) for n, a in layout({n: np.asarray(a) for n, a in inputs.items()}).items()}
    dram = {n[3:]: nc.dram_tensor(n, a.shape, mybir.dt.from_np(a.dtype), kind="ExternalInput").ap() for n, a in arrays.items()}
    dram["cs"] = nc.dram_tensor("scan_cs", (GROUPS, HG * P), F32).ap()
    out = nc.dram_tensor("out_x", (P, D), F32, kind="ExternalOutput").ap()
    build(nc, dram, out)
    result = run_bass_kernel_spmd(nc, [arrays], core_ids=[0])
    return result.results[0]["out_x"].reshape(1, P, D)
```
